# Optimizing a Trainium2 kernel written in Bass

```python
import numpy as np
import jax
import jax.numpy as jnp

def _softmax(x, axis=-1):
    return jax.nn.softmax(x, axis=axis)

def _gelu(x):
    return jax.nn.gelu(x, approximate=True)

def _silu(x):
    return jax.nn.silu(x)

def _sigmoid(x):
    return jax.nn.sigmoid(x)

def _layernorm(x, axis=-1, eps=1e-05):
    m = jnp.mean(x, axis=axis, keepdims=True)
    v = jnp.var(x, axis=axis, keepdims=True)
    return (x - m) / jnp.sqrt(v + eps)

def _scatter_add(tgt, idx, src, axis=0):
    return tgt.at[idx].add(src)

def _segment_sum(src, seg, n):
    return jax.ops.segment_sum(src, seg, n)
kernel_name = 'mk_xattn_ffn_d4_seqx_r8_baeb7c'

def setup_inputs(seed: int=0):
    np.random.seed(seed)
    _w = jnp.asarray

    def _rec_inputs():
        import jax
        import jax.numpy as jnp
        _rk = jax.random.key(seed)
        x = 0.5 + 0.2887 * jax.random.normal(jax.random.fold_in(_rk, 1), (4, 256, 256), jnp.float32)
        _lenS = 256 - jax.random.randint(jax.random.fold_in(_rk, 7), (4,), 0, max(1, 256 // 4) + 1, jnp.int32)
        _lenS2 = 256 - jax.random.randint(jax.random.fold_in(_rk, 8), (4,), 0, max(1, 256 // 4) + 1, jnp.int32)
        _ctx_512P = jax.random.normal(jax.random.fold_in(_rk, 11), (4, 16, 64), jnp.float32)
        _ctx_512c = jax.random.dirichlet(jax.random.fold_in(_rk, 511), 0.3 * jnp.ones((16,), jnp.float32), (4, 256))
        _ctx_512t = jnp.einsum('bsk,bkd->bsd', _ctx_512c, _ctx_512P)
        _ctx_512t = _ctx_512t * jax.lax.rsqrt(jnp.mean(jnp.square(_ctx_512t)) + 1e-12) * 0.953939
        ctx_512 = 7.22013e-05 + 1.00017 * (_ctx_512t + 0.3 * jax.random.normal(jax.random.fold_in(_rk, 611), (4, 256, 64), jnp.float32))
        _validS = jnp.arange(256)[None, :] < _lenS[:, None]
        _validS2 = jnp.arange(256)[None, :] < _lenS2[:, None]
        _causal = jnp.tril(jnp.ones((256, 256), dtype=bool))
        mask_SxS2_bk1 = jnp.broadcast_to(_validS2[0:1, :], (256, 256))
        mask_BxS2_bf0 = jnp.logical_not(jnp.ones((4, 256), dtype=bool))
        return (x, ctx_512, mask_SxS2_bk1, mask_BxS2_bf0)
    x, ctx_512, mask_SxS2_bk1, mask_BxS2_bf0 = _rec_inputs()

    def _L0_xattn_setup():
        import jax, jax.numpy as jnp
        import numpy as np
        B, S, H = (8, 256, 64)
        key = jax.random.key(seed)
        kq, kk, kqc, kwq, kwk = jax.random.split(key, 5)
        q = jax.random.normal(kq, (B, S, H), dtype=jnp.float32)
        k = jax.random.normal(kk, (B, S, H), dtype=jnp.float32)
        qc_score = jax.random.uniform(kqc, (B, S, S), dtype=jnp.float32)
        attn_mask = jnp.triu(jnp.ones((S, S), dtype=bool), k=1)
        key_padding_mask = jnp.zeros((B, S), dtype=bool)
        scale = 1.0 / np.sqrt(H)
        Wq = jax.random.normal(kwq, (H, H), dtype=jnp.float32) * scale
        Wk = jax.random.normal(kwk, (H, H), dtype=jnp.float32) * scale
        bq = jnp.zeros((H,), dtype=jnp.float32)
        bk = jnp.zeros((H,), dtype=jnp.float32)
        return {'q': q, 'k': k, 'attn_mask': attn_mask, 'key_padding_mask': key_padding_mask, 'qc_score': qc_score, 'Wq': Wq, 'bq': bq, 'Wk': Wk, 'bk': bk}
    _L0_xattn_all = _L0_xattn_setup()
    _L0_xattn_in = {k: v for k, v in _L0_xattn_all.items() if k in ('Wq', 'bq', 'Wk', 'bk')}
    del _L0_xattn_all

    def _L0_ffn_setup():
        import jax, jax.numpy as jnp
        import numpy as np
        B, S, H = (2, 256, 256)
        INTER = 128
        N_ROUTED = 8
        ZERO = 4
        TOTAL = N_ROUTED + ZERO
        TOP_K = 2
        SCALE = 1.5
        key = jax.random.key(seed)
        k0, k1, k2, k3, k4, k5 = jax.random.split(key, 6)
        w = 0.02
        return {'hidden_states': jax.random.normal(k0, (B, S, H), jnp.float32), 'classifier_w': jax.random.normal(k1, (TOTAL, H), jnp.float32) * w, 'e_score_correction_bias': jax.random.normal(k2, (TOTAL,), jnp.float32) * w, 'gate_w': jax.random.normal(k3, (N_ROUTED, INTER, H), jnp.float32) * w, 'up_w': jax.random.normal(k4, (N_ROUTED, INTER, H), jnp.float32) * w, 'down_w': jax.random.normal(k5, (N_ROUTED, H, INTER), jnp.float32) * w}
    _L0_ffn_all = _L0_ffn_setup()
    _L0_ffn_in = {k: v for k, v in _L0_ffn_all.items() if k in ('classifier_w', 'e_score_correction_bias', 'gate_w', 'up_w', 'down_w')}
    del _L0_ffn_all

    def _L1_xattn_setup():
        import jax, jax.numpy as jnp
        import numpy as np
        import math
        NUM_Q_HEADS = 32
        NUM_KV_HEADS = 8
        key = jax.random.key(seed)
        k1, k2, k3 = jax.random.split(key, 3)
        B, S, E = (2, 256, 256)
        kv_E = NUM_KV_HEADS * (E // NUM_Q_HEADS)
        q = jax.random.normal(k1, (B, S, E), dtype=jnp.float32)
        k = jax.random.normal(k2, (B, S, kv_E), dtype=jnp.float32)
        v = jax.random.normal(k3, (B, S, kv_E), dtype=jnp.float32)
        return {'q': q, 'k': k, 'v': v}
    _L1_xattn_all = _L1_xattn_setup()
    _L1_xattn_in = {k: v for k, v in _L1_xattn_all.items() if k in ()}
    del _L1_xattn_all

    def _L1_ffn_setup():
        import jax, jax.numpy as jnp
        import numpy as np
        HID = 256
        INTER = 1024
        NEXP = 8
        TOPK = 2
        EPS = 1e-05

        def _mock_fused_moe(x, selected_experts, routing_weights, expert_weight):
            y = jnp.einsum('bsh,hd->bsd', x, expert_weight)
            scale = routing_weights.sum(axis=-1, keepdims=True)
            return y * scale
        key = jax.random.key(seed)
        ks = jax.random.split(key, 6)
        s = lambda fan_in: 1.0 / np.sqrt(fan_in)
        return {'hidden_states': jax.random.normal(ks[0], (4, 512, HID), dtype=jnp.float32), 'gate_w': jax.random.uniform(ks[1], (HID, NEXP), jnp.float32, -s(HID), s(HID)), 'up_w': jax.random.uniform(ks[2], (HID, INTER), jnp.float32, -s(HID), s(HID)), 'down_w': jax.random.uniform(ks[3], (INTER, HID), jnp.float32, -s(INTER), s(INTER)), 'expert_weight': jax.random.normal(ks[4], (HID, HID), dtype=jnp.float32), 'ln_gamma': jnp.ones((HID,), jnp.float32), 'ln_beta': jnp.zeros((HID,), jnp.float32)}
    _L1_ffn_all = _L1_ffn_setup()
    _L1_ffn_in = {k: v for k, v in _L1_ffn_all.items() if k in ('gate_w', 'up_w', 'down_w', 'expert_weight', 'ln_gamma', 'ln_beta')}
    del _L1_ffn_all

    def _L2_xattn_setup():
        import jax, jax.numpy as jnp
        import numpy as np
        N_HEADS = 16
        N_KV_HEADS = 4
        ROPE_THETA = 10000.0
        EPS = 1e-05

        def _rms_norm(x, w):
            var = jnp.mean(x * x, axis=-1, keepdims=True)
            return x * jax.lax.rsqrt(var + EPS) * w

        def _rope_sin_cos(T, head_dim, dtype):
            inv_freq = 1.0 / ROPE_THETA ** (jnp.arange(0, head_dim, 2, dtype=jnp.float32) / head_dim)
            t = jnp.arange(T, dtype=jnp.float32)
            freqs = jnp.outer(t, inv_freq)
            emb = jnp.concatenate([freqs, freqs], -1)
            return (jnp.sin(emb).astype(dtype)[None, None], jnp.cos(emb).astype(dtype)[None, None])

        def _rotate_half(x):
            h = x.shape[-1] // 2
            x1, x2 = (x[..., :h], x[..., h:])
            return jnp.concatenate([-x2, x1], axis=-1)
        key = jax.random.key(seed)
        ks = jax.random.split(key, 6)
        B, T, C = (2, 256, 256)
        Ckv = C // N_HEADS * N_KV_HEADS
        return {'q': jax.random.normal(ks[0], (B, T, C), jnp.float32), 'k': jax.random.normal(ks[1], (B, T, Ckv), jnp.float32), 'v': jax.random.normal(ks[2], (B, T, Ckv), jnp.float32), 'q_norm_w': jnp.ones((C,), jnp.float32), 'k_norm_w': jnp.ones((Ckv,), jnp.float32), 'w_out': jax.random.normal(ks[3], (C, C), jnp.float32) * C ** (-0.5)}
    _L2_xattn_all = _L2_xattn_setup()
    _L2_xattn_in = {k: v for k, v in _L2_xattn_all.items() if k in ('q_norm_w', 'k_norm_w', 'w_out')}
    del _L2_xattn_all

    def _L2_ffn_setup():
        import jax, jax.numpy as jnp
        import numpy as np
        B, S, H = (4, 256, 256)
        E, K, I = (32, 4, 128)
        key = jax.random.key(seed)
        k0, k1, k2, k3, k4 = jax.random.split(key, 5)
        scale = 0.02
        x = jax.random.normal(k0, (B, S, H), dtype=jnp.float32)
        Wgate = jax.random.normal(k1, (E, H), dtype=jnp.float32) * scale
        Wg = jax.random.normal(k2, (E, H, I), dtype=jnp.float32) * scale
        Wu = jax.random.normal(k3, (E, H, I), dtype=jnp.float32) * scale
        Wd = jax.random.normal(k4, (E, I, H), dtype=jnp.float32) * scale
        return {'x': x, 'Wgate': Wgate, 'Wg': Wg, 'Wu': Wu, 'Wd': Wd}
    _L2_ffn_all = _L2_ffn_setup()
    _L2_ffn_in = {k: v for k, v in _L2_ffn_all.items() if k in ('Wgate', 'Wg', 'Wu', 'Wd')}
    del _L2_ffn_all

    def _L3_xattn_setup():
        import jax, jax.numpy as jnp
        import numpy as np
        B, S, E = (2, 256, 256)
        QH, KVH = (32, 8)
        D = E // QH
        G = QH // KVH
        DROPOUT = 1.0
        key = jax.random.key(seed)
        k1, k2, k3 = jax.random.split(key, 3)
        q = jax.random.normal(k1, (B, S, E), dtype=jnp.float32)
        k = jax.random.normal(k2, (B, S, E // G), dtype=jnp.float32)
        v = jax.random.normal(k3, (B, S, E // G), dtype=jnp.float32)
        return {'q': q, 'k': k, 'v': v}
    _L3_xattn_all = _L3_xattn_setup()
    _L3_xattn_in = {k: v for k, v in _L3_xattn_all.items() if k in ()}
    del _L3_xattn_all

    def _L3_ffn_setup():
        import jax, jax.numpy as jnp
        import numpy as np
        NUM_EXPERTS_PER_TOK = 2
        key = jax.random.key(seed)
        k1, k2, k3, k4 = jax.random.split(key, 4)
        B, S, D, O, E = (4, 256, 256, 256, 8)
        x = jax.random.normal(k1, (B, S, D), dtype=jnp.float32)
        gate_w = jax.random.normal(k2, (E, D), dtype=jnp.float32) * (1.0 / np.sqrt(D))
        expert_w = jax.random.normal(k3, (E, O, D), dtype=jnp.float32) * (1.0 / np.sqrt(D))
        expert_b = jax.random.normal(k4, (E, O), dtype=jnp.float32) * 0.01
        return {'x': x, 'gate_w': gate_w, 'expert_w': expert_w, 'expert_b': expert_b}
    _L3_ffn_all = _L3_ffn_setup()
    _L3_ffn_in = {k: v for k, v in _L3_ffn_all.items() if k in ('gate_w', 'expert_w', 'expert_b')}
    del _L3_ffn_all
    return {'x': x, 'ctx_512': ctx_512, 'mask_SxS2_bk1': mask_SxS2_bk1, 'mask_BxS2_bf0': mask_BxS2_bf0, 'L0_xattn_Wq': _L0_xattn_in['Wq'], 'L0_xattn_bq': _L0_xattn_in['bq'], 'L0_xattn_Wk': _L0_xattn_in['Wk'], 'L0_xattn_bk': _L0_xattn_in['bk'], 'L0_ffn_classifier_w': _L0_ffn_in['classifier_w'], 'L0_ffn_e_score_correction_bias': _L0_ffn_in['e_score_correction_bias'], 'L0_ffn_gate_w': _L0_ffn_in['gate_w'], 'L0_ffn_up_w': _L0_ffn_in['up_w'], 'L0_ffn_down_w': _L0_ffn_in['down_w'], 'L1_ffn_gate_w': _L1_ffn_in['gate_w'], 'L1_ffn_up_w': _L1_ffn_in['up_w'], 'L1_ffn_down_w': _L1_ffn_in['down_w'], 'L1_ffn_expert_weight': _L1_ffn_in['expert_weight'], 'L1_ffn_ln_gamma': _L1_ffn_in['ln_gamma'], 'L1_ffn_ln_beta': _L1_ffn_in['ln_beta'], 'L2_xattn_q_norm_w': _L2_xattn_in['q_norm_w'], 'L2_xattn_k_norm_w': _L2_xattn_in['k_norm_w'], 'L2_xattn_w_out': _L2_xattn_in['w_out'], 'L2_ffn_Wgate': _L2_ffn_in['Wgate'], 'L2_ffn_Wg': _L2_ffn_in['Wg'], 'L2_ffn_Wu': _L2_ffn_in['Wu'], 'L2_ffn_Wd': _L2_ffn_in['Wd'], 'L3_ffn_gate_w': _L3_ffn_in['gate_w'], 'L3_ffn_expert_w': _L3_ffn_in['expert_w'], 'L3_ffn_expert_b': _L3_ffn_in['expert_b']}

def reference(x, ctx_512, mask_SxS2_bk1, mask_BxS2_bf0, L0_xattn_Wq, L0_xattn_bq, L0_xattn_Wk, L0_xattn_bk, L0_ffn_classifier_w, L0_ffn_e_score_correction_bias, L0_ffn_gate_w, L0_ffn_up_w, L0_ffn_down_w, L1_ffn_gate_w, L1_ffn_up_w, L1_ffn_down_w, L1_ffn_expert_weight, L1_ffn_ln_gamma, L1_ffn_ln_beta, L2_xattn_q_norm_w, L2_xattn_k_norm_w, L2_xattn_w_out, L2_ffn_Wgate, L2_ffn_Wg, L2_ffn_Wu, L2_ffn_Wd, L3_ffn_gate_w, L3_ffn_expert_w, L3_ffn_expert_b):
    import jax
    import jax.numpy as jnp

    def _L0_xattn_ref(q, k, attn_mask, key_padding_mask, qc_score, Wq, bq, Wk, bk):
        import jax, jax.numpy as jnp
        import numpy as np
        B, S, H = (8, 256, 64)
        qp = jnp.einsum('bsh,oh->bso', q, Wq) + bq
        kp = jnp.einsum('bth,oh->bto', k, Wk) + bk
        scaling = jnp.asarray(float(H) ** (-0.5), dtype=qp.dtype)
        scores = jnp.einsum('bsh,bth->bst', qp, kp) * scaling
        scores = scores * qc_score
        mask = attn_mask[None, :, :] | key_padding_mask[:, None, :]
        scores = jnp.where(mask, -jnp.inf, scores)
        return jax.nn.softmax(scores, axis=-1)

    def _L0_ffn_ref(hidden_states, classifier_w, e_score_correction_bias, gate_w, up_w, down_w):
        import jax, jax.numpy as jnp
        import numpy as np
        B, S, H = (2, 256, 256)
        INTER = 128
        N_ROUTED = 8
        ZERO = 4
        TOTAL = N_ROUTED + ZERO
        TOP_K = 2
        SCALE = 1.5
        x = hidden_states
        total = classifier_w.shape[0]
        n_routed = gate_w.shape[0]
        logits = jnp.einsum('bsh,eh->bse', x, classifier_w)
        probs = jax.nn.softmax(logits, axis=-1)
        biased = probs + e_score_correction_bias
        _, idx = jax.lax.top_k(biased, TOP_K)
        rw = jnp.take_along_axis(probs, idx, axis=-1) * SCALE
        w_full = jnp.sum(jax.nn.one_hot(idx, total, dtype=x.dtype) * rw[..., None], axis=-2)
        g = jnp.einsum('bsh,eih->bsei', x, gate_w)
        u = jnp.einsum('bsh,eih->bsei', x, up_w)
        act = jax.nn.silu(g) * u
        expert_out = jnp.einsum('bsei,ehi->bseh', act, down_w)
        out = jnp.einsum('bse,bseh->bsh', w_full[..., :n_routed], expert_out)
        out = out + x * jnp.sum(w_full[..., n_routed:], axis=-1, keepdims=True)
        return out

    def _L1_xattn_ref(q, k, v):
        import jax, jax.numpy as jnp
        import numpy as np
        import math
        NUM_Q_HEADS = 32
        NUM_KV_HEADS = 8
        B, S, E = q.shape
        H, KV = (NUM_Q_HEADS, NUM_KV_HEADS)
        D = E // H
        G = H // KV
        scale = math.sqrt(D)
        qh = q.reshape(B, S, KV, G, D).transpose(0, 2, 3, 1, 4)
        kh = k.reshape(B, S, KV, D).transpose(0, 2, 1, 3)
        vh = v.reshape(B, S, KV, D).transpose(0, 2, 1, 3)
        scores = jnp.einsum('bkgsd,bktd->bkgst', qh, kh) / scale
        weights = jax.nn.softmax(scores, axis=-1)
        out = jnp.einsum('bkgst,bktd->bkgsd', weights, vh)
        return out.transpose(0, 3, 1, 2, 4).reshape(B, S, E)

    def _L1_ffn_ref(hidden_states, gate_w, up_w, down_w, expert_weight, ln_gamma, ln_beta):
        import jax, jax.numpy as jnp
        import numpy as np
        HID = 256
        INTER = 1024
        NEXP = 8
        TOPK = 2
        EPS = 1e-05

        def _mock_fused_moe(x, selected_experts, routing_weights, expert_weight):
            y = jnp.einsum('bsh,hd->bsd', x, expert_weight)
            scale = routing_weights.sum(axis=-1, keepdims=True)
            return y * scale
        residuals = hidden_states
        logits = jnp.einsum('bsh,he->bse', hidden_states, gate_w)
        routing_weights, selected_experts = jax.lax.top_k(logits, TOPK)
        h = jnp.einsum('bsh,hi->bsi', residuals, up_w)
        h = jnp.square(jax.nn.relu(h))
        shared_out = jnp.einsum('bsi,ih->bsh', h, down_w)
        moe_out = _mock_fused_moe(hidden_states, selected_experts, routing_weights, expert_weight)
        y = shared_out + moe_out
        mu = y.mean(axis=-1, keepdims=True)
        var = jnp.mean(jnp.square(y - mu), axis=-1, keepdims=True)
        return (y - mu) * jax.lax.rsqrt(var + EPS) * ln_gamma + ln_beta

    def _L2_xattn_ref(q, k, v, q_norm_w, k_norm_w, w_out):
        import jax, jax.numpy as jnp
        import numpy as np
        N_HEADS = 16
        N_KV_HEADS = 4
        ROPE_THETA = 10000.0
        EPS = 1e-05

        def _rms_norm(x, w):
            var = jnp.mean(x * x, axis=-1, keepdims=True)
            return x * jax.lax.rsqrt(var + EPS) * w

        def _rope_sin_cos(T, head_dim, dtype):
            inv_freq = 1.0 / ROPE_THETA ** (jnp.arange(0, head_dim, 2, dtype=jnp.float32) / head_dim)
            t = jnp.arange(T, dtype=jnp.float32)
            freqs = jnp.outer(t, inv_freq)
            emb = jnp.concatenate([freqs, freqs], -1)
            return (jnp.sin(emb).astype(dtype)[None, None], jnp.cos(emb).astype(dtype)[None, None])

        def _rotate_half(x):
            h = x.shape[-1] // 2
            x1, x2 = (x[..., :h], x[..., h:])
            return jnp.concatenate([-x2, x1], axis=-1)
        B, T, C = q.shape
        hd = C // N_HEADS
        g = N_HEADS // N_KV_HEADS
        q = _rms_norm(q, q_norm_w)
        k = _rms_norm(k, k_norm_w)
        q = q.reshape(B, T, N_HEADS, hd).transpose(0, 2, 1, 3)
        k = k.reshape(B, T, N_KV_HEADS, hd).transpose(0, 2, 1, 3)
        v = v.reshape(B, T, N_KV_HEADS, hd).transpose(0, 2, 1, 3)
        sin, cos = _rope_sin_cos(T, hd, q.dtype)
        q = q * cos + _rotate_half(q) * sin
        k = k * cos + _rotate_half(k) * sin
        qg = q.reshape(B, N_KV_HEADS, g, T, hd)
        scale = 1.0 / jnp.sqrt(jnp.asarray(hd, q.dtype))
        scores = jnp.einsum('bgnqd,bgkd->bgnqk', qg, k) * scale
        causal = jnp.tril(jnp.ones((T, T), bool))
        scores = jnp.where(causal, scores, jnp.asarray(-1e+30, scores.dtype))
        attn = jax.nn.softmax(scores, axis=-1)
        out = jnp.einsum('bgnqk,bgkd->bgnqd', attn, v)
        out = out.reshape(B, N_HEADS, T, hd).transpose(0, 2, 1, 3).reshape(B, T, C)
        return out @ w_out.T

    def _L2_ffn_ref(x, Wgate, Wg, Wu, Wd):
        import jax, jax.numpy as jnp
        import numpy as np
        B, S, H = (4, 256, 256)
        E, K, I = (32, 4, 128)
        b, s, h = x.shape
        xf = x.reshape(-1, h)
        n = xf.shape[0]
        logits = xf @ Wgate.T
        scores = jax.nn.softmax(logits, axis=-1)
        topk_w, topk_ids = jax.lax.top_k(scores, K)
        w_dense = jnp.zeros((n, E), dtype=xf.dtype).at[jnp.arange(n)[:, None], topk_ids].add(topk_w.astype(xf.dtype))

        def step(acc, params):
            wg, wu, wd, we = params
            hmid = jax.nn.silu(xf @ wg) * (xf @ wu)
            return (acc + hmid @ wd * we[:, None], None)
        out, _ = jax.lax.scan(step, jnp.zeros_like(xf), (Wg, Wu, Wd, w_dense.T))
        return out.reshape(b, s, h)

    def _L3_xattn_ref(q, k, v):
        import jax, jax.numpy as jnp
        import numpy as np
        B, S, E = (2, 256, 256)
        QH, KVH = (32, 8)
        D = E // QH
        G = QH // KVH
        DROPOUT = 1.0
        b, s, _ = q.shape
        qh = q.reshape(b, s, KVH, G, D).transpose(0, 2, 3, 1, 4)
        kh = k.reshape(b, s, KVH, D).transpose(0, 2, 1, 3)
        vh = v.reshape(b, s, KVH, D).transpose(0, 2, 1, 3)
        scale = 1.0 / jnp.sqrt(jnp.float32(D))
        scores = jnp.einsum('bkgsd,bktd->bkgst', qh, kh) * scale
        attn = jax.nn.softmax(scores, axis=-1) / DROPOUT
        out = jnp.einsum('bkgst,bktd->bkgsd', attn, vh)
        return out.transpose(0, 3, 1, 2, 4).reshape(b, s, E)

    def _L3_ffn_ref(x, gate_w, expert_w, expert_b):
        import jax, jax.numpy as jnp
        import numpy as np
        NUM_EXPERTS_PER_TOK = 2
        B, S, D = x.shape
        xf = x.reshape(B * S, D)
        gate_logits = xf @ gate_w.T
        top_vals, top_idx = jax.lax.top_k(gate_logits, NUM_EXPERTS_PER_TOK)
        w = jax.nn.softmax(top_vals.astype(jnp.float32), axis=-1).astype(x.dtype)
        y_all = jnp.einsum('td,eod->teo', xf, expert_w) + expert_b[None, :, :]
        y_sel = jnp.take_along_axis(y_all, top_idx[:, :, None], axis=1)
        out = jnp.sum(y_sel * w[:, :, None], axis=1)
        return out.reshape(B, S, -1)
    x = x + _L0_xattn_ref(ctx_512, ctx_512, mask_SxS2_bk1, mask_BxS2_bf0, _layernorm(x, axis=-1), L0_xattn_Wq, L0_xattn_bq, L0_xattn_Wk, L0_xattn_bk)
    x = x + _L0_ffn_ref(_layernorm(x, axis=-1), L0_ffn_classifier_w, L0_ffn_e_score_correction_bias, L0_ffn_gate_w, L0_ffn_up_w, L0_ffn_down_w)
    x = x + _L1_xattn_ref(_layernorm(x, axis=-1), ctx_512, ctx_512)
    x = x + _L1_ffn_ref(_layernorm(x, axis=-1), L1_ffn_gate_w, L1_ffn_up_w, L1_ffn_down_w, L1_ffn_expert_weight, L1_ffn_ln_gamma, L1_ffn_ln_beta)
    x = x + _L2_xattn_ref(_layernorm(x, axis=-1), ctx_512, ctx_512, L2_xattn_q_norm_w, L2_xattn_k_norm_w, L2_xattn_w_out)
    x = x + _L2_ffn_ref(_layernorm(x, axis=-1), L2_ffn_Wgate, L2_ffn_Wg, L2_ffn_Wu, L2_ffn_Wd)
    x = x + _L3_xattn_ref(_layernorm(x, axis=-1), ctx_512, ctx_512)
    x = x + _L3_ffn_ref(_layernorm(x, axis=-1), L3_ffn_gate_w, L3_ffn_expert_w, L3_ffn_expert_b)
    return x

_drawn_inputs = setup_inputs


def setup_inputs(seed=0):
    import zlib

    import numpy as np

    out = dict(_drawn_inputs(seed))
    spreads = {'L0_xattn_bq': (0.0, 0.285),
     'L0_xattn_bk': (0.0, 0.376),
     'L1_ffn_ln_gamma': (1.0, 0.2),
     'L1_ffn_ln_beta': (0.0, 0.1),
     'L2_xattn_q_norm_w': (1.0, 0.2),
     'L2_xattn_k_norm_w': (1.0, 0.2)}
    factors = {'L0_ffn_gate_w': 3.719,
     'L0_ffn_up_w': 3.479,
     'L0_ffn_down_w': 3.798,
     'L2_ffn_Wgate': 6.642,
     'L2_ffn_Wg': 7.26,
     'L2_ffn_Wu': 7.94,
     'L2_ffn_Wd': 8.0,
     'L3_ffn_expert_b': 35.751}
    for name, (base, spread) in spreads.items():
        noise = np.random.default_rng([zlib.crc32(name.encode()), seed]).standard_normal(out[name].shape)
        drawn = base * np.exp(spread * noise) if base else spread * noise
        out[name] = jnp.asarray(drawn.astype(out[name].dtype))
    for name, factor in factors.items():
        out[name] = (out[name] * factor).astype(out[name].dtype)
    return out
```

```python
from contextlib import ExitStack

import numpy as np

import concourse.bass as bass
from concourse import mybir

F32 = mybir.dt.float32
F32R = mybir.dt.float32r
BF16 = mybir.dt.bfloat16
I32 = mybir.dt.int32
U8 = mybir.dt.uint8
U32 = mybir.dt.uint32
ALU = mybir.AluOpType
ACT = mybir.ActivationFunctionType
AX_X = mybir.AxisListType.X

P = 128
B, S, H = 4, 256, 256
TOK = B * S
TILES = TOK // P
HALF = TOK // 2
CTX = 64
EPS = 1e-5
ROOT_GUESS = float(0x5F3759DF)
MASKED = -3.0e38
T_BANK = 2
MAX_BANK = 0
ST_BANK = 2
OT_BANK, SUM_BANK = 6, 7
G_BANK, U_BANK, W_BANK, LOGIT_BANK = 4, 5, 6, 7
ROUTED = (12, 8, 32, 8)
ROUTER_AT = (0, 12, 20, 52)
SENTINEL = -3.0e38
TAKEN = 3.0e38


class Chain:

    def __init__(self, eng, sem):
        self.eng, self.sem, self.n = eng, sem, 0

    def mark(self, ins):
        ins.then_inc(self.sem, 1)
        self.n += 1

    def join(self):
        self.eng.wait_ge(self.sem, self.n)

    def step(self, ins):
        self.mark(ins)
        self.join()


def product3(pe, out, parts, start, stop):
    ins = None
    for n, (Lh, Ll, Rh, Rl) in enumerate(parts):
        first, last = n == 0, n == len(parts) - 1
        pe.matmul(out, Lh, Rh, start=start and first, stop=False, skip_group_check=True)
        pe.matmul(out, Lh, Rl, start=False, stop=False, skip_group_check=True)
        ins = pe.matmul(out, Ll, Rh, start=False, stop=stop and last, skip_group_check=True)
    return ins


TURNS = ("f0", "a1", "f1", "a2", "o2", "f2", "a3", "f3")


def z_at(tag, n):
    return TILES * TURNS.index(tag) + n


def bank_at(tag, n):
    return 4 * TURNS.index(tag) + n


class Head:

    def __init__(self, D, causal, before):
        self.D, self.causal = D, causal
        self.HJ = P // D
        self.KJ = self.HJ // 4
        self.R = 4 * D + 2
        self.scale = D ** -0.5
        self.steps = 2 * B
        self.units = self.steps * self.KJ
        self.chunks = 3 if causal else 4
        self.step0 = before.step0 + before.steps if before else 0
        self.unit0 = before.unit0 + before.units if before else 0
        self.chunk0 = before.chunk0 + before.units * before.chunks if before else 0

    def buf(self, n):
        return (self.step0 + n) % 3

    def uses(self, n):
        return (self.step0 + n) // 3 + 1


def build(nc, a, out):
    ctx = ExitStack()
    with ctx:
        def sb(name, shape, dt=F32):
            return ctx.enter_context(nc.sbuf_tensor(name, list(shape), dt))

        sems = {}

        def sem(name):
            if name not in sems:
                sems[name] = ctx.enter_context(nc.semaphore(name))
            return sems[name]

        ps = ctx.enter_context(nc.psum_tensor("ps", [P, 8, 512], F32))

        x = sb("x", [P, TILES, H])
        z = sb("z", [P, TILES, H])
        zh = sb("zh", [P, 2, TOK], F32R)
        zl = sb("zl", [P, 2, TOK], F32R)
        ident = sb("ident", [P, P])
        identb = sb("identb", [P, P], BF16)
        mask_q = sb("mask_q", [P, 512], BF16)
        mask_k = sb("mask_k", [P, 512], BF16)
        sel8 = sb("sel8", [P, 18])
        sel16 = sb("sel16", [P, 34])
        cosr = sb("cosr", [P, 2, 16])
        sinr = sb("sinr", [P, 2, 16])
        qw = sb("qw", [P, H])
        kw = sb("kw", [P, CTX])
        ctxt = sb("ctxt", [P, TILES, CTX])
        kr = sb("kr", [P, TILES, CTX])
        v8 = sb("v8", [P, TILES, 8, 32])
        v16 = sb("v16", [P, TILES, 4, 32])
        ctxT = sb("ctxT", [CTX, TOK])
        wqk = sb("wqk", [CTX, 2, CTX])
        bqk = sb("bqk", [CTX, 2])
        m1 = sb("m1", [P, 2, S // 4], U32)
        m2 = sb("m2", [P, B, S // 4], U32)
        mask8 = sb("mask8", [P, TILES, S], U8)
        raw = sb("raw", [P, 2, 1024])
        wh = sb("wh", [P, 2, 1024], F32R)
        wl = sb("wl", [P, 2, 1024], F32R)
        router = sb("router", [P, 2, 60])
        router_h = sb("router_h", [P, 2, 60], F32R)
        router_l = sb("router_l", [P, 2, 60], F32R)
        dense = sb("dense", [P, 2, 2, H])
        dense_h = sb("dense_h", [P, 2, 2, H], F32R)
        dense_l = sb("dense_l", [P, 2, 2, H], F32R)
        gamma = sb("gamma", [P, H])
        beta = sb("beta", [P, H])
        bias0 = sb("bias0", [P, 12])
        bias3 = sb("bias3", [8, H])
        bias3h = sb("bias3h", [8, H], F32R)
        bias3l = sb("bias3l", [8, H], F32R)
        one = sb("one", [P, 1])
        ones2f = sb("ones2f", [2, P])
        ones2 = sb("ones2", [2, P], F32R)
        qs = sb("qs", [P, 3, 4096], F32R)
        ks8 = sb("ks8", [34, 3, 4 * S], F32R)
        ks16 = sb("ks16", [66, 3, 2 * S], F32R)
        e = sb("e", [P, 2, 2, 1024])
        ot = sb("ot", [P, 2, 512])
        mx = sb("mx", [P, 2, 32])
        mT = sb("mT", [32, 2, 2, P], F32R)
        att = sb("att", [P, 2, 2, 16 * 9 + 8])
        attr = sb("attr", [P, 2, 16])
        attn = sb("attn", [P, 2, P])
        ef = e[:, :, :, :].rearrange("p a b c -> p (a b c)")
        qf = qs[:, :, :].rearrange("p a b -> p (a b)")

        def pair_of(flat, at, rows=P, n=512):
            return flat[0:rows, at:at + 2 * n].rearrange("p (a b) -> p a b", a=2)

        sg, t1, hm = (pair_of(ef, at) for at in (0, 1024, 2048))
        acc = pair_of(ef, 0, n=TOK)
        hh, hl = (pair_of(qf, at) for at in (0, 1024))
        wrow = pair_of(qf, 2048, 2, TOK)
        wT = pair_of(qf, 4096, 32, TOK)
        gs = sb("gs", [P, TILES, 40])
        gr = sb("gr", [P, TILES, 40])
        gp = sb("gp", [P, TILES, 32])
        gw = sb("gw", [P, TILES, 32])
        g8 = sb("g8", [P, TILES, 8])
        ga = sb("ga", [P, TILES])
        gb = sb("gb", [P, TILES])
        bst = sb("bst", [P, TILES, 6])
        mv = sb("mv", [P, TILES, 2])
        rstd = sb("rstd", [P, TILES])
        var = sb("var", [P, TILES])
        root = sb("root", [P, TILES])
        nmx = sb("nmx", [P, TILES])
        rsum = sb("rsum", [P, TILES])

        kst8 = nc.dram_tensor("kst8", [32, 8, TOK], F32).ap()
        kst16 = nc.dram_tensor("kst16", [64, 4, TOK], F32).ap()
        wsc = {L: nc.dram_tensor(f"wsc{L}", [ROUTED[L], 2, TOK], F32).ap() for L in (0, 2)}

        rh = [router_h[:, :, ROUTER_AT[L]:ROUTER_AT[L] + ROUTED[L]] for L in range(4)]
        rl = [router_l[:, :, ROUTER_AT[L]:ROUTER_AT[L] + ROUTED[L]] for L in range(4)]
        grouped = {1: Head(8, False, None)}
        grouped[2] = Head(16, True, grouped[1])
        grouped[3] = Head(8, False, grouped[2])
        NEXP = {0: 8, 1: 8, 2: 32}
        WCOLS = {0: 768, 1: 512, 2: 768}

        def units(hd):
            return range(hd.units + hd.KJ + 3)

        hi8, lo8 = hh[0:CTX, :, :].rearrange("p a b -> p (a b)"), hl[0:CTX, :, :].rearrange("p a b -> p (a b)")
        hi16, lo16 = wh[0:CTX, 0, :], wl[0:CTX, 0, :]

        hide = att[:, :, :, :].rearrange("p a b c -> p (a b c)")[:, 0:2 * P]
        a0q, a0k = ef[0:CTX, 2048:3072], ef[0:CTX, 3072:4096]
        a0s = ef[:, 0:2048].rearrange("p (t s) -> p t s", s=S)

        def b3(pair):
            return wrow[:, pair // 2, (pair % 2) * 512:(pair % 2 + 1) * 512]

        block = ctx.enter_context(nc.Block())

        @block.sync
        def _(sp):
            def load(dst, src, s):
                sp.dma_start(dst, src).then_inc(sem(s), 16)

            load(ctxT[:, :], a["ctxP"], "l_ctxT")
            load(ctxt[:, :, :], a["ctx"].rearrange("(t p) d -> p t d", p=P), "l_ctx")
            load(kw[:, :], a["kw"].partition_broadcast(P), "l_ctx")
            load(cosr[:, :, :], a["cos"], "l_ctx")
            load(sinr[:, :, :], a["sin"], "l_ctx")
            load(x[:, :, :], a["x"].rearrange("(t p) d -> p t d", p=P), "l_x")
            load(wqk[:, :, :], a["wqk"], "l_ctxT")
            load(bqk[:, :], a["bqk"], "l_ctxT")
            load(m1[:, :, :], a["m1"].rearrange("(t p) s -> p t s", p=P), "l_mask")
            load(m2[:, :, :], a["m2"].partition_broadcast(P), "l_mask")
            load(ident[:, :], a["ident"], "l_ident")
            load(router[:, :, :], a["router"], "l_dense")
            load(dense[:, :, :, :], a["dense"], "l_dense")
            load(bias3[:, :], a["bias3"], "l_dense")
            load(bias0[:, :], a["bias0"].partition_broadcast(P), "l_rows")
            load(gamma[:, :], a["gamma"].partition_broadcast(P), "l_rows")
            load(beta[:, :], a["beta"].partition_broadcast(P), "l_rows")
            load(qw[:, :], a["qw"].partition_broadcast(P), "l_rows")
            load(hide, a["hide"], "l_att")
            load(sel8[:, :], a["sel8"], "l_att")
            load(sel16[:, :], a["sel16"], "l_att")
            sp.wait_ge(sem("k8_split"), 2)
            for part, src in enumerate((0, 0, 1, 1)):
                load(kst8[part * 8:part * 8 + 8, :, :], (hi8, lo8)[src].bitcast(F32), "k8_stored")
            sp.wait_ge(sem("k16_split"), 2)
            for part, src in enumerate((0, 0, 1, 1)):
                load(kst16[part * 16:part * 16 + 16, :, :], (hi16, lo16)[src].bitcast(F32), "k16_stored")

            def experts(L):
                pk = a[f"experts{L}"]

                def raw_load(pair, eb):
                    sp.dma_start(raw[:, eb, 0:WCOLS[L]], pk[2 * pair + eb, :, :]).then_inc(sem(f"f{L}_raw{eb}"), 16)

                def row_load(pair, eb):
                    sp.dma_start(wrow[:, eb, :].bitcast(F32), wsc[L][2 * pair + eb, :, :]).then_inc(sem(f"f{L}_row{eb}"), 16)

                gated = L != 1
                if L > 0:
                    sp.wait_ge(sem(f"f{L-1}_split0"), NEXP[L - 1] // 2)
                    sp.wait_ge(sem(f"f{L-1}_split1"), NEXP[L - 1] // 2)
                raw_load(0, 0)
                raw_load(0, 1)
                if gated:
                    sp.wait_ge(sem(f"f{L}_wlo"), 1)
                    sp.dma_start(wsc[L][:, :, :], wT[0:ROUTED[L], :, :].bitcast(F32)).then_inc(sem(f"f{L}_wsc"), 16)
                    sp.wait_ge(sem(f"f{L}_wsc"), 16)
                    row_load(0, 0)
                    row_load(0, 1)
                with sp.Fori(1, NEXP[L] // 2) as pair:
                    for eb in (0, 1):
                        sp.wait_ge(sem(f"f{L}_split{eb}"), pair)
                        raw_load(pair, eb)
                        if gated:
                            sp.wait_ge(sem(f"f{L}_spread"), pair * 4 + (2 * eb - 2))
                            row_load(pair, eb)

            def attention(L):
                hd, ks = grouped[L], (ks16 if grouped[L].causal else ks8)
                kst = kst16 if hd.causal else kst8
                sp.wait_ge(sem("lo_ready"), bank_at(f"a{L}", 4))
                if L == 1:
                    sp.wait_ge(sem("k8_stored"), 64)
                if L == 2:
                    sp.wait_ge(sem("k16_stored"), 64)
                sp.wait_ge(sem("minus_ones"), 2)

                def step_load(n):
                    b, j = divmod(n, 2)
                    if n >= 3:
                        sp.wait_ge(sem("a_st1"), hd.unit0 + (n - 2) * hd.KJ)
                    cols = slice(b * S, b * S + S)
                    for part, src in enumerate((zh, zl, zh, zl)):
                        sp.dma_start(qs[part * hd.D:(part + 1) * hd.D, hd.buf(n), 0:hd.HJ * S].bitcast(F32),
                                     src[:, j, cols].bitcast(F32)).then_inc(sem(f"a_q{hd.buf(n)}"), 16)
                    sp.dma_start(ks[0:4 * hd.D, hd.buf(n), :].rearrange("r (k t) -> r k t", t=S).bitcast(F32),
                                 kst[:, j * hd.KJ:(j + 1) * hd.KJ, cols]).then_inc(sem(f"a_q{hd.buf(n)}"), 16)

                step_load(0)
                step_load(1)
                step_load(2)
                for n in range(hd.steps):
                    sp.wait_ge(sem("a_mlo"), hd.step0 + n + 1)
                    for part in (0, 1):
                        for st in (0, 1):
                            dst = qs[4 * hd.D + part:4 * hd.D + part + 1, hd.buf(n), 0:hd.HJ * S].rearrange(
                                "o (h s) -> o h s", s=S)[:, :, st * P:st * P + P]
                            sp.dma_start(dst.bitcast(F32),
                                         mT[st * hd.HJ:(st + 1) * hd.HJ, n % 2, part, :].bitcast(F32)
                                         ).then_inc(sem(f"a_m{hd.buf(n)}"), 16)
                    if 1 <= n < hd.steps - 2:
                        step_load(n + 2)

            experts(0)
            attention(1)
            experts(1)
            attention(2)
            experts(2)
            attention(3)
            sp.wait_ge(sem("a_st1"), grouped[3].unit0 + grouped[3].units)
            sp.dma_start(wrow[0:1, :, :].bitcast(F32), bias3h[:, :].bitcast(F32)).then_inc(sem("bias3_ready"), 16)
            sp.dma_start(wrow[1:2, :, :].bitcast(F32), bias3l[:, :].bitcast(F32)).then_inc(sem("bias3_ready"), 16)
            sp.wait_ge(sem("f2_split0"), 16)
            sp.wait_ge(sem("f2_split1"), 16)
            for pair in range(4):
                if pair >= 2:
                    sp.wait_ge(sem(f"f3_split{pair % 2}"), pair // 2)
                sp.dma_start(raw[:, pair % 2, :], a["experts3"][pair]).then_inc(sem(f"f3_raw{pair % 2}"), 16)
            for t in range(TILES):
                sp.wait_ge(sem("f3_add"), 3 * TILES + t + 1)
                sp.dma_start(out[t * P:(t + 1) * P, :], x[:, t, :]).then_inc(sem("stored"), 16)
            sp.wait_ge(sem("stored"), 16 * TILES)

        @block.gpsimd
        def _(pool):
            c = Chain(pool, sem("pool_step"))
            c.mark(pool.memset(one[:, :], 1.0))
            c.mark(pool.memset(v8[:, :, :, :], 0.0))
            c.mark(pool.memset(v16[:, :, :, :], 0.0))
            c.join()
            c.mark(pool.memset(v8[:, :, :, 8:9], 1.0))
            c.mark(pool.memset(v16[:, :, :, 16:17], 1.0))
            c.join()
            pool.wait_ge(sem("l_ctx"), 64)
            pool.tensor_copy(v8[:, :, :, 0:8], ctxt[:, :, :].rearrange("p t (k d) -> p t k d", d=8)
                             ).then_inc(sem("v_ready"), 1)
            pool.tensor_copy(v16[:, :, :, 0:16], ctxt[:, :, :].rearrange("p t (k d) -> p t k d", d=16)
                             ).then_inc(sem("v_ready"), 1)
            pool.wait_ge(sem("l_dense"), 48)
            c.mark(pool.tensor_copy(router_h[:, :, :], router[:, :, :]))
            c.mark(pool.tensor_copy(dense_h[:, :, :, :], dense[:, :, :, :]))
            c.mark(pool.tensor_copy(bias3h[:, :], bias3[:, :]))
            c.join()
            pool.tensor_tensor(router_l[:, :, :], router[:, :, :], router_h[:, :, :].bitcast(F32),
                               ALU.subtract).then_inc(sem("dense_split"), 1)
            pool.tensor_tensor(dense_l[:, :, :, :], dense[:, :, :, :], dense_h[:, :, :, :].bitcast(F32),
                               ALU.subtract).then_inc(sem("dense_split"), 1)
            pool.tensor_tensor(bias3l[:, :], bias3[:, :], bias3h[:, :].bitcast(F32),
                               ALU.subtract).then_inc(sem("dense_split"), 1)

            def experts(L):
                cols = WCOLS[L]
                n_pair = NEXP[L] // 2
                if L == 0:
                    pool.wait_ge(sem("k16_stored"), 64)
                else:
                    pool.wait_ge(sem(f"f{L-1}_down"), 2 * NEXP[L - 1])

                def split(pair, eb, peeled):
                    pool.wait_ge(sem(f"f{L}_raw{eb}"), 16 * (pair + 1))
                    if not peeled:
                        pool.wait_ge(sem(f"f{L}_down"), pair * 4 + (2 * eb - 2))
                    pool.tensor_tensor(wh[:, eb, 0:cols], raw[:, eb, 0:cols], one[:, :].broadcast_to([P, cols]),
                                       ALU.mult).then_inc(sem(f"f{L}_hi{eb}"), 1)
                    pool.wait_ge(sem(f"f{L}_hi{eb}"), pair + 1)
                    pool.tensor_tensor(wl[:, eb, 0:cols], raw[:, eb, 0:cols], wh[:, eb, 0:cols].bitcast(F32),
                                       ALU.subtract).then_inc(sem(f"f{L}_split{eb}"), 1)

                split(0, 0, True)
                split(0, 1, True)
                with pool.Fori(1, n_pair) as pair:
                    split(pair, 0, False)
                    split(pair, 1, False)

            experts(0)
            experts(1)
            experts(2)
            pool.wait_ge(sem("f2_down"), 2 * NEXP[2])
            for pair in range(4):
                eb = pair % 2
                pool.wait_ge(sem(f"f3_raw{eb}"), 16 * (pair // 2 + 1))
                if pair >= 2:
                    pool.wait_ge(sem("f3_y"), 8 * (pair - 1))
                pool.tensor_copy(wh[:, eb, :], raw[:, eb, :]).then_inc(sem(f"f3_hi{eb}"), 1)
                pool.wait_ge(sem(f"f3_hi{eb}"), pair // 2 + 1)
                pool.tensor_tensor(wl[:, eb, :], raw[:, eb, :], wh[:, eb, :].bitcast(F32),
                                   ALU.subtract).then_inc(sem(f"f3_split{eb}"), 1)

        @block.tensor
        def _(pe):
            def turn(tag):
                for u in range(4):
                    hf, j = divmod(u, 2)
                    pe.wait_ge(sem("z_ready"), z_at(tag, 4 * hf + 4))
                    for q in range(4):
                        ins = pe.transpose(ps[:, T_BANK + u, q * P:(q + 1) * P],
                                           z[:, hf * 4 + q, j * P:(j + 1) * P], ident[:, :])
                    ins.then_inc(sem("turned"), 1)

            def attention0():
                pe.wait_ge(sem("l_ctxT"), 48)
                for m in (0, 1):
                    for hf in (0, 1):
                        pe.matmul(ps[0:CTX, 2 * m + hf, :], wqk[:, m, :], ctxT[:, hf * HALF:(hf + 1) * HALF],
                                  start=True, stop=True).then_inc(sem("a0_proj"), 1)
                pe.wait_ge(sem("l_ident"), 16)
                pe.wait_ge(sem("kr_ready"), 1)
                for t in range(TILES):
                    ins = pe.transpose(ps[0:CTX, 4 + t // 4, (t % 4) * P:(t % 4 + 1) * P],
                                       kr[:, t, :], ident[:, :])
                ins.then_inc(sem("kr_turned"), 1)
                pe.wait_ge(sem("a0_qk"), 4)
                pe.wait_ge(sem("k16_split"), 2)
                for t in range(TILES):
                    b = t // 2
                    ins = pe.matmul(ps[:, 4 + t // 2, (t % 2) * S:(t % 2 + 1) * S], a0q[:, t * P:(t + 1) * P],
                                    a0k[:, b * S:(b + 1) * S], start=True, stop=True)
                    if t % 2:
                        ins.then_inc(sem("a0_scores"), 1)

            def logits(L):
                pe.wait_ge(sem("lo_ready"), bank_at(f"f{L}", 4))
                if L == 0:
                    pe.wait_ge(sem("dense_split"), 3)
                for t in range(TILES):
                    tok = slice(t * P, (t + 1) * P)
                    parts = [(zh[:, j, tok], zl[:, j, tok], rh[L][:, j, :], rl[L][:, j, :]) for j in (0, 1)]
                    ins = product3(pe, ps[:, LOGIT_BANK, t * ROUTED[L]:(t + 1) * ROUTED[L]], parts, True, True)
                ins.then_inc(sem("logits"), 1)

            def experts(L):
                gated = L != 1
                n_pair = NEXP[L] // 2

                def up(eb, hf, bank, at, signal):
                    tok = slice(hf * HALF, (hf + 1) * HALF)
                    parts = [(wh[:, eb, at + k * P:at + (k + 1) * P], wl[:, eb, at + k * P:at + (k + 1) * P],
                              zh[:, k, tok], zl[:, k, tok]) for k in (0, 1)]
                    product3(pe, ps[:, bank, :], parts, True, True).then_inc(sem(signal), 1)

                def down(unit, eb, hf, first, last):
                    pe.wait_ge(sem(f"f{L}_hl"), unit + 1)
                    at = WCOLS[L] - H
                    for hb in (0, 1):
                        cols = slice(at + hb * P, at + (hb + 1) * P)
                        ins = product3(pe, ps[:, 2 * hb + hf, :],
                                       [(wh[:, eb, cols], wl[:, eb, cols], hh[:, hf, :], hl[:, hf, :])], first, last)
                    ins.then_inc(sem(f"f{L}_down"), 1)

                def pair_units(pair, first, last):
                    for eb in (0, 1):
                        pe.wait_ge(sem(f"f{L}_split{eb}"), pair + 1)
                        for hf in (0, 1):
                            k = 2 * eb + hf
                            unit = pair * 4 + k
                            start = first and k == 0
                            if gated:
                                if not start:
                                    pe.wait_ge(sem(f"f{L}_act"), unit)
                                up(eb, hf, G_BANK, 0, f"f{L}_g")
                                if not start:
                                    pe.wait_ge(sem(f"f{L}_gu"), unit)
                                up(eb, hf, U_BANK, H, f"f{L}_u")
                                if start:
                                    turn_weights(L)
                                else:
                                    pe.wait_ge(sem(f"f{L}_hm"), unit)
                                if hf == 0:
                                    pe.wait_ge(sem(f"f{L}_row{eb}"), 16 * (pair + 1))
                                pe.matmul(ps[:, W_BANK, :], ones2[:, :], wrow[:, eb, hf * HALF:(hf + 1) * HALF],
                                          start=True, stop=True).then_inc(sem(f"f{L}_spread"), 1)
                            else:
                                if not (first and k < 2):
                                    pe.wait_ge(sem(f"f{L}_hm"), unit - 1)
                                up(eb, hf, G_BANK + hf, 0, f"f{L}_u")
                            if not start:
                                before = (eb, 0) if hf else (1 - eb, 1)
                                down(unit - 1, *before, first and k in (1, 2), last and k == 3)
                    if last:
                        down(4 * n_pair - 1, 1, 1, False, True)

                def turn_weights(L):
                    E = ROUTED[L]
                    pe.wait_ge(sem(f"f{L}_w"), 1)
                    for t in range(TILES):
                        ins = pe.transpose(ps[0:E, W_BANK + t // 4, (t % 4) * P:(t % 4 + 1) * P],
                                           gw[:, t, 0:E], ident[:, :])
                    ins.then_inc(sem(f"f{L}_wturned"), 1)
                    pe.wait_ge(sem(f"f{L}_wlo"), 1)

                pair_units(0, True, False)
                with pe.Fori(1, n_pair - 1) as pair:
                    pair_units(pair, False, False)
                pair_units(n_pair - 1, False, True)
                if L == 1:
                    for i in range(4):
                        if i == 0:
                            pe.wait_ge(sem("f1_hm"), 2 * NEXP[1])
                        for t in (2 * i, 2 * i + 1):
                            tok = slice(t * P, (t + 1) * P)
                            parts = [(zh[:, j, tok], zl[:, j, tok], dense_h[:, 0, j, :], dense_l[:, 0, j, :])
                                     for j in (0, 1)]
                            ins = product3(pe, ps[:, 4 + i, (t % 2) * H:(t % 2 + 1) * H], parts, True, True)
                        ins.then_inc(sem("f1_moe"), 1)
                pe.wait_ge(sem(f"f{L}_acc"), 2)
                for i in range(4):
                    if L == 1:
                        pe.wait_ge(sem("f1_moe_read"), i + 1)
                    for t in (2 * i, 2 * i + 1):
                        for hb in (0, 1):
                            ins = pe.transpose(ps[:, 4 + i, (t % 2) * H + hb * P:(t % 2) * H + (hb + 1) * P],
                                               acc[:, hb, t * P:(t + 1) * P], ident[:, :])
                    ins.then_inc(sem(f"f{L}_back"), 1)

            def attention(L):
                hd, ks = grouped[L], (ks16 if grouped[L].causal else ks8)
                D, KJ, R = hd.D, hd.KJ, hd.R
                v = v16 if hd.causal else v8
                sel = sel16 if hd.causal else sel8
                if L == 1:
                    pe.wait_ge(sem("l_att"), 48)
                    pe.wait_ge(sem("v_ready"), 2)

                def q_of(n, h0, h1, s0=0, s1=S, rows=R):
                    return qs[0:rows, hd.buf(n), 0:hd.HJ * S].rearrange("r (h s) -> r h s", s=S)[:, h0:h1, s0:s1]

                def k_of(n, k, t0, t1, rows=R):
                    return ks[0:rows, hd.buf(n), k * S + t0:k * S + t1]

                def max_chunk(U, c):
                    n, k = divmod(U, KJ)
                    C = U * hd.chunks + c
                    if C >= 2:
                        pe.wait_ge(sem("a_max"), hd.chunk0 + C - 1)
                    out = ps[:, MAX_BANK + C % 2, :]
                    if not hd.causal:
                        st, hp = divmod(c, 2)
                        for i in (0, 1):
                            h = 4 * k + 2 * hp + i
                            ins = pe.matmul(out[:, i * S:(i + 1) * S], q_of(n, h, h + 1, st * P, st * P + P, 4 * D),
                                            k_of(n, k, 0, S, 4 * D), start=i == 0, stop=i == 1, skip_group_check=True)
                    elif c == 0:
                        for i in range(4):
                            h = 4 * k + i
                            pe.matmul(out[:, i * P:(i + 1) * P], q_of(n, h, h + 1, 0, P, 4 * D),
                                      k_of(n, k, 0, P, 4 * D), start=i == 0, stop=False, skip_group_check=True)
                        ins = pe.matmul(out, identb[:, :], mask_q[:, :], start=False, stop=True, skip_group_check=True)
                    else:
                        for i in (0, 1):
                            h = 4 * k + 2 * (c - 1) + i
                            pe.matmul(out[:, i * S:(i + 1) * S], q_of(n, h, h + 1, P, S, 4 * D),
                                      k_of(n, k, 0, S, 4 * D), start=i == 0, stop=False, skip_group_check=True)
                        ins = pe.matmul(out.rearrange("p (h t) -> p h t", t=S)[:, :, P:S], identb[:, :],
                                        mask_q[:, 0:S], start=False, stop=True, skip_group_check=True)
                    ins.then_inc(sem("a_rows"), 1)

                def scores(U, tt):
                    n, k = divmod(U, KJ)
                    if U >= 1:
                        pe.wait_ge(sem(f"a_e{tt}"), hd.unit0 + U)
                    bank = ST_BANK + 2 * tt
                    kt = k_of(n, k, tt * P, (tt + 1) * P)
                    if hd.causal and tt == 1:
                        pe.matmul(ps[:, bank, :], kt, q_of(n, 4 * k, 4 * k + 4, P, S), start=True, stop=False,
                                  skip_group_check=True)
                        ins = pe.matmul(ps[:, bank, :], identb[:, :], mask_k[:, :], start=False, stop=True,
                                        skip_group_check=True)
                    else:
                        for i in (0, 1):
                            ins = pe.matmul(ps[:, bank + i, :], kt, q_of(n, 4 * k + 2 * i, 4 * k + 2 * i + 2),
                                            start=True, stop=not hd.causal, skip_group_check=True)
                            if hd.causal:
                                ins = pe.matmul(ps[:, bank + i, :].rearrange("p (h s) -> p h s", s=S)[:, :, 0:P],
                                                identb[:, :], mask_k[:, 0:S], start=False, stop=True,
                                                skip_group_check=True)
                    ins.then_inc(sem(f"a_st{tt}"), 1)

                def values(U):
                    n, k = divmod(U, KJ)
                    b, j = divmod(n, 2)
                    if U >= 1:
                        pe.wait_ge(sem("a_ot"), hd.unit0 + U)
                    pe.wait_ge(sem("a_e0"), hd.unit0 + U + 1)
                    pe.wait_ge(sem("a_e1"), hd.unit0 + U + 1)
                    for tt in (0, 1):
                        vt = v[:, 2 * b + tt, j * KJ + k, :]
                        for i in (0, 1):
                            cg = 2 * tt + i
                            o = ps[32 * cg:32 * cg + 32, OT_BANK, :]
                            if hd.causal and tt == 1:
                                o = o.rearrange("p (h s) -> p h s", s=S)[:, :, P:S]
                                r = e[:, U % 2, 1, i * S:(i + 1) * S]
                            else:
                                r = e[:, U % 2, tt, i * 512:(i + 1) * 512]
                            ins = pe.matmul(o, vt, r, start=True, stop=True)
                    ins.then_inc(sem("a_pv"), 1)

                def gather(U):
                    pe.wait_ge(sem("a_ot"), hd.unit0 + U + 1)
                    if U >= 1:
                        pe.wait_ge(sem("a_att"), hd.unit0 + U)
                    d1 = D + 1
                    for st in (0, 1):
                        o = ps[:, SUM_BANK, st * 4 * d1:(st + 1) * 4 * d1].rearrange("p (i g d) -> p i g d", i=2, g=2)
                        rows = 64 if hd.causal and st == 0 else P
                        for g in (0, 1):
                            ins = pe.matmul(o[:, :, g, :], ot[0:rows, U % 2, g * S + st * P:g * S + st * P + P],
                                            sel[0:rows, :], start=st == 0 and g == 0, stop=st == 1 and g == 1,
                                            skip_group_check=True)
                    ins.then_inc(sem("a_sum"), 1)

                def turn_max(n, gathered):
                    pe.wait_ge(sem("a_max"), hd.chunk0 + (n + 1) * KJ * hd.chunks)
                    if gathered:
                        pe.wait_ge(sem("a_att"), hd.unit0 + gathered)
                    pe.transpose(ps[0:2 * hd.HJ, SUM_BANK, 384:512],
                                 mx[:, n % 2, 0:2 * hd.HJ], ident[:, :]).then_inc(sem("a_mt"), 1)

                for s in units(hd):
                    mU, sU, vU, gU = s, s - KJ - 1, s - KJ - 2, s - KJ - 3
                    step_begins = mU % KJ == 0 and mU < hd.units
                    if step_begins:
                        n = mU // KJ
                        pe.wait_ge(sem(f"a_q{hd.buf(n)}"), 80 * hd.uses(n))
                    if mU < hd.units:
                        max_chunk(mU, 0)
                    if 0 <= sU < hd.units:
                        if sU % KJ == 0:
                            n = sU // KJ
                            pe.wait_ge(sem(f"a_m{hd.buf(n)}"), 64 * hd.uses(n))
                        scores(sU, 0)
                    if mU < hd.units:
                        max_chunk(mU, 1)
                    if mU % KJ == 0 and 0 < mU <= hd.units:
                        turn_max(mU // KJ - 1, max(0, gU))
                    if 0 <= vU < hd.units:
                        values(vU)
                    if mU < hd.units:
                        max_chunk(mU, 2)
                    if 0 <= sU < hd.units:
                        scores(sU, 1)
                    if 0 <= gU < hd.units:
                        pe.wait_ge(sem("a_mlo"), hd.step0 + min(mU // KJ, hd.steps))
                        gather(gU)
                    if mU < hd.units and hd.chunks == 4:
                        max_chunk(mU, 3)


            def project():
                pe.wait_ge(sem("lo_ready"), bank_at("o2", 4))
                for i in range(4):
                    for t in (2 * i, 2 * i + 1):
                        tok = slice(t * P, (t + 1) * P)
                        parts = [(zh[:, j, tok], zl[:, j, tok], dense_h[:, 1, j, :], dense_l[:, 1, j, :])
                                 for j in (0, 1)]
                        ins = product3(pe, ps[:, (0, 1, 6, 7)[i], (t % 2) * H:(t % 2 + 1) * H], parts, True, True)
                    ins.then_inc(sem("o2_y"), 1)

            def experts3():
                for pair in range(4):
                    eb = pair % 2
                    pe.wait_ge(sem(f"f3_split{eb}"), pair // 2 + 1)
                    if pair == 0:
                        pe.wait_ge(sem("bias3_ready"), 32)
                    for t in range(TILES):
                        n = pair * TILES + t
                        if n >= 4:
                            pe.wait_ge(sem("f3_add"), n - 3)
                        tok = slice(t * P, (t + 1) * P)
                        o = ps[:, n % 4, :]
                        pe.matmul(o, ones2[:, :], b3(pair), start=True, stop=False, skip_group_check=True)
                        parts = [(zh[:, j, tok], zl[:, j, tok], wh[:, eb, j * 512:(j + 1) * 512],
                                  wl[:, eb, j * 512:(j + 1) * 512]) for j in (0, 1)]
                        product3(pe, o, parts, False, True).then_inc(sem("f3_y"), 1)

            attention0()
            turn("f0")
            logits(0)
            experts(0)
            turn("a1")
            attention(1)
            turn("f1")
            logits(1)
            experts(1)
            turn("a2")
            attention(2)
            turn("o2")
            project()
            turn("f2")
            logits(2)
            experts(2)
            turn("a3")
            attention(3)
            turn("f3")
            logits(3)
            experts3()


        @block.scalar
        def _(act):
            def split_hi(tag):
                for u in range(4):
                    hf, j = divmod(u, 2)
                    act.wait_ge(sem("turned"), bank_at(tag, u + 1))
                    act.copy(zh[:, j, hf * HALF:(hf + 1) * HALF], ps[:, T_BANK + u, :]).then_inc(sem("hi_ready"), 1)

            def attention0():
                act.wait_ge(sem("l_ctxT"), 48)
                for m, dst in ((0, a0q), (1, a0k)):
                    for hf in (0, 1):
                        act.wait_ge(sem("a0_proj"), 2 * m + hf + 1)
                        act.activation(dst[:, hf * HALF:(hf + 1) * HALF], ps[0:CTX, 2 * m + hf, :], ACT.Identity,
                                       bias=bqk[:, m:m + 1]).then_inc(sem("a0_qk"), 1)
                act.wait_ge(sem("kr_turned"), 1)
                act.copy(hi16.rearrange("p (a b) -> p a b", a=2), ps[0:CTX, 4:6, :]).then_inc(sem("k16_split"), 1)
                act.wait_ge(sem("a0_nmx"), 1)
                for t in range(TILES):
                    act.activation(a0s[:, t, :], a0s[:, t, :], ACT.Exp, bias=nmx[:, t:t + 1],
                                   accum_out=rsum[:, t:t + 1]).then_inc(sem("a0_exp"), 1)

            def gate(L):
                if L != 1:
                    act.wait_ge(sem(f"f{L}_gd"), 1)
                    act.activation(gp[:, :, 0:ROUTED[L]], gp[:, :, 0:ROUTED[L]], ACT.Exp).then_inc(sem(f"f{L}_ge"), 1)

            def experts(L):
                gated = L != 1
                n_pair = NEXP[L] // 2

                def pair_units(pair, first):
                    for k in range(4):
                        hf = k % 2
                        unit = pair * 4 + k
                        early = first and k < 2
                        act.wait_ge(sem(f"f{L}_g" if gated else f"f{L}_u"), unit + 1)
                        if not early:
                            act.wait_ge(sem(f"f{L}_gu" if gated else f"f{L}_hm"), unit - 1)
                        act.activation(sg[:, hf, :], ps[:, G_BANK if gated else G_BANK + hf, :],
                                       ACT.Silu if gated else ACT.Relu).then_inc(sem(f"f{L}_act"), 1)
                        if gated and first and k == 0:
                            act.wait_ge(sem(f"f{L}_wturned"), 1)
                            act.copy(wT[0:ROUTED[L], 0, :].rearrange("e (a b) -> e a b", a=2),
                                     ps[0:ROUTED[L], W_BANK:W_BANK + 2, :]).then_inc(sem(f"f{L}_whi"), 1)
                        act.wait_ge(sem(f"f{L}_hm"), unit + 1)
                        if not early:
                            act.wait_ge(sem(f"f{L}_down"), unit - 1)
                        act.copy(hh[:, hf, :], hm[:, hf, :]).then_inc(sem(f"f{L}_hh"), 1)

                if L == 0:
                    act.wait_ge(sem("k8_stored"), 64)
                pair_units(0, True)
                with act.Fori(1, n_pair) as pair:
                    pair_units(pair, False)
                act.wait_ge(sem(f"f{L}_down"), 4 * n_pair)
                act.copy(acc[:, 0, :].rearrange("p (a b) -> p a b", a=2), ps[:, 0:2, :]).then_inc(sem(f"f{L}_acc"), 1)

            def attention(L):
                hd = grouped[L]
                for s in units(hd):
                    mU, sU, vU = s, s - hd.KJ - 1, s - hd.KJ - 2
                    for tt in (0, 1):
                        if 0 <= sU < hd.units:
                            act.wait_ge(sem(f"a_st{tt}"), hd.unit0 + sU + 1)
                            if sU >= 2:
                                act.wait_ge(sem("a_pv"), hd.unit0 + sU - 1)
                            if hd.causal and tt == 1:
                                dst, src = e[:, sU % 2, 1, 0:512], ps[:, ST_BANK + 2, :]
                            else:
                                dst = e[:, sU % 2, tt, :].rearrange("p (a b) -> p a b", a=2)
                                src = ps[:, ST_BANK + 2 * tt:ST_BANK + 2 * tt + 2, :]
                            act.activation(dst, src, ACT.Exp, scale=hd.scale).then_inc(sem(f"a_e{tt}"), 1)
                        if tt:
                            continue
                        if mU % hd.KJ == 0 and 0 < mU <= hd.units:
                            n = mU // hd.KJ - 1
                            act.wait_ge(sem("a_mt"), hd.step0 + n + 1)
                            if n >= 2:
                                act.wait_ge(sem(f"a_m{hd.buf(n - 2)}"), 64 * hd.uses(n - 2))
                            act.copy(mT[0:2 * hd.HJ, n % 2, 0, :], ps[0:2 * hd.HJ, SUM_BANK, 384:512]
                                     ).then_inc(sem("a_mhi"), 1)
                        if 0 <= vU < hd.units:
                            act.wait_ge(sem("a_pv"), hd.unit0 + vU + 1)
                            if vU >= 2:
                                act.wait_ge(sem("a_sum"), hd.unit0 + vU - 1)
                            if hd.causal:
                                act.copy(ot[0:64, vU % 2, :], ps[0:64, OT_BANK, :])
                                cut = "p (h s) -> p h s"
                                act.copy(ot[64:P, vU % 2, :].rearrange(cut, s=S)[:, :, P:S],
                                         ps[64:P, OT_BANK, :].rearrange(cut, s=S)[:, :, P:S]
                                         ).then_inc(sem("a_ot"), 1)
                            else:
                                act.copy(ot[:, vU % 2, :], ps[:, OT_BANK, :]).then_inc(sem("a_ot"), 1)

            def squares():
                act.wait_ge(sem("a2_q"), 8)
                for t in range(TILES):
                    act.activation(ef[:, 3072:3072 + H], z[:, t, :], ACT.Square,
                                   accum_out=rsum[:, t:t + 1]).then_inc(sem("a2_sq"), 1)
                    act.wait_ge(sem("a2_sq"), t + 1)

            attention0()
            split_hi("f0")
            gate(0)
            experts(0)
            split_hi("a1")
            attention(1)
            split_hi("f1")
            experts(1)
            squares()
            split_hi("a2")
            attention(2)
            split_hi("o2")
            split_hi("f2")
            gate(2)
            experts(2)
            split_hi("a3")
            attention(3)
            split_hi("f3")
            gate(3)

        @block.vector
        def _(dve):
            c = Chain(dve, sem("dve_step"))

            def inverse_root(v, scale):
                c.step(dve.tensor_scalar(var[:, :], v, scale, EPS, ALU.mult, ALU.add))
                c.step(dve.tensor_scalar(rstd[:, :].bitcast(I32), var[:, :].bitcast(I32), -0.5, ROOT_GUESS,
                                         ALU.mult, ALU.add))
                for _ in range(3):
                    c.step(dve.tensor_tensor(root[:, :], rstd[:, :], rstd[:, :], ALU.mult))
                    c.step(dve.scalar_tensor_tensor(root[:, :], root[:, :], -0.5, var[:, :], ALU.mult, ALU.mult))
                    c.step(dve.scalar_tensor_tensor(rstd[:, :], root[:, :], 1.5, rstd[:, :], ALU.add, ALU.mult))

            def normalise(src, dst, signal=None, D=None):
                for t in range(TILES):
                    c.mark(dve.bn_stats(bst[:, t, :], src[:, t, :]))
                c.join()
                for t in range(TILES):
                    c.mark(dve.bn_aggr(mv[:, t, :], bst[:, t, :]))
                c.join()
                inverse_root(mv[:, :, 1], 1.0)
                for t in range(TILES):
                    o, i = dst[:, t, :], src[:, t, :]
                    if D:
                        o = o.rearrange("p (j d h) -> p j d h", j=2, d=D)
                        i = i.rearrange("p (j h d) -> p j d h", j=2, d=D)
                    ins = dve.tensor_scalar(o, i, mv[:, t, 0:1], rstd[:, t:t + 1],
                                            ALU.subtract, ALU.mult)
                    if signal:
                        ins.then_inc(sem(signal), 1)
                    else:
                        c.mark(ins)

            def split_lo(tag):
                for u in range(4):
                    hf, j = divmod(u, 2)
                    tok = slice(hf * HALF, (hf + 1) * HALF)
                    dve.wait_ge(sem("hi_ready"), bank_at(tag, u + 1))
                    dve.tensor_tensor(zl[:, j, tok], ps[:, T_BANK + u, :], zh[:, j, tok].bitcast(F32),
                                      ALU.subtract).then_inc(sem("lo_ready"), 1)

            def rotate(src, dst, tmp, J, heads):
                q = src.rearrange("p (b t) (j h d) -> p b t j h d", t=2, j=J, d=16)
                o = dst.rearrange("p (b t) (j d h) -> p b t j h d", t=2, j=J, d=16)
                w = tmp.rearrange("p (b h d) -> p b h d", b=B, d=16)
                for st in (0, 1):
                    cb = cosr[:, st:st + 1, :].rearrange("p (a b) d -> p a b d", a=1)
                    sb_ = sinr[:, st:st + 1, :].rearrange("p (a b) d -> p a b d", a=1)
                    for j in range(J):
                        c.mark(dve.tensor_tensor(o[:, :, st, j], q[:, :, st, j],
                                                 cb.broadcast_to([P, B, heads, 16]), ALU.mult))
                        for lo, hi in ((0, 8), (8, 0)):
                            c.mark(dve.tensor_tensor(w[:, :, :, lo:lo + 8], q[:, :, st, j, :, hi:hi + 8],
                                                     sb_[:, :, :, lo:lo + 8].broadcast_to([P, B, heads, 8]), ALU.mult))
                        c.join()
                        c.step(dve.tensor_tensor(o[:, :, st, j], o[:, :, st, j], w, ALU.add))

            def keys():
                dve.wait_ge(sem("l_ctxT"), 48)
                dve.tensor_copy(hi8, ctxT[:, :]).then_inc(sem("k8_split"), 1)
                dve.wait_ge(sem("k8_split"), 1)
                dve.tensor_tensor(lo8, ctxT[:, :], hi8.bitcast(F32), ALU.subtract).then_inc(sem("k8_split"), 1)
                dve.wait_ge(sem("l_ctx"), 64)
                sq = ef[:, 0:TILES * CTX].rearrange("p (t d) -> p t d", d=CTX)
                kn = ef[:, 1024:1024 + TILES * CTX].rearrange("p (t d) -> p t d", d=CTX)
                c.step(dve.tensor_tensor(sq, ctxt[:, :, :], ctxt[:, :, :], ALU.mult))
                c.step(dve.tensor_reduce(rsum[:, :], sq, AX_X, ALU.add))
                inverse_root(rsum[:, :], 1.0 / CTX)
                c.step(dve.tensor_tensor(kn, ctxt[:, :, :],
                                         rstd[:, :].rearrange("p (t o) -> p t o", o=1).broadcast_to([P, TILES, CTX]),
                                         ALU.mult))
                c.step(dve.tensor_tensor(kn, kn, kw[:, :].rearrange("p (o d) -> p o d", o=1)
                                         .broadcast_to([P, TILES, CTX]), ALU.mult))
                rotate(kn, kr[:, :, :], ef[:, 512:768], 1, 4)
                dve.tensor_copy(kn[:, 0:1, 0:1], kr[:, 0:1, 0:1]).then_inc(sem("kr_ready"), 1)

            def attention0():
                dve.memset(ks8[32:34, :, :].bitcast(F32), -1.0).then_inc(sem("minus_ones"), 1)
                dve.memset(ks16[64:66, :, :].bitcast(F32), -1.0).then_inc(sem("minus_ones"), 1)
                dve.memset(ones2f[:, :], 1.0).then_inc(sem("ones_f"), 1)
                dve.wait_ge(sem("ones_f"), 1)
                dve.tensor_copy(ones2[:, :], ones2f[:, :]).then_inc(sem("ones_ready"), 1)
                keys()
                dve.wait_ge(sem("l_x"), 16)
                normalise(x, z, "a0_z")
                dve.wait_ge(sem("l_mask"), 32)
                for b in range(B):
                    ins = dve.tensor_tensor(mask8[:, 2 * b:2 * b + 2, :], m1[:, :, :].bitcast(U8),
                                            m2[:, b:b + 1, :].bitcast(U8).broadcast_to([P, 2, S]), ALU.max)
                    c.mark(ins)
                dve.wait_ge(sem("k16_split"), 1)
                dve.tensor_tensor(lo16.rearrange("p (a b) -> p a b", a=2), ps[0:CTX, 4:6, :],
                                  hi16.rearrange("p (a b) -> p a b", a=2).bitcast(F32), ALU.subtract
                                  ).then_inc(sem("k16_split"), 1)
                hidden = attn[:, :, :].rearrange("p a b -> p (a b)")
                c.mark(dve.memset(hidden, MASKED))
                dve.wait_ge(sem("a0_z"), TILES)
                for i in range(4):
                    dve.wait_ge(sem("a0_scores"), i + 1)
                    c.mark(dve.scalar_tensor_tensor(a0s[:, 2 * i:2 * i + 2, :],
                                                    ps[:, 4 + i, :].rearrange("p (t s) -> p t s", s=S), CTX ** -0.5,
                                                    z[:, 2 * i:2 * i + 2, :], ALU.mult, ALU.mult))
                c.join()
                for t in range(TILES):
                    c.mark(dve.copy_predicated(a0s[:, t, :], mask8[:, t, :], hidden))
                c.join()
                c.step(dve.tensor_reduce(ga[:, :], a0s, AX_X, ALU.max))
                dve.tensor_scalar(nmx[:, :], ga[:, :], -1.0, None, ALU.mult).then_inc(sem("a0_nmx"), 1)
                for t in range(TILES):
                    dve.wait_ge(sem("a0_exp"), t + 1)
                    c.step(dve.reciprocal(gb[:, t:t + 1], rsum[:, t:t + 1]))
                    c.mark(dve.scalar_tensor_tensor(x[:, t, :], a0s[:, t, :], gb[:, t:t + 1], x[:, t, :],
                                                    ALU.mult, ALU.add))
                c.join()

            def choose(L, k, width):
                W = width + 8 - k
                for t in range(TILES):
                    c.mark(dve.max(g8[:, t, :], gs[:, t, 0:W]))
                c.join()
                if L == 3:
                    c.mark(dve.tensor_copy(ga[:, :], g8[:, :, 0]))
                c.step(dve.memset(g8[:, :, k:8], SENTINEL))
                for t in range(TILES):
                    c.mark(dve.match_replace(gr[:, t, 0:W], g8[:, t, :], gs[:, t, 0:W], TAKEN))
                c.join()
                c.step(dve.tensor_scalar(gr[:, :, 0:width], gr[:, :, 0:width], TAKEN, None, ALU.is_equal))

            def per_tile(v, n):
                return v[:, :].rearrange("p (t o) -> p t o", o=1).broadcast_to([P, TILES, n])

            def gate(L):
                E = ROUTED[L]
                dve.wait_ge(sem("logits"), L + 1)
                lg = ps[:, LOGIT_BANK, 0:TILES * E].rearrange("p (t e) -> p t e", e=E)
                p_ = gp[:, :, 0:E]
                if L == 1:
                    for t in range(TILES):
                        c.mark(dve.max(g8[:, t, :], lg[:, t, :]))
                    c.join()
                    c.step(dve.tensor_tensor(ga[:, :], g8[:, :, 0], g8[:, :, 1], ALU.add))
                    return
                if L == 3:
                    c.mark(dve.memset(gs[:, :, E:E + 6], SENTINEL))
                    c.step(dve.tensor_copy(gs[:, :, 0:E], lg))
                    choose(3, 2, E)
                    dve.tensor_tensor(p_, gs[:, :, 0:E], per_tile(ga, E), ALU.subtract).then_inc(sem("f3_gd"), 1)
                    dve.wait_ge(sem("f3_ge"), 1)
                    c.step(dve.tensor_tensor(gw[:, :, 0:E], gr[:, :, 0:E], p_, ALU.mult))
                    c.step(dve.tensor_reduce(ga[:, :], gw[:, :, 0:E], AX_X, ALU.add))
                    c.step(dve.reciprocal(gb[:, :], ga[:, :]))
                    c.step(dve.tensor_tensor(gw[:, :, 0:E], gw[:, :, 0:E], per_tile(gb, E), ALU.mult))
                    return
                c.step(dve.tensor_reduce(ga[:, :], lg, AX_X, ALU.max))
                dve.tensor_tensor(p_, lg, per_tile(ga, E), ALU.subtract).then_inc(sem(f"f{L}_gd"), 1)
                k = 2 if L == 0 else 4
                c.mark(dve.memset(gs[:, :, E:E + 8 - k], SENTINEL))
                dve.wait_ge(sem(f"f{L}_ge"), 1)
                c.step(dve.tensor_reduce(ga[:, :], p_, AX_X, ALU.add))
                c.step(dve.reciprocal(gb[:, :], ga[:, :]))
                if L == 0:
                    c.step(dve.tensor_tensor(p_, p_, per_tile(gb, E), ALU.mult))
                    dve.wait_ge(sem("l_rows"), 64)
                    c.step(dve.tensor_tensor(gs[:, :, 0:E], p_, bias0[:, :].rearrange("p (o e) -> p o e", o=1)
                                             .broadcast_to([P, TILES, E]), ALU.add))
                    choose(0, 2, E)
                    dve.scalar_tensor_tensor(gw[:, :, 0:E], gr[:, :, 0:E], 1.5, p_, ALU.mult, ALU.mult
                                             ).then_inc(sem("f0_w"), 1)
                else:
                    c.step(dve.tensor_tensor(gs[:, :, 0:E], p_, per_tile(gb, E), ALU.mult))
                    choose(2, 4, E)
                    dve.tensor_tensor(gw[:, :, 0:E], gr[:, :, 0:E], gs[:, :, 0:E], ALU.mult).then_inc(sem("f2_w"), 1)

            def experts(L):
                gated = L != 1
                n_pair = NEXP[L] // 2

                def pair_units(pair, first):
                    for k in range(4):
                        hf = k % 2
                        unit = pair * 4 + k
                        early = first and k < 2
                        dve.wait_ge(sem(f"f{L}_act"), unit + 1)
                        dve.wait_ge(sem(f"f{L}_u"), unit + 1)
                        if gated:
                            dve.tensor_tensor(t1[:, hf, :], sg[:, hf, :], ps[:, U_BANK, :], ALU.mult
                                              ).then_inc(sem(f"f{L}_gu"), 1)
                            dve.wait_ge(sem(f"f{L}_gu"), unit + 1)
                            dve.wait_ge(sem(f"f{L}_spread"), unit + 1)
                        if not early:
                            dve.wait_ge(sem(f"f{L}_hh"), unit - 1)
                        if gated:
                            ins = dve.tensor_tensor(hm[:, hf, :], t1[:, hf, :], ps[:, W_BANK, :], ALU.mult)
                        else:
                            ins = dve.tensor_tensor(hm[:, hf, :], sg[:, hf, :], ps[:, G_BANK + hf, :], ALU.mult)
                        ins.then_inc(sem(f"f{L}_hm"), 1)
                        dve.wait_ge(sem(f"f{L}_hh"), unit + 1)
                        if not early:
                            dve.wait_ge(sem(f"f{L}_down"), unit - 1)
                        dve.tensor_tensor(hl[:, hf, :], hm[:, hf, :], hh[:, hf, :].bitcast(F32), ALU.subtract
                                          ).then_inc(sem(f"f{L}_hl"), 1)

                if gated:
                    E = ROUTED[L]
                    dve.wait_ge(sem(f"f{L}_whi"), 1)
                    cut = "e (a b) -> e a b"
                    dve.tensor_tensor(wT[0:E, 1, :].rearrange(cut, a=2), ps[0:E, W_BANK:W_BANK + 2, :],
                                      wT[0:E, 0, :].rearrange(cut, a=2).bitcast(F32), ALU.subtract
                                      ).then_inc(sem(f"f{L}_wlo"), 1)
                if L == 0:
                    dve.wait_ge(sem("f0_w"), 1)
                    c.step(dve.tensor_reduce(gb[:, :], gw[:, :, 8:12], AX_X, ALU.add))
                    for t in range(TILES):
                        c.mark(dve.scalar_tensor_tensor(x[:, t, :], z[:, t, :], gb[:, t:t + 1], x[:, t, :],
                                                        ALU.mult, ALU.add))
                    dve.wait_ge(sem("k8_stored"), 64)
                pair_units(0, True)
                with dve.Fori(1, n_pair) as pair:
                    pair_units(pair, False)
                dve.wait_ge(sem(f"f{L}_down"), 4 * n_pair)
                dve.tensor_copy(acc[:, 1, :].rearrange("p (a b) -> p a b", a=2), ps[:, 2:4, :]
                                ).then_inc(sem(f"f{L}_acc"), 1)
                c.join()
                if L == 1:
                    for i in range(4):
                        dve.wait_ge(sem("f1_moe"), i + 1)
                        c.mark(dve.tensor_scalar(z[:, 2 * i, :], ps[:, 4 + i, 0:H], ga[:, 2 * i:2 * i + 1], None,
                                                 ALU.mult))
                        c.join()
                        dve.tensor_scalar(z[:, 2 * i + 1, :], ps[:, 4 + i, H:2 * H], ga[:, 2 * i + 1:2 * i + 2], None,
                                          ALU.mult).then_inc(sem("f1_moe_read"), 1)
                    dve.wait_ge(sem("f1_moe_read"), 4)
                base = z if L == 1 else x
                for i in range(4):
                    dve.wait_ge(sem(f"f{L}_back"), i + 1)
                    o = base[:, 2 * i:2 * i + 2, :]
                    c.mark(dve.tensor_tensor(o, ps[:, 4 + i, :].rearrange("p (t d) -> p t d", d=H), o, ALU.add))
                c.join()
                if L == 1:
                    normalise(z, z)
                    c.join()
                    for row, op in ((gamma, ALU.mult), (beta, ALU.add)):
                        c.step(dve.tensor_tensor(z[:, :, :], z[:, :, :], row[:, :].rearrange("p (o d) -> p o d", o=1)
                                                 .broadcast_to([P, TILES, H]), op))
                    c.step(dve.tensor_tensor(x[:, :, :], x[:, :, :], z[:, :, :], ALU.add))

            def attention(L):
                hd = grouped[L]
                D, KJ, HJ, d1 = hd.D, hd.KJ, hd.HJ, hd.D + 1

                def maxima(U, ch):
                    n, k = divmod(U, KJ)
                    C = U * hd.chunks + ch
                    dve.wait_ge(sem("a_rows"), hd.chunk0 + C + 1)
                    if n >= 2 and U % KJ == 0 and ch == 0:
                        dve.wait_ge(sem("a_mt"), hd.step0 + n - 1)
                    bank = ps[:, MAX_BANK + C % 2, :]
                    if hd.causal:
                        w, st = (P, 0) if ch == 0 else (S, 1)
                        h0 = 4 * k + (0 if ch == 0 else 2 * (ch - 1))
                    else:
                        w, st, h0 = S, ch // 2, 4 * k + 2 * (ch % 2)
                    dve.tensor_reduce(mx[:, n % 2, st * HJ + h0:st * HJ + h0 + 512 // w], bank.rearrange("p (h t) -> p h t", t=w),
                                      AX_X, ALU.max).then_inc(sem("a_max"), 1)

                def collect(U):
                    n, k = divmod(U, KJ)
                    dve.wait_ge(sem("a_sum"), hd.unit0 + U + 1)
                    dve.tensor_copy(att[:, n % 2, :, k * 4 * d1:(k + 1) * 4 * d1],
                                    ps[:, SUM_BANK, 0:8 * d1].rearrange("p (t q) -> p t q", t=2)
                                    ).then_inc(sem("a_att"), 1)

                def finish(n):
                    b, j = divmod(n, 2)
                    dve.wait_ge(sem("a_att"), hd.unit0 + (n + 1) * KJ)
                    v = att[:, n % 2, :, 0:HJ * d1].rearrange("p t (h d) -> p t h d", d=d1)
                    c.step(dve.reciprocal(attr[:, :, 0:HJ], v[:, :, :, D]))
                    r = attr[:, :, 0:HJ].rearrange("p t (h o) -> p t h o", o=1).broadcast_to([P, 2, HJ, D])
                    c.step(dve.tensor_tensor(attn[:, :, :].rearrange("p t (h d) -> p t h d", d=D),
                                             v[:, :, :, 0:D], r, ALU.mult))
                    cols = slice(j * P, (j + 1) * P)
                    if hd.causal:
                        dve.tensor_copy(z[:, 2 * b:2 * b + 2, cols], attn[:, :, :]).then_inc(sem("z_ready"), 1)
                    else:
                        c.step(dve.tensor_tensor(x[:, 2 * b:2 * b + 2, cols], x[:, 2 * b:2 * b + 2, cols],
                                                 attn[:, :, :], ALU.add))

                for s in units(hd):
                    mU, gU = s, s - KJ - 3
                    if mU < hd.units:
                        maxima(mU, 0)
                        maxima(mU, 1)
                    if mU % KJ == 0 and 0 < mU <= hd.units:
                        n = mU // KJ - 1
                        dve.wait_ge(sem("a_mhi"), hd.step0 + n + 1)
                        dve.tensor_tensor(mT[0:2 * HJ, n % 2, 1, :], ps[0:2 * HJ, SUM_BANK, 384:512],
                                          mT[0:2 * HJ, n % 2, 0, :].bitcast(F32), ALU.subtract
                                          ).then_inc(sem("a_mlo"), 1)
                    if mU < hd.units:
                        for ch in range(2, hd.chunks):
                            maxima(mU, ch)
                    if 0 <= gU < hd.units:
                        collect(gU)
                        if gU % KJ == KJ - 1:
                            finish(gU // KJ)

            def queries():
                normalise(x, z, "a2_q")
                dve.wait_ge(sem("a2_sq"), TILES)
                inverse_root(rsum[:, :], 1.0 / H)
                qn = ef[:, 0:2048].rearrange("p (t d) -> p t d", d=H)
                for t in range(TILES):
                    c.mark(dve.scalar_tensor_tensor(qn[:, t, :], z[:, t, :], rstd[:, t:t + 1], qw[:, :],
                                                    ALU.mult, ALU.mult))
                c.join()
                rotate(qn, z[:, :, :], ef[:, 2048:2560], 2, 8)
                for t in range(TILES):
                    dve.sem_inc(sem("z_ready"), 1)

            def project():
                for i in range(4):
                    dve.wait_ge(sem("o2_y"), i + 1)
                    o = x[:, 2 * i:2 * i + 2, :]
                    c.mark(dve.tensor_tensor(o, ps[:, (0, 1, 6, 7)[i], :].rearrange("p (t d) -> p t d", d=H), o,
                                             ALU.add))
                c.join()

            def experts3():
                for pair in range(4):
                    for t in range(TILES):
                        n = pair * TILES + t
                        dve.wait_ge(sem("f3_y"), n + 1)
                        for i in (0, 1):
                            ins = dve.scalar_tensor_tensor(x[:, t, :], ps[:, n % 4, i * H:(i + 1) * H],
                                                           gw[:, t, 2 * pair + i:2 * pair + i + 1], x[:, t, :],
                                                           ALU.mult, ALU.add)
                            if i == 0:
                                c.step(ins)
                            else:
                                ins.then_inc(sem("f3_add"), 1)

            attention0()
            dve.wait_ge(sem("l_ident"), 16)
            dve.wait_ge(sem("l_att"), 48)
            c.mark(dve.tensor_copy(identb[:, :], ident[:, :]))
            for m, mask in enumerate((mask_q, mask_k)):
                c.mark(dve.tensor_copy(mask[:, :].rearrange("p (g s) -> p g s", g=4),
                                       hide[:, m * P:(m + 1) * P].rearrange("p (o s) -> p o s", o=1)
                                       .broadcast_to([P, 4, P])))
            c.join()
            normalise(x, z, "z_ready")
            split_lo("f0")
            gate(0)
            experts(0)
            normalise(x, z, "z_ready", 8)
            split_lo("a1")
            attention(1)
            normalise(x, z, "z_ready")
            split_lo("f1")
            gate(1)
            experts(1)
            queries()
            split_lo("a2")
            attention(2)
            split_lo("o2")
            project()
            normalise(x, z, "z_ready")
            split_lo("f2")
            gate(2)
            experts(2)
            normalise(x, z, "z_ready", 8)
            split_lo("a3")
            attention(3)
            normalise(x, z, "z_ready")
            split_lo("f3")
            gate(3)
            experts3()


def constants():
    i = np.arange(P)
    hide = np.where(i[None, :] > i[:, None], -1e30, 0.0).astype(np.float32)
    inv = 1.0 / 10000.0 ** (np.arange(0, 16, 2, dtype=np.float32) / 16)
    angle = np.outer(np.arange(S, dtype=np.float32), inv.astype(np.float32)).astype(np.float32)
    angle = np.concatenate([angle, angle], -1)
    cos, sin = np.cos(angle), np.sin(angle)
    sin[:, :8] *= -1.0
    turn = lambda v: np.ascontiguousarray(v.reshape(2, P, 16).transpose(1, 0, 2)).astype(np.float32)
    sel = {}
    for d in (8, 16):
        s = np.zeros((P, 2, d + 1), np.float32)
        for cg in range(4):
            for r in range(d + 1):
                s[32 * cg + r, cg % 2, r] = 1.0
        sel[d] = s.reshape(P, 2 * (d + 1))
    return {
        "ident": np.eye(P, dtype=np.float32), "hide": np.concatenate([hide, hide.T], axis=1),
        "cos": turn(cos), "sin": turn(sin), "sel8": sel[8], "sel16": sel[16],
    }


def kernel(**inp):
    import concourse.bacc as _bacc
    from concourse.bass_utils import run_bass_kernel_spmd as _run

    g = {k: np.asarray(v) for k, v in inp.items()}

    def rows(w):
        return w.reshape(2, P, -1).transpose(1, 0, 2)

    def packed(gate, up, down):
        flat = [w.reshape(-1, 2, P, P).transpose(0, 2, 1, 3).reshape(-1, P, 2 * P) for w in (gate, up) if w is not None]
        return np.concatenate(flat + [down], axis=2)

    by_kd = np.arange(CTX).reshape(8, 8).T.reshape(-1)
    arrays = dict(constants())
    arrays.update({
        "x": g["x"].reshape(TOK, H),
        "ctx": g["ctx_512"].reshape(TOK, CTX),
        "ctxP": g["ctx_512"].reshape(TOK, CTX).T[by_kd],
        "wqk": np.stack([g["L0_xattn_Wq"].T[by_kd], g["L0_xattn_Wk"].T[by_kd]], axis=1),
        "bqk": np.stack([g["L0_xattn_bq"], g["L0_xattn_bk"]], axis=1),
        "m1": np.ascontiguousarray(g["mask_SxS2_bk1"]).view(np.uint32),
        "m2": np.ascontiguousarray(g["mask_BxS2_bf0"]).view(np.uint32),
        "router": rows(np.concatenate([g["L0_ffn_classifier_w"].T, g["L1_ffn_gate_w"], g["L2_ffn_Wgate"].T,
                                       g["L3_ffn_gate_w"].T], axis=1)),
        "dense": np.stack([rows(g["L1_ffn_expert_weight"]), rows(g["L2_xattn_w_out"].T)], axis=1),
        "bias0": g["L0_ffn_e_score_correction_bias"],
        "bias3": g["L3_ffn_expert_b"],
        "gamma": g["L1_ffn_ln_gamma"], "beta": g["L1_ffn_ln_beta"],
        "qw": g["L2_xattn_q_norm_w"], "kw": g["L2_xattn_k_norm_w"],
        "experts0": packed(g["L0_ffn_gate_w"].transpose(0, 2, 1), g["L0_ffn_up_w"].transpose(0, 2, 1),
                           g["L0_ffn_down_w"].transpose(0, 2, 1)),
        "experts1": packed(None, g["L1_ffn_up_w"].reshape(H, 8, P).transpose(1, 0, 2),
                           g["L1_ffn_down_w"].reshape(8, P, H)),
        "experts2": packed(g["L2_ffn_Wg"], g["L2_ffn_Wu"], g["L2_ffn_Wd"]),
        "experts3": g["L3_ffn_expert_w"].transpose(0, 2, 1).reshape(4, 2, 2, P, H).transpose(0, 3, 2, 1, 4)
                     .reshape(4, P, 1024),
    })
    arrays = {f"in_{k}": np.ascontiguousarray(v) for k, v in arrays.items()}
    nc = _bacc.Bacc("TRN2", target_bir_lowering=False, num_devices=1)
    aps = {k[3:]: nc.dram_tensor(k, v.shape, mybir.dt.from_np(v.dtype), kind="ExternalInput").ap()
           for k, v in arrays.items()}
    out = nc.dram_tensor("out_x", (TOK, H), F32, kind="ExternalOutput").ap()
    build(nc, aps, out)
    r = _run(nc, [arrays], core_ids=[0])
    return r.results[0]["out_x"].reshape(B, S, H)
```

```python
from contextlib import ExitStack

import numpy as np

import concourse.bass as bass
from concourse import mybir

F32 = mybir.dt.float32
F32R = mybir.dt.float32r
BF16 = mybir.dt.bfloat16
I32 = mybir.dt.int32
U8 = mybir.dt.uint8
U32 = mybir.dt.uint32
ALU = mybir.AluOpType
ACT = mybir.ActivationFunctionType
AX_X = mybir.AxisListType.X

P = 128
B, S, H = 4, 256, 256
TOK = B * S
TILES = TOK // P
HALF = TOK // 2
CTX = 64
EPS = 1e-5
ROOT_GUESS = float(0x5F3759DF)
MASKED = -3.0e38
TURN_BANKS = {"a": ((0, 2), (6, 7)), "f": ((0, 1), (2, 3)), "o": ((0, 1), (2, 3))}
MAX_BANK = 0
ST_BANK = 2
OT_BANK, SUM_BANK = 6, 7
G_BANK, U_BANK, W_BANK, LOGIT_BANK = 4, 5, 6, 7
ROUTED = (12, 8, 32, 8)
ROUTER_AT = (0, 12, 20, 52)
SENTINEL = -3.0e38
TAKEN = 3.0e38


class Chain:

    def __init__(self, eng, sem):
        self.eng, self.sem, self.n = eng, sem, 0

    def mark(self, ins):
        ins.then_inc(self.sem, 1)
        self.n += 1

    def join(self):
        self.eng.wait_ge(self.sem, self.n)

    def step(self, ins):
        self.mark(ins)
        self.join()


def product3(pe, out, parts, start, stop):
    ins = None
    for n, (Lh, Ll, Rh, Rl) in enumerate(parts):
        first, last = n == 0, n == len(parts) - 1
        pe.matmul(out, Lh, Rh, start=start and first, stop=False, skip_group_check=True)
        pe.matmul(out, Lh, Rl, start=False, stop=False, skip_group_check=True)
        ins = pe.matmul(out, Ll, Rh, start=False, stop=stop and last, skip_group_check=True)
    return ins


TURNS = ("f0", "a1", "f1", "a2", "o2", "f2", "a3", "f3")


def z_at(tag, n):
    return TILES * TURNS.index(tag) + n


def bank_at(tag, n):
    return 4 * TURNS.index(tag) + n


class Head:

    def __init__(self, D, causal, before, peer=None):
        self.D, self.causal = D, causal
        self.HJ = P // D
        self.KJ = self.HJ // 4
        self.R = 4 * D + 2
        self.scale = D ** -0.5
        self.steps = 2 * B
        self.units = self.steps * self.KJ
        self.chunks = 3 if causal else 4
        self.bufs = 6 if causal else 3
        self.tile = "c" if causal else "g"
        self.first = peer.first + peer.steps if peer else 0
        self.step0 = before.step0 + before.steps if before else 0
        self.unit0 = before.unit0 + before.units if before else 0
        self.chunk0 = before.chunk0 + before.units * before.chunks if before else 0

    def buf(self, n):
        return (self.first + n) % self.bufs

    def uses(self, n):
        return (self.first + n) // self.bufs + 1

    def q_sem(self, n):
        return f"a_{self.tile}q{self.buf(n)}"

    def k_sem(self, n):
        return f"a_{self.tile}k{self.buf(n)}"

    def m_sem(self, n):
        return f"a_{self.tile}m{self.buf(n)}"


def build(nc, a, out):
    ctx = ExitStack()
    with ctx:
        def sb(name, shape, dt=F32):
            return ctx.enter_context(nc.sbuf_tensor(name, list(shape), dt))

        sems = {}

        def sem(name):
            if name not in sems:
                sems[name] = ctx.enter_context(nc.semaphore(name))
            return sems[name]

        ps = ctx.enter_context(nc.psum_tensor("ps", [P, 8, 512], F32))

        x = sb("x", [P, TILES, H])
        z = sb("z", [P, TILES, H])
        zh = sb("zh", [P, 2, TOK], F32R)
        zl = sb("zl", [P, 2, TOK], F32R)
        ident = sb("ident", [P, P])
        identb = sb("identb", [P, P], BF16)
        mask_q = sb("mask_q", [P, 512], BF16)
        mask_k = sb("mask_k", [P, 512], BF16)
        sel8 = sb("sel8", [P, 18])
        sel16 = sb("sel16", [P, 34])
        cosr = sb("cosr", [P, 2, 16])
        sinr = sb("sinr", [P, 2, 16])
        qw = sb("qw", [P, H])
        kw = sb("kw", [P, CTX])
        ctxt = sb("ctxt", [P, TILES, CTX])
        kr = sb("kr", [P, TILES, CTX])
        v8 = sb("v8", [P, TILES, 8, 32])
        v16 = sb("v16", [P, TILES, 4, 32])
        ctxT = sb("ctxT", [CTX, TOK])
        wqk = sb("wqk", [CTX, 2, CTX])
        bqk = sb("bqk", [CTX, 2])
        mask8 = sb("mask8", [P, TILES, S], U8)
        raw = sb("raw", [P, 2, 1024])
        wh = sb("wh", [P, 2, 1024], F32R)
        wl = sb("wl", [P, 2, 1024], F32R)
        router = sb("router", [P, 2, 60])
        router_h = sb("router_h", [P, 2, 60], F32R)
        router_l = sb("router_l", [P, 2, 60], F32R)
        dense = sb("dense", [P, 2, 2, H])
        dense_h = sb("dense_h", [P, 2, 2, H], F32R)
        dense_l = sb("dense_l", [P, 2, 2, H], F32R)
        gamma = sb("gamma", [P, H])
        beta = sb("beta", [P, H])
        bias0 = sb("bias0", [P, 12])
        bias3 = sb("bias3", [8, H])
        bias3h = sb("bias3h", [8, H], F32R)
        bias3l = sb("bias3l", [8, H], F32R)
        one = sb("one", [P, 1])
        ones2f = sb("ones2f", [2, P])
        ones2 = sb("ones2", [2, P], F32R)
        qs = sb("qs", [P, 3, 4096], F32R)
        ks8 = sb("ks8", [P, 3, 4 * S], F32R)
        ks16 = sb("ks16", [P, 6, 2 * S], F32R)
        zeros = sb("zeros", [2, 1, S])
        e = sb("e", [P, 2, 2, 1024])
        ot = sb("ot", [P, 2, 512])
        mx = sb("mx", [P, 2, 32])
        mT = sb("mT", [32, 2, 2, P], F32R)
        att = sb("att", [P, 2, 2, 16 * 9 + 8])
        attr = sb("attr", [P, 2, 16])
        attn = sb("attn", [P, 2, P])
        ef = e[:, :, :, :].rearrange("p a b c -> p (a b c)")
        qf = qs[:, :, :].rearrange("p a b -> p (a b)")

        def stacked(hd, n, r0=0, r1=P):
            at = hd.buf(n) * hd.HJ * S
            return qf[r0:r1, at:at + hd.HJ * S]

        def pair_of(flat, at, rows=P, n=512):
            return flat[0:rows, at:at + 2 * n].rearrange("p (a b) -> p a b", a=2)

        sg, t1, hm = (pair_of(ef, at) for at in (0, 1024, 2048))
        acc = pair_of(ef, 0, n=TOK)
        hh, hl = (pair_of(qf, at) for at in (0, 1024))
        wrow = pair_of(qf, 2048, 2, TOK)
        wT = pair_of(qf, 4096, 32, TOK)
        gs = sb("gs", [P, TILES, 40])
        gr = sb("gr", [P, TILES, 40])
        gp = sb("gp", [P, TILES, 32])
        gw = sb("gw", [P, TILES, 32])
        g8 = sb("g8", [P, TILES, 8])
        ga = sb("ga", [P, TILES])
        gb = sb("gb", [P, TILES])
        bst = sb("bst", [P, TILES, 6])
        mv = sb("mv", [P, TILES, 2])
        rstd = sb("rstd", [P, TILES])
        var = sb("var", [P, TILES])
        root = sb("root", [P, TILES])
        nmx = sb("nmx", [P, TILES])
        rsum = sb("rsum", [P, TILES])

        kst8 = nc.dram_tensor("kst8", [32, 8, TOK], F32).ap()
        kst16 = nc.dram_tensor("kst16", [64, 4, TOK], F32).ap()
        wsc = {L: nc.dram_tensor(f"wsc{L}", [ROUTED[L], 2, TOK], F32).ap() for L in (0, 2)}

        rh = [router_h[:, :, ROUTER_AT[L]:ROUTER_AT[L] + ROUTED[L]] for L in range(4)]
        rl = [router_l[:, :, ROUTER_AT[L]:ROUTER_AT[L] + ROUTED[L]] for L in range(4)]
        grouped = {1: Head(8, False, None)}
        grouped[2] = Head(16, True, grouped[1])
        grouped[3] = Head(8, False, grouped[2], grouped[1])
        NEXP = {0: 8, 1: 8, 2: 32}
        WCOLS = {0: 768, 1: 512, 2: 768}

        def units(hd):
            return range(hd.units + hd.KJ + 4)

        def stages(hd, s):
            return s, s - hd.KJ - 2, s - hd.KJ - 3, s - hd.KJ - 4

        hi8, lo8 = hh[0:CTX, :, :].rearrange("p a b -> p (a b)"), hl[0:CTX, :, :].rearrange("p a b -> p (a b)")
        hi16, lo16 = wh[0:CTX, 0, :], wl[0:CTX, 0, :]

        m1 = gw[:, 0:4, :].rearrange("p a b -> p (a b)").rearrange("p (t s) -> p t s", t=2).bitcast(U32)
        m2 = gp[:, :, :].rearrange("p a b -> p (a b)").rearrange("p (t s) -> p t s", t=B).bitcast(U32)
        hide = att[:, :, :, :].rearrange("p a b c -> p (a b c)")[:, 0:2 * P]
        a0q, a0k = ef[0:CTX, 2048:3072], ef[0:CTX, 3072:4096]
        a0s = ef[:, 0:2048].rearrange("p (t s) -> p t s", s=S)

        def b3(pair):
            return wrow[:, pair // 2, (pair % 2) * 512:(pair % 2 + 1) * 512]

        block = ctx.enter_context(nc.Block())

        @block.sync
        def _(sp):
            def load(dst, src, s):
                sp.dma_start(dst, src).then_inc(sem(s), 16)

            load(ctxT[:, :], a["ctxP"], "l_ctxT")
            load(ctxt[:, :, :], a["ctx"].rearrange("(t p) d -> p t d", p=P), "l_ctx")
            load(kw[:, :], a["kw"].partition_broadcast(P), "l_ctx")
            load(cosr[:, :, :], a["cos"], "l_ctx")
            load(sinr[:, :, :], a["sin"], "l_ctx")
            load(x[:, :, :], a["x"].rearrange("(t p) d -> p t d", p=P), "l_x")
            load(wqk[:, :, :], a["wqk"], "l_ctxT")
            load(bqk[:, :], a["bqk"], "l_ctxT")
            load(m1, a["m1"].rearrange("(t p) s -> p t s", p=P), "l_mask")
            load(m2, a["m2"].partition_broadcast(P), "l_mask")
            load(ident[:, :], a["ident"], "l_ident")
            load(router[:, :, :], a["router"], "l_dense")
            load(dense[:, :, :, :], a["dense"], "l_dense")
            load(bias3[:, :], a["bias3"], "l_dense")
            load(bias0[:, :], a["bias0"].partition_broadcast(P), "l_rows")
            load(gamma[:, :], a["gamma"].partition_broadcast(P), "l_rows")
            load(beta[:, :], a["beta"].partition_broadcast(P), "l_rows")
            load(qw[:, :], a["qw"].partition_broadcast(P), "l_rows")
            load(hide, a["hide"], "l_att")
            load(sel8[:, :], a["sel8"], "l_att")
            load(sel16[:, :], a["sel16"], "l_att")
            sp.wait_ge(sem("k8_split"), 2)
            for part, src in enumerate((0, 0, 1, 1)):
                load(kst8[part * 8:part * 8 + 8, :, :], (hi8, lo8)[src].bitcast(F32), "k8_stored")
            sp.wait_ge(sem("k16_split"), 2)
            for part, src in enumerate((0, 0, 1, 1)):
                load(kst16[part * 16:part * 16 + 16, :, :], (hi16, lo16)[src].bitcast(F32), "k16_stored")

            def experts(L):
                pk = a[f"experts{L}"]

                def raw_load(pair, eb):
                    sp.dma_start(raw[:, eb, 0:WCOLS[L]], pk[2 * pair + eb, :, :]).then_inc(sem(f"f{L}_raw{eb}"), 16)

                def row_load(pair, eb):
                    sp.dma_start(wrow[:, eb, :].bitcast(F32), wsc[L][2 * pair + eb, :, :]).then_inc(sem(f"f{L}_row{eb}"), 16)

                gated = L != 1
                if L == 0:
                    sp.wait_ge(sem("pads"), 1)
                if L > 0:
                    sp.wait_ge(sem(f"f{L-1}_split0"), NEXP[L - 1] // 2)
                    sp.wait_ge(sem(f"f{L-1}_split1"), NEXP[L - 1] // 2)
                raw_load(0, 0)
                raw_load(0, 1)
                if gated:
                    sp.wait_ge(sem(f"f{L}_wlo"), 1)
                    sp.dma_start(wsc[L][:, :, :], wT[0:ROUTED[L], :, :].bitcast(F32)).then_inc(sem(f"f{L}_wsc"), 16)
                    sp.wait_ge(sem(f"f{L}_wsc"), 16)
                    row_load(0, 0)
                    row_load(0, 1)
                with sp.Fori(1, NEXP[L] // 2) as pair:
                    for eb in (0, 1):
                        sp.wait_ge(sem(f"f{L}_split{eb}"), pair)
                        raw_load(pair, eb)
                        if gated:
                            sp.wait_ge(sem(f"f{L}_spread"), pair * 4 + (2 * eb - 2))
                            row_load(pair, eb)

            def attention(L):
                hd = grouped[L]
                sp.wait_ge(sem("lo_ready"), bank_at(f"a{L}", 4))
                def step_load(n):
                    b, j = divmod(n, 2)
                    if n >= hd.bufs:
                        sp.wait_ge(sem("a_st1"), hd.unit0 + (n - hd.bufs + 1) * hd.KJ)
                    cols = slice(b * S, b * S + S)
                    for part, src in enumerate((zh, zl, zh, zl)):
                        sp.dma_start(stacked(hd, n, part * hd.D, (part + 1) * hd.D).bitcast(F32),
                                     src[:, j, cols].bitcast(F32)).then_inc(sem(hd.q_sem(n)), 16)

                for n in range(3):
                    step_load(n)
                for n in range(hd.steps):
                    sp.wait_ge(sem("a_mlo"), hd.step0 + n + 1)
                    for part in (0, 1):
                        row = 4 * hd.D + part
                        sp.dma_start(stacked(hd, n, row, row + 1).bitcast(F32),
                                     mT[0:2 * hd.HJ, n % 2, part, :].bitcast(F32)).then_inc(sem(hd.m_sem(n)), 16)
                    if 1 <= n < hd.steps - 2:
                        step_load(n + 2)

            experts(0)
            attention(1)
            experts(1)
            attention(2)
            experts(2)
            attention(3)
            sp.wait_ge(sem("a_st1"), grouped[3].unit0 + grouped[3].units)
            sp.dma_start(wrow[0:1, :, :].bitcast(F32), bias3h[:, :].bitcast(F32)).then_inc(sem("bias3_ready"), 16)
            sp.dma_start(wrow[1:2, :, :].bitcast(F32), bias3l[:, :].bitcast(F32)).then_inc(sem("bias3_ready"), 16)
            sp.wait_ge(sem("f2_split0"), 16)
            sp.wait_ge(sem("f2_split1"), 16)
            for pair in range(4):
                if pair >= 2:
                    sp.wait_ge(sem(f"f3_split{pair % 2}"), pair // 2)
                sp.dma_start(raw[:, pair % 2, :], a["experts3"][pair]).then_inc(sem(f"f3_raw{pair % 2}"), 16)
            for t in range(TILES):
                sp.wait_ge(sem("f3_add"), 3 * TILES + t + 1)
                sp.dma_start(out[t * P:(t + 1) * P, :], x[:, t, :]).then_inc(sem("stored"), 16)
            sp.wait_ge(sem("stored"), 16 * TILES)

        @block.gpsimd
        def _(pool):
            c = Chain(pool, sem("pool_step"))
            c.mark(pool.memset(one[:, :], 1.0))
            c.mark(pool.memset(v8[:, :, :, :], 0.0))
            c.mark(pool.memset(v16[:, :, :, :], 0.0))
            c.mark(pool.memset(ks8[:, :, :].bitcast(F32), 0.0))
            c.mark(pool.memset(ks16[:, :, :].bitcast(F32), 0.0))
            c.mark(pool.memset(zeros[:, :, :], 0.0))
            c.join()
            c.mark(pool.memset(v8[:, :, :, 8:9], 1.0))
            c.mark(pool.memset(v16[:, :, :, 16:17], 1.0))
            c.join()
            c.step(pool.memset(ks8[32:34, :, :].bitcast(F32), -1.0))
            c.step(pool.memset(ks16[64:66, :, :].bitcast(F32), -1.0))
            pool.memset(qf[:, 2048:12288].bitcast(F32), 0.0).then_inc(sem("pads"), 1)
            pool.wait_ge(sem("l_ctx"), 64)
            pool.tensor_copy(v8[:, :, :, 0:8], ctxt[:, :, :].rearrange("p t (k d) -> p t k d", d=8)
                             ).then_inc(sem("v_ready"), 1)
            pool.tensor_copy(v16[:, :, :, 0:16], ctxt[:, :, :].rearrange("p t (k d) -> p t k d", d=16)
                             ).then_inc(sem("v_ready"), 1)
            pool.wait_ge(sem("l_dense"), 48)
            c.mark(pool.tensor_copy(router_h[:, :, :], router[:, :, :]))
            c.mark(pool.tensor_copy(dense_h[:, :, :, :], dense[:, :, :, :]))
            c.mark(pool.tensor_copy(bias3h[:, :], bias3[:, :]))
            c.join()
            pool.tensor_tensor(router_l[:, :, :], router[:, :, :], router_h[:, :, :].bitcast(F32),
                               ALU.subtract).then_inc(sem("dense_split"), 1)
            pool.tensor_tensor(dense_l[:, :, :, :], dense[:, :, :, :], dense_h[:, :, :, :].bitcast(F32),
                               ALU.subtract).then_inc(sem("dense_split"), 1)
            pool.tensor_tensor(bias3l[:, :], bias3[:, :], bias3h[:, :].bitcast(F32),
                               ALU.subtract).then_inc(sem("dense_split"), 1)

            def experts(L):
                cols = WCOLS[L]
                n_pair = NEXP[L] // 2
                if L == 0:
                    pool.wait_ge(sem("k16_stored"), 64)
                else:
                    pool.wait_ge(sem(f"f{L-1}_down"), 2 * NEXP[L - 1])

                def split(pair, eb, peeled):
                    pool.wait_ge(sem(f"f{L}_raw{eb}"), 16 * (pair + 1))
                    if not peeled:
                        pool.wait_ge(sem(f"f{L}_down"), pair * 4 + (2 * eb - 2))
                    pool.tensor_tensor(wh[:, eb, 0:cols], raw[:, eb, 0:cols], one[:, :].broadcast_to([P, cols]),
                                       ALU.mult).then_inc(sem(f"f{L}_hi{eb}"), 1)
                    pool.wait_ge(sem(f"f{L}_hi{eb}"), pair + 1)
                    pool.tensor_tensor(wl[:, eb, 0:cols], raw[:, eb, 0:cols], wh[:, eb, 0:cols].bitcast(F32),
                                       ALU.subtract).then_inc(sem(f"f{L}_split{eb}"), 1)

                split(0, 0, True)
                split(0, 1, True)
                with pool.Fori(1, n_pair) as pair:
                    split(pair, 0, False)
                    split(pair, 1, False)

            def attention(L):
                hd, ks = grouped[L], (ks16 if grouped[L].causal else ks8)
                kst = kst16 if hd.causal else kst8
                pool.wait_ge(sem("lo_ready"), bank_at(f"a{L}", 4))
                if L == 1:
                    pool.wait_ge(sem("k8_stored"), 64)
                if L == 2:
                    pool.wait_ge(sem("k16_stored"), 64)
                for n in range(hd.steps):
                    b, j = divmod(n, 2)
                    if n >= hd.bufs:
                        pool.wait_ge(sem("a_st1"), hd.unit0 + (n - hd.bufs + 1) * hd.KJ)
                    pool.dma_start(ks[0:4 * hd.D, hd.buf(n), :].rearrange("r (k t) -> r k t", t=S).bitcast(F32),
                                   kst[:, j * hd.KJ:(j + 1) * hd.KJ, b * S:b * S + S]).then_inc(sem(hd.k_sem(n)), 16)
                    pool.dma_start(stacked(hd, n, 4 * hd.D, 4 * hd.D + 2).rearrange("r (h s) -> r h s", s=S).bitcast(F32),
                                   zeros[:, :, :].broadcast_to([2, hd.HJ, S])).then_inc(sem(hd.k_sem(n)), 16)

            experts(0)
            attention(1)
            experts(1)
            attention(2)
            experts(2)
            attention(3)
            pool.wait_ge(sem("f2_down"), 2 * NEXP[2])
            for pair in range(4):
                eb = pair % 2
                pool.wait_ge(sem(f"f3_raw{eb}"), 16 * (pair // 2 + 1))
                if pair >= 2:
                    pool.wait_ge(sem("f3_y"), 8 * (pair - 1))
                pool.tensor_copy(wh[:, eb, :], raw[:, eb, :]).then_inc(sem(f"f3_hi{eb}"), 1)
                pool.wait_ge(sem(f"f3_hi{eb}"), pair // 2 + 1)
                pool.tensor_tensor(wl[:, eb, :], raw[:, eb, :], wh[:, eb, :].bitcast(F32),
                                   ALU.subtract).then_inc(sem(f"f3_split{eb}"), 1)

        @block.tensor
        def _(pe):
            def turn(tag, hf):
                pe.wait_ge(sem("z_ready"), z_at(tag, 4 * hf + 4))
                for j in (0, 1):
                    for q in range(4):
                        ins = pe.transpose(ps[:, TURN_BANKS[tag[0]][hf][j], q * P:(q + 1) * P],
                                           z[:, hf * 4 + q, j * P:(j + 1) * P], ident[:, :])
                    ins.then_inc(sem("turned"), 1)

            def attention0():
                pe.wait_ge(sem("l_ctxT"), 48)
                for m in (0, 1):
                    for hf in (0, 1):
                        pe.matmul(ps[0:CTX, 2 * m + hf, :], wqk[:, m, :], ctxT[:, hf * HALF:(hf + 1) * HALF],
                                  start=True, stop=True).then_inc(sem("a0_proj"), 1)
                pe.wait_ge(sem("l_ident"), 16)
                pe.wait_ge(sem("kr_ready"), 1)
                for t in range(TILES):
                    ins = pe.transpose(ps[0:CTX, 4 + t // 4, (t % 4) * P:(t % 4 + 1) * P],
                                       kr[:, t, :], ident[:, :])
                ins.then_inc(sem("kr_turned"), 1)
                pe.wait_ge(sem("a0_qk"), 4)
                pe.wait_ge(sem("k16_split"), 2)
                for t in range(TILES):
                    b = t // 2
                    ins = pe.matmul(ps[:, 4 + t // 2, (t % 2) * S:(t % 2 + 1) * S], a0q[:, t * P:(t + 1) * P],
                                    a0k[:, b * S:(b + 1) * S], start=True, stop=True)
                    if t % 2:
                        ins.then_inc(sem("a0_scores"), 1)

            def logits(L):
                pe.wait_ge(sem("lo_ready"), bank_at(f"f{L}", 4))
                if L == 0:
                    pe.wait_ge(sem("dense_split"), 3)
                for t in range(TILES):
                    tok = slice(t * P, (t + 1) * P)
                    parts = [(zh[:, j, tok], zl[:, j, tok], rh[L][:, j, :], rl[L][:, j, :]) for j in (0, 1)]
                    ins = product3(pe, ps[:, LOGIT_BANK, t * ROUTED[L]:(t + 1) * ROUTED[L]], parts, True, True)
                ins.then_inc(sem("logits"), 1)

            def experts(L):
                gated = L != 1
                n_pair = NEXP[L] // 2

                def up(eb, hf, bank, at, signal):
                    tok = slice(hf * HALF, (hf + 1) * HALF)
                    parts = [(wh[:, eb, at + k * P:at + (k + 1) * P], wl[:, eb, at + k * P:at + (k + 1) * P],
                              zh[:, k, tok], zl[:, k, tok]) for k in (0, 1)]
                    product3(pe, ps[:, bank, :], parts, True, True).then_inc(sem(signal), 1)

                def down(unit, eb, hf, first, last):
                    pe.wait_ge(sem(f"f{L}_hl"), unit + 1)
                    at = WCOLS[L] - H
                    for hb in (0, 1):
                        cols = slice(at + hb * P, at + (hb + 1) * P)
                        ins = product3(pe, ps[:, 2 * hb + hf, :],
                                       [(wh[:, eb, cols], wl[:, eb, cols], hh[:, hf, :], hl[:, hf, :])], first, last)
                    ins.then_inc(sem(f"f{L}_down"), 1)

                def pair_units(pair, first, last):
                    for eb in (0, 1):
                        pe.wait_ge(sem(f"f{L}_split{eb}"), pair + 1)
                        for hf in (0, 1):
                            k = 2 * eb + hf
                            unit = pair * 4 + k
                            start = first and k == 0
                            if gated:
                                if not start:
                                    pe.wait_ge(sem(f"f{L}_act"), unit)
                                up(eb, hf, G_BANK, 0, f"f{L}_g")
                                if not start:
                                    pe.wait_ge(sem(f"f{L}_gu"), unit)
                                up(eb, hf, U_BANK, H, f"f{L}_u")
                                if start:
                                    turn_weights(L)
                                else:
                                    pe.wait_ge(sem(f"f{L}_hm"), unit)
                                if hf == 0:
                                    pe.wait_ge(sem(f"f{L}_row{eb}"), 16 * (pair + 1))
                                pe.matmul(ps[:, W_BANK, :], ones2[:, :], wrow[:, eb, hf * HALF:(hf + 1) * HALF],
                                          start=True, stop=True).then_inc(sem(f"f{L}_spread"), 1)
                            else:
                                if not (first and k < 2):
                                    pe.wait_ge(sem(f"f{L}_hm"), unit - 1)
                                up(eb, hf, G_BANK + hf, 0, f"f{L}_u")
                            if not start:
                                before = (eb, 0) if hf else (1 - eb, 1)
                                down(unit - 1, *before, first and k in (1, 2), last and k == 3)
                    if last:
                        down(4 * n_pair - 1, 1, 1, False, True)

                def turn_weights(L):
                    E = ROUTED[L]
                    pe.wait_ge(sem(f"f{L}_w"), 1)
                    for t in range(TILES):
                        ins = pe.transpose(ps[0:E, W_BANK + t // 4, (t % 4) * P:(t % 4 + 1) * P],
                                           gw[:, t, 0:E], ident[:, :])
                    ins.then_inc(sem(f"f{L}_wturned"), 1)
                    pe.wait_ge(sem(f"f{L}_wlo"), 1)

                pair_units(0, True, False)
                with pe.Fori(1, n_pair - 1) as pair:
                    pair_units(pair, False, False)
                pair_units(n_pair - 1, False, True)
                if L == 1:
                    for i in range(4):
                        if i == 0:
                            pe.wait_ge(sem("f1_hm"), 2 * NEXP[1])
                        for t in (2 * i, 2 * i + 1):
                            tok = slice(t * P, (t + 1) * P)
                            parts = [(zh[:, j, tok], zl[:, j, tok], dense_h[:, 0, j, :], dense_l[:, 0, j, :])
                                     for j in (0, 1)]
                            ins = product3(pe, ps[:, 4 + i, (t % 2) * H:(t % 2 + 1) * H], parts, True, True)
                        ins.then_inc(sem("f1_moe"), 1)
                pe.wait_ge(sem(f"f{L}_acc"), 2)
                for i in range(4):
                    if L == 1:
                        pe.wait_ge(sem("f1_moe_read"), i + 1)
                    for t in (2 * i, 2 * i + 1):
                        for hb in (0, 1):
                            ins = pe.transpose(ps[:, 4 + i, (t % 2) * H + hb * P:(t % 2) * H + (hb + 1) * P],
                                               acc[:, hb, t * P:(t + 1) * P], ident[:, :])
                    ins.then_inc(sem(f"f{L}_back"), 1)

            def attention(L):
                hd, ks = grouped[L], (ks16 if grouped[L].causal else ks8)
                D, KJ = hd.D, hd.KJ
                v = v16 if hd.causal else v8
                sel = sel16 if hd.causal else sel8
                if L == 1:
                    pe.wait_ge(sem("l_att"), 48)
                    pe.wait_ge(sem("v_ready"), 2)

                def q_of(n, h0, h1, s0=0, s1=S):
                    return stacked(hd, n).rearrange("r (h s) -> r h s", s=S)[:, h0:h1, s0:s1]

                def k_of(n, k, t0, t1):
                    return ks[:, hd.buf(n), k * S + t0:k * S + t1]

                def max_chunk(U, c):
                    n, k = divmod(U, KJ)
                    C = U * hd.chunks + c
                    if C >= 2:
                        pe.wait_ge(sem("a_max"), hd.chunk0 + C - 1)
                    out = ps[:, MAX_BANK + C % 2, :]
                    if not hd.causal:
                        st, hp = divmod(c, 2)
                        for i in (0, 1):
                            h = 4 * k + 2 * hp + i
                            ins = pe.matmul(out[:, i * S:(i + 1) * S], q_of(n, h, h + 1, st * P, st * P + P),
                                            k_of(n, k, 0, S), start=i == 0, stop=i == 1, skip_group_check=True)
                    elif c == 0:
                        for i in range(4):
                            h = 4 * k + i
                            pe.matmul(out[:, i * P:(i + 1) * P], q_of(n, h, h + 1, 0, P),
                                      k_of(n, k, 0, P), start=i == 0, stop=False, skip_group_check=True)
                        ins = pe.matmul(out, identb[:, :], mask_q[:, :], start=False, stop=True, skip_group_check=True)
                    else:
                        for i in (0, 1):
                            h = 4 * k + 2 * (c - 1) + i
                            pe.matmul(out[:, i * S:(i + 1) * S], q_of(n, h, h + 1, P, S),
                                      k_of(n, k, 0, S), start=i == 0, stop=False, skip_group_check=True)
                        ins = pe.matmul(out.rearrange("p (h t) -> p h t", t=S)[:, :, P:S], identb[:, :],
                                        mask_q[:, 0:S], start=False, stop=True, skip_group_check=True)
                    ins.then_inc(sem("a_rows"), 1)

                def scores(U, tt):
                    n, k = divmod(U, KJ)
                    if U >= 1:
                        pe.wait_ge(sem(f"a_e{tt}"), hd.unit0 + U)
                    bank = ST_BANK + 2 * tt
                    kt = k_of(n, k, tt * P, (tt + 1) * P)
                    if hd.causal and tt == 1:
                        pe.matmul(ps[:, bank, :], kt, q_of(n, 4 * k, 4 * k + 4, P, S), start=True, stop=False,
                                  skip_group_check=True)
                        ins = pe.matmul(ps[:, bank, :], identb[:, :], mask_k[:, :], start=False, stop=True,
                                        skip_group_check=True)
                    else:
                        for i in (0, 1):
                            ins = pe.matmul(ps[:, bank + i, :], kt, q_of(n, 4 * k + 2 * i, 4 * k + 2 * i + 2),
                                            start=True, stop=not hd.causal, skip_group_check=True)
                            if hd.causal:
                                ins = pe.matmul(ps[:, bank + i, :].rearrange("p (h s) -> p h s", s=S)[:, :, 0:P],
                                                identb[:, :], mask_k[:, 0:S], start=False, stop=True,
                                                skip_group_check=True)
                    ins.then_inc(sem(f"a_st{tt}"), 1)

                def values(U):
                    n, k = divmod(U, KJ)
                    b, j = divmod(n, 2)
                    if U >= 1:
                        pe.wait_ge(sem("a_ot"), hd.unit0 + U)
                    pe.wait_ge(sem("a_e0"), hd.unit0 + U + 1)
                    pe.wait_ge(sem("a_e1"), hd.unit0 + U + 1)
                    for tt in (0, 1):
                        vt = v[:, 2 * b + tt, j * KJ + k, :]
                        for i in (0, 1):
                            cg = 2 * tt + i
                            o = ps[32 * cg:32 * cg + 32, OT_BANK, :]
                            if hd.causal and tt == 1:
                                o = o.rearrange("p (h s) -> p h s", s=S)[:, :, P:S]
                                r = e[:, U % 2, 1, i * S:(i + 1) * S]
                            else:
                                r = e[:, U % 2, tt, i * 512:(i + 1) * 512]
                            ins = pe.matmul(o, vt, r, start=True, stop=True)
                    ins.then_inc(sem("a_pv"), 1)

                def gather(U):
                    pe.wait_ge(sem("a_ot"), hd.unit0 + U + 1)
                    if U >= 1:
                        pe.wait_ge(sem("a_att"), hd.unit0 + U)
                    d1 = D + 1
                    for st in (0, 1):
                        o = ps[:, SUM_BANK, st * 4 * d1:(st + 1) * 4 * d1].rearrange("p (i g d) -> p i g d", i=2, g=2)
                        rows = 64 if hd.causal and st == 0 else P
                        for g in (0, 1):
                            ins = pe.matmul(o[:, :, g, :], ot[0:rows, U % 2, g * S + st * P:g * S + st * P + P],
                                            sel[0:rows, :], start=st == 0 and g == 0, stop=st == 1 and g == 1,
                                            skip_group_check=True)
                    ins.then_inc(sem("a_sum"), 1)

                def turn_max(n, gathered):
                    pe.wait_ge(sem("a_max"), hd.chunk0 + (n + 1) * KJ * hd.chunks)
                    if gathered:
                        pe.wait_ge(sem("a_att"), hd.unit0 + gathered)
                    pe.transpose(ps[0:2 * hd.HJ, SUM_BANK, 384:512],
                                 mx[:, n % 2, 0:2 * hd.HJ], ident[:, :]).then_inc(sem("a_mt"), 1)

                for s in units(hd):
                    mU, sU, vU, gU = stages(hd, s)
                    if mU < hd.units:
                        if mU % KJ == 0:
                            pe.wait_ge(sem(hd.q_sem(mU // KJ)), 64 * hd.uses(mU // KJ))
                            pe.wait_ge(sem(hd.k_sem(mU // KJ)), 32 * hd.uses(mU // KJ))
                        max_chunk(mU, 0)
                    if mU % KJ == 0 and 0 < mU <= hd.units:
                        turn_max(mU // KJ - 1, max(0, gU))
                    if 0 <= sU < hd.units:
                        if sU % KJ == 0:
                            pe.wait_ge(sem(hd.m_sem(sU // KJ)), 32 * hd.uses(sU // KJ))
                        scores(sU, 0)
                    if mU < hd.units:
                        max_chunk(mU, 1)
                    if 0 <= sU < hd.units:
                        scores(sU, 1)
                    if mU < hd.units:
                        max_chunk(mU, 2)
                    if 0 <= gU < hd.units:
                        pe.wait_ge(sem("a_mlo"), hd.step0 + min(mU // KJ, hd.steps))
                        gather(gU)
                    if mU < hd.units and hd.chunks == 4:
                        max_chunk(mU, 3)
                    if 0 <= vU < hd.units:
                        values(vU)

            def project():
                pe.wait_ge(sem("lo_ready"), bank_at("o2", 4))
                for i in range(4):
                    for t in (2 * i, 2 * i + 1):
                        tok = slice(t * P, (t + 1) * P)
                        parts = [(zh[:, j, tok], zl[:, j, tok], dense_h[:, 1, j, :], dense_l[:, 1, j, :])
                                 for j in (0, 1)]
                        ins = product3(pe, ps[:, (0, 1, 6, 7)[i], (t % 2) * H:(t % 2 + 1) * H], parts, True, True)
                    ins.then_inc(sem("o2_y"), 1)

            def experts3():
                for pair in range(4):
                    eb = pair % 2
                    pe.wait_ge(sem(f"f3_split{eb}"), pair // 2 + 1)
                    if pair == 0:
                        pe.wait_ge(sem("bias3_ready"), 32)
                    for t in range(TILES):
                        n = pair * TILES + t
                        if n >= 4:
                            pe.wait_ge(sem("f3_add"), n - 3)
                        tok = slice(t * P, (t + 1) * P)
                        o = ps[:, n % 4, :]
                        pe.matmul(o, ones2[:, :], b3(pair), start=True, stop=False, skip_group_check=True)
                        parts = [(zh[:, j, tok], zl[:, j, tok], wh[:, eb, j * 512:(j + 1) * 512],
                                  wl[:, eb, j * 512:(j + 1) * 512]) for j in (0, 1)]
                        product3(pe, o, parts, False, True).then_inc(sem("f3_y"), 1)

            attention0()
            turn("f0", 0)
            turn("f0", 1)
            logits(0)
            experts(0)
            turn("a1", 0)
            turn("a1", 1)
            attention(1)
            turn("f1", 0)
            turn("f1", 1)
            logits(1)
            experts(1)
            turn("a2", 0)
            turn("a2", 1)
            attention(2)
            turn("o2", 0)
            turn("o2", 1)
            project()
            turn("f2", 0)
            turn("f2", 1)
            logits(2)
            experts(2)
            turn("a3", 0)
            turn("a3", 1)
            attention(3)
            turn("f3", 0)
            turn("f3", 1)
            logits(3)
            experts3()


        @block.scalar
        def _(act):
            def split_hi(tag, hf):
                for j in (0, 1):
                    act.wait_ge(sem("turned"), bank_at(tag, 2 * hf + j + 1))
                    act.copy(zh[:, j, hf * HALF:(hf + 1) * HALF], ps[:, TURN_BANKS[tag[0]][hf][j], :]
                             ).then_inc(sem("hi_ready"), 1)

            def attention0():
                act.wait_ge(sem("l_ctxT"), 48)
                for m, dst in ((0, a0q), (1, a0k)):
                    for hf in (0, 1):
                        act.wait_ge(sem("a0_proj"), 2 * m + hf + 1)
                        act.activation(dst[:, hf * HALF:(hf + 1) * HALF], ps[0:CTX, 2 * m + hf, :], ACT.Identity,
                                       bias=bqk[:, m:m + 1]).then_inc(sem("a0_qk"), 1)
                act.wait_ge(sem("kr_turned"), 1)
                act.copy(hi16.rearrange("p (a b) -> p a b", a=2), ps[0:CTX, 4:6, :]).then_inc(sem("k16_split"), 1)
                act.wait_ge(sem("a0_nmx"), 1)
                for t in range(TILES):
                    act.activation(a0s[:, t, :], a0s[:, t, :], ACT.Exp, bias=nmx[:, t:t + 1],
                                   accum_out=rsum[:, t:t + 1]).then_inc(sem("a0_exp"), 1)

            def gate(L):
                if L != 1:
                    act.wait_ge(sem(f"f{L}_gd"), 1)
                    act.activation(gp[:, :, 0:ROUTED[L]], gp[:, :, 0:ROUTED[L]], ACT.Exp).then_inc(sem(f"f{L}_ge"), 1)

            def experts(L):
                gated = L != 1
                n_pair = NEXP[L] // 2

                def pair_units(pair, first):
                    for k in range(4):
                        hf = k % 2
                        unit = pair * 4 + k
                        early = first and k < 2
                        act.wait_ge(sem(f"f{L}_g" if gated else f"f{L}_u"), unit + 1)
                        if not early:
                            act.wait_ge(sem(f"f{L}_gu" if gated else f"f{L}_hm"), unit - 1)
                        act.activation(sg[:, hf, :], ps[:, G_BANK if gated else G_BANK + hf, :],
                                       ACT.Silu if gated else ACT.Relu).then_inc(sem(f"f{L}_act"), 1)
                        if gated and first and k == 0:
                            act.wait_ge(sem(f"f{L}_wturned"), 1)
                            if L == 0:
                                act.wait_ge(sem("pads"), 1)
                            act.copy(wT[0:ROUTED[L], 0, :].rearrange("e (a b) -> e a b", a=2),
                                     ps[0:ROUTED[L], W_BANK:W_BANK + 2, :]).then_inc(sem(f"f{L}_whi"), 1)
                        act.wait_ge(sem(f"f{L}_hm"), unit + 1)
                        if not early:
                            act.wait_ge(sem(f"f{L}_down"), unit - 1)
                        act.copy(hh[:, hf, :], hm[:, hf, :]).then_inc(sem(f"f{L}_hh"), 1)

                if L == 0:
                    act.wait_ge(sem("k8_stored"), 64)
                pair_units(0, True)
                with act.Fori(1, n_pair) as pair:
                    pair_units(pair, False)
                act.wait_ge(sem(f"f{L}_down"), 4 * n_pair)
                act.copy(acc[:, 0, :].rearrange("p (a b) -> p a b", a=2), ps[:, 0:2, :]).then_inc(sem(f"f{L}_acc"), 1)

            def attention(L):
                hd = grouped[L]
                for s in units(hd):
                    mU, sU, vU, _ = stages(hd, s)
                    if mU % hd.KJ == 0 and 0 < mU <= hd.units:
                        n = mU // hd.KJ - 1
                        act.wait_ge(sem("a_mt"), hd.step0 + n + 1)
                        if n >= 2:
                            act.wait_ge(sem(hd.m_sem(n - 2)), 32 * hd.uses(n - 2))
                        act.copy(mT[0:2 * hd.HJ, n % 2, 0, :], ps[0:2 * hd.HJ, SUM_BANK, 384:512]
                                 ).then_inc(sem("a_mhi"), 1)
                    for tt in (0, 1):
                        if 0 <= sU < hd.units:
                            act.wait_ge(sem(f"a_st{tt}"), hd.unit0 + sU + 1)
                            if sU >= 2:
                                act.wait_ge(sem("a_pv"), hd.unit0 + sU - 1)
                            if hd.causal and tt == 1:
                                dst, src = e[:, sU % 2, 1, 0:512], ps[:, ST_BANK + 2, :]
                            else:
                                dst = e[:, sU % 2, tt, :].rearrange("p (a b) -> p a b", a=2)
                                src = ps[:, ST_BANK + 2 * tt:ST_BANK + 2 * tt + 2, :]
                            act.activation(dst, src, ACT.Exp, scale=hd.scale).then_inc(sem(f"a_e{tt}"), 1)
                    if 0 <= vU < hd.units:
                        act.wait_ge(sem("a_pv"), hd.unit0 + vU + 1)
                        if vU >= 2:
                            act.wait_ge(sem("a_sum"), hd.unit0 + vU - 1)
                        if hd.causal:
                            act.copy(ot[0:64, vU % 2, :], ps[0:64, OT_BANK, :])
                            cut = "p (h s) -> p h s"
                            act.copy(ot[64:P, vU % 2, :].rearrange(cut, s=S)[:, :, P:S],
                                     ps[64:P, OT_BANK, :].rearrange(cut, s=S)[:, :, P:S]
                                     ).then_inc(sem("a_ot"), 1)
                        else:
                            act.copy(ot[:, vU % 2, :], ps[:, OT_BANK, :]).then_inc(sem("a_ot"), 1)

            def squares():
                act.wait_ge(sem("a2_q"), 8)
                for t in range(TILES):
                    act.activation(ef[:, 3072:3072 + H], z[:, t, :], ACT.Square,
                                   accum_out=rsum[:, t:t + 1]).then_inc(sem("a2_sq"), 1)
                    act.wait_ge(sem("a2_sq"), t + 1)

            attention0()
            split_hi("f0", 0)
            split_hi("f0", 1)
            gate(0)
            experts(0)
            split_hi("a1", 0)
            split_hi("a1", 1)
            attention(1)
            split_hi("f1", 0)
            split_hi("f1", 1)
            experts(1)
            squares()
            split_hi("a2", 0)
            split_hi("a2", 1)
            attention(2)
            split_hi("o2", 0)
            split_hi("o2", 1)
            split_hi("f2", 0)
            split_hi("f2", 1)
            gate(2)
            experts(2)
            split_hi("a3", 0)
            split_hi("a3", 1)
            attention(3)
            split_hi("f3", 0)
            split_hi("f3", 1)
            gate(3)

        @block.vector
        def _(dve):
            c = Chain(dve, sem("dve_step"))

            def inverse_root(v, scale, t0, t1):
                y, w, r = rstd[:, t0:t1], var[:, t0:t1], root[:, t0:t1]
                c.step(dve.tensor_scalar(w, v, scale, EPS, ALU.mult, ALU.add))
                c.step(dve.tensor_scalar(y.bitcast(I32), w.bitcast(I32), -0.5, ROOT_GUESS, ALU.mult, ALU.add))
                for _ in range(3):
                    c.step(dve.tensor_tensor(r, y, y, ALU.mult))
                    c.step(dve.scalar_tensor_tensor(r, r, -0.5, w, ALU.mult, ALU.mult))
                    c.step(dve.scalar_tensor_tensor(y, r, 1.5, y, ALU.add, ALU.mult))

            def normalise(src, dst, hf, signal=None, D=None):
                tiles = range(4 * hf, 4 * hf + 4)
                for t in tiles:
                    c.mark(dve.bn_stats(bst[:, t, :], src[:, t, :]))
                c.join()
                for t in tiles:
                    c.mark(dve.bn_aggr(mv[:, t, :], bst[:, t, :]))
                c.join()
                inverse_root(mv[:, 4 * hf:4 * hf + 4, 1], 1.0, 4 * hf, 4 * hf + 4)
                for t in tiles:
                    o, i = dst[:, t, :], src[:, t, :]
                    if D:
                        o = o.rearrange("p (j d h) -> p j d h", j=2, d=D)
                        i = i.rearrange("p (j h d) -> p j d h", j=2, d=D)
                    ins = dve.tensor_scalar(o, i, mv[:, t, 0:1], rstd[:, t:t + 1],
                                            ALU.subtract, ALU.mult)
                    if signal:
                        ins.then_inc(sem(signal), 1)
                    else:
                        c.mark(ins)

            def split_lo(tag, hf):
                for j in (0, 1):
                    tok = slice(hf * HALF, (hf + 1) * HALF)
                    dve.wait_ge(sem("hi_ready"), bank_at(tag, 2 * hf + j + 1))
                    dve.tensor_tensor(zl[:, j, tok], ps[:, TURN_BANKS[tag[0]][hf][j], :],
                                      zh[:, j, tok].bitcast(F32), ALU.subtract).then_inc(sem("lo_ready"), 1)

            def rotate(src, dst, tmp, J, heads):
                q = src.rearrange("p (b t) (j h d) -> p b t j h d", t=2, j=J, d=16)
                o = dst.rearrange("p (b t) (j d h) -> p b t j h d", t=2, j=J, d=16)
                w = tmp.rearrange("p (b h d) -> p b h d", b=B, d=16)
                for st in (0, 1):
                    cb = cosr[:, st:st + 1, :].rearrange("p (a b) d -> p a b d", a=1)
                    sb_ = sinr[:, st:st + 1, :].rearrange("p (a b) d -> p a b d", a=1)
                    for j in range(J):
                        c.mark(dve.tensor_tensor(o[:, :, st, j], q[:, :, st, j],
                                                 cb.broadcast_to([P, B, heads, 16]), ALU.mult))
                        for lo, hi in ((0, 8), (8, 0)):
                            c.mark(dve.tensor_tensor(w[:, :, :, lo:lo + 8], q[:, :, st, j, :, hi:hi + 8],
                                                     sb_[:, :, :, lo:lo + 8].broadcast_to([P, B, heads, 8]), ALU.mult))
                        c.join()
                        c.step(dve.tensor_tensor(o[:, :, st, j], o[:, :, st, j], w, ALU.add))

            def keys():
                dve.wait_ge(sem("l_ctxT"), 48)
                dve.tensor_copy(hi8, ctxT[:, :]).then_inc(sem("k8_split"), 1)
                dve.wait_ge(sem("k8_split"), 1)
                dve.tensor_tensor(lo8, ctxT[:, :], hi8.bitcast(F32), ALU.subtract).then_inc(sem("k8_split"), 1)
                dve.wait_ge(sem("l_ctx"), 64)
                sq = ef[:, 0:TILES * CTX].rearrange("p (t d) -> p t d", d=CTX)
                kn = ef[:, 1024:1024 + TILES * CTX].rearrange("p (t d) -> p t d", d=CTX)
                c.step(dve.tensor_tensor(sq, ctxt[:, :, :], ctxt[:, :, :], ALU.mult))
                c.step(dve.tensor_reduce(rsum[:, :], sq, AX_X, ALU.add))
                inverse_root(rsum[:, :], 1.0 / CTX, 0, TILES)
                c.step(dve.tensor_tensor(kn, ctxt[:, :, :],
                                         rstd[:, :].rearrange("p (t o) -> p t o", o=1).broadcast_to([P, TILES, CTX]),
                                         ALU.mult))
                c.step(dve.tensor_tensor(kn, kn, kw[:, :].rearrange("p (o d) -> p o d", o=1)
                                         .broadcast_to([P, TILES, CTX]), ALU.mult))
                rotate(kn, kr[:, :, :], ef[:, 512:768], 1, 4)
                dve.tensor_copy(kn[:, 0:1, 0:1], kr[:, 0:1, 0:1]).then_inc(sem("kr_ready"), 1)

            def attention0():
                dve.memset(ones2f[:, :], 1.0).then_inc(sem("ones_f"), 1)
                dve.wait_ge(sem("ones_f"), 1)
                dve.tensor_copy(ones2[:, :], ones2f[:, :]).then_inc(sem("ones_ready"), 1)
                keys()
                dve.wait_ge(sem("l_x"), 16)
                normalise(x, z, 0, "a0_z")
                normalise(x, z, 1, "a0_z")
                dve.wait_ge(sem("l_mask"), 32)
                for b in range(B):
                    ins = dve.tensor_tensor(mask8[:, 2 * b:2 * b + 2, :], m1.bitcast(U8),
                                            m2[:, b:b + 1, :].bitcast(U8).broadcast_to([P, 2, S]), ALU.max)
                    c.mark(ins)
                dve.wait_ge(sem("k16_split"), 1)
                dve.tensor_tensor(lo16.rearrange("p (a b) -> p a b", a=2), ps[0:CTX, 4:6, :],
                                  hi16.rearrange("p (a b) -> p a b", a=2).bitcast(F32), ALU.subtract
                                  ).then_inc(sem("k16_split"), 1)
                hidden = attn[:, :, :].rearrange("p a b -> p (a b)")
                c.mark(dve.memset(hidden, MASKED))
                dve.wait_ge(sem("a0_z"), TILES)
                for i in range(4):
                    dve.wait_ge(sem("a0_scores"), i + 1)
                    c.mark(dve.scalar_tensor_tensor(a0s[:, 2 * i:2 * i + 2, :],
                                                    ps[:, 4 + i, :].rearrange("p (t s) -> p t s", s=S), CTX ** -0.5,
                                                    z[:, 2 * i:2 * i + 2, :], ALU.mult, ALU.mult))
                c.join()
                for t in range(TILES):
                    c.mark(dve.copy_predicated(a0s[:, t, :], mask8[:, t, :], hidden))
                c.join()
                c.step(dve.tensor_reduce(ga[:, :], a0s, AX_X, ALU.max))
                dve.tensor_scalar(nmx[:, :], ga[:, :], -1.0, None, ALU.mult).then_inc(sem("a0_nmx"), 1)
                for t in range(TILES):
                    dve.wait_ge(sem("a0_exp"), t + 1)
                    c.step(dve.reciprocal(gb[:, t:t + 1], rsum[:, t:t + 1]))
                    c.mark(dve.scalar_tensor_tensor(x[:, t, :], a0s[:, t, :], gb[:, t:t + 1], x[:, t, :],
                                                    ALU.mult, ALU.add))
                c.join()

            def choose(L, k, width):
                W = width + 8 - k
                for t in range(TILES):
                    c.mark(dve.max(g8[:, t, :], gs[:, t, 0:W]))
                c.join()
                if L == 3:
                    c.mark(dve.tensor_copy(ga[:, :], g8[:, :, 0]))
                c.step(dve.memset(g8[:, :, k:8], SENTINEL))
                for t in range(TILES):
                    c.mark(dve.match_replace(gr[:, t, 0:W], g8[:, t, :], gs[:, t, 0:W], TAKEN))
                c.join()
                c.step(dve.tensor_scalar(gr[:, :, 0:width], gr[:, :, 0:width], TAKEN, None, ALU.is_equal))

            def per_tile(v, n):
                return v[:, :].rearrange("p (t o) -> p t o", o=1).broadcast_to([P, TILES, n])

            def gate(L):
                E = ROUTED[L]
                dve.wait_ge(sem("logits"), L + 1)
                lg = ps[:, LOGIT_BANK, 0:TILES * E].rearrange("p (t e) -> p t e", e=E)
                p_ = gp[:, :, 0:E]
                if L == 1:
                    for t in range(TILES):
                        c.mark(dve.max(g8[:, t, :], lg[:, t, :]))
                    c.join()
                    c.step(dve.tensor_tensor(ga[:, :], g8[:, :, 0], g8[:, :, 1], ALU.add))
                    return
                if L == 3:
                    c.mark(dve.memset(gs[:, :, E:E + 6], SENTINEL))
                    c.step(dve.tensor_copy(gs[:, :, 0:E], lg))
                    choose(3, 2, E)
                    dve.tensor_tensor(p_, gs[:, :, 0:E], per_tile(ga, E), ALU.subtract).then_inc(sem("f3_gd"), 1)
                    dve.wait_ge(sem("f3_ge"), 1)
                    c.step(dve.tensor_tensor(gw[:, :, 0:E], gr[:, :, 0:E], p_, ALU.mult))
                    c.step(dve.tensor_reduce(ga[:, :], gw[:, :, 0:E], AX_X, ALU.add))
                    c.step(dve.reciprocal(gb[:, :], ga[:, :]))
                    c.step(dve.tensor_tensor(gw[:, :, 0:E], gw[:, :, 0:E], per_tile(gb, E), ALU.mult))
                    return
                c.step(dve.tensor_reduce(ga[:, :], lg, AX_X, ALU.max))
                dve.tensor_tensor(p_, lg, per_tile(ga, E), ALU.subtract).then_inc(sem(f"f{L}_gd"), 1)
                k = 2 if L == 0 else 4
                c.mark(dve.memset(gs[:, :, E:E + 8 - k], SENTINEL))
                dve.wait_ge(sem(f"f{L}_ge"), 1)
                c.step(dve.tensor_reduce(ga[:, :], p_, AX_X, ALU.add))
                c.step(dve.reciprocal(gb[:, :], ga[:, :]))
                if L == 0:
                    c.step(dve.tensor_tensor(p_, p_, per_tile(gb, E), ALU.mult))
                    dve.wait_ge(sem("l_rows"), 64)
                    c.step(dve.tensor_tensor(gs[:, :, 0:E], p_, bias0[:, :].rearrange("p (o e) -> p o e", o=1)
                                             .broadcast_to([P, TILES, E]), ALU.add))
                    choose(0, 2, E)
                    dve.scalar_tensor_tensor(gw[:, :, 0:E], gr[:, :, 0:E], 1.5, p_, ALU.mult, ALU.mult
                                             ).then_inc(sem("f0_w"), 1)
                else:
                    c.step(dve.tensor_tensor(gs[:, :, 0:E], p_, per_tile(gb, E), ALU.mult))
                    choose(2, 4, E)
                    dve.tensor_tensor(gw[:, :, 0:E], gr[:, :, 0:E], gs[:, :, 0:E], ALU.mult).then_inc(sem("f2_w"), 1)

            def experts(L):
                gated = L != 1
                n_pair = NEXP[L] // 2

                def pair_units(pair, first):
                    for k in range(4):
                        hf = k % 2
                        unit = pair * 4 + k
                        early = first and k < 2
                        dve.wait_ge(sem(f"f{L}_act"), unit + 1)
                        dve.wait_ge(sem(f"f{L}_u"), unit + 1)
                        if gated:
                            dve.tensor_tensor(t1[:, hf, :], sg[:, hf, :], ps[:, U_BANK, :], ALU.mult
                                              ).then_inc(sem(f"f{L}_gu"), 1)
                            dve.wait_ge(sem(f"f{L}_gu"), unit + 1)
                            dve.wait_ge(sem(f"f{L}_spread"), unit + 1)
                        if not early:
                            dve.wait_ge(sem(f"f{L}_hh"), unit - 1)
                        if gated:
                            ins = dve.tensor_tensor(hm[:, hf, :], t1[:, hf, :], ps[:, W_BANK, :], ALU.mult)
                        else:
                            ins = dve.tensor_tensor(hm[:, hf, :], sg[:, hf, :], ps[:, G_BANK + hf, :], ALU.mult)
                        ins.then_inc(sem(f"f{L}_hm"), 1)
                        dve.wait_ge(sem(f"f{L}_hh"), unit + 1)
                        if not early:
                            dve.wait_ge(sem(f"f{L}_down"), unit - 1)
                        dve.tensor_tensor(hl[:, hf, :], hm[:, hf, :], hh[:, hf, :].bitcast(F32), ALU.subtract
                                          ).then_inc(sem(f"f{L}_hl"), 1)

                if gated:
                    E = ROUTED[L]
                    dve.wait_ge(sem(f"f{L}_whi"), 1)
                    cut = "e (a b) -> e a b"
                    dve.tensor_tensor(wT[0:E, 1, :].rearrange(cut, a=2), ps[0:E, W_BANK:W_BANK + 2, :],
                                      wT[0:E, 0, :].rearrange(cut, a=2).bitcast(F32), ALU.subtract
                                      ).then_inc(sem(f"f{L}_wlo"), 1)
                if L == 0:
                    dve.wait_ge(sem("f0_w"), 1)
                    c.step(dve.tensor_reduce(gb[:, :], gw[:, :, 8:12], AX_X, ALU.add))
                    for t in range(TILES):
                        c.mark(dve.scalar_tensor_tensor(x[:, t, :], z[:, t, :], gb[:, t:t + 1], x[:, t, :],
                                                        ALU.mult, ALU.add))
                    dve.wait_ge(sem("k8_stored"), 64)
                pair_units(0, True)
                with dve.Fori(1, n_pair) as pair:
                    pair_units(pair, False)
                dve.wait_ge(sem(f"f{L}_down"), 4 * n_pair)
                dve.tensor_copy(acc[:, 1, :].rearrange("p (a b) -> p a b", a=2), ps[:, 2:4, :]
                                ).then_inc(sem(f"f{L}_acc"), 1)
                c.join()
                if L == 1:
                    for i in range(4):
                        dve.wait_ge(sem("f1_moe"), i + 1)
                        c.mark(dve.tensor_scalar(z[:, 2 * i, :], ps[:, 4 + i, 0:H], ga[:, 2 * i:2 * i + 1], None,
                                                 ALU.mult))
                        c.join()
                        dve.tensor_scalar(z[:, 2 * i + 1, :], ps[:, 4 + i, H:2 * H], ga[:, 2 * i + 1:2 * i + 2], None,
                                          ALU.mult).then_inc(sem("f1_moe_read"), 1)
                    dve.wait_ge(sem("f1_moe_read"), 4)
                base = z if L == 1 else x
                for i in range(4):
                    dve.wait_ge(sem(f"f{L}_back"), i + 1)
                    o = base[:, 2 * i:2 * i + 2, :]
                    c.mark(dve.tensor_tensor(o, ps[:, 4 + i, :].rearrange("p (t d) -> p t d", d=H), o, ALU.add))
                c.join()
                if L == 1:
                    normalise(z, z, 0)
                    normalise(z, z, 1)
                    c.join()
                    for row, op in ((gamma, ALU.mult), (beta, ALU.add)):
                        c.step(dve.tensor_tensor(z[:, :, :], z[:, :, :], row[:, :].rearrange("p (o d) -> p o d", o=1)
                                                 .broadcast_to([P, TILES, H]), op))
                    c.step(dve.tensor_tensor(x[:, :, :], x[:, :, :], z[:, :, :], ALU.add))

            def attention(L):
                hd = grouped[L]
                D, KJ, HJ, d1 = hd.D, hd.KJ, hd.HJ, hd.D + 1

                def maxima(U, ch):
                    n, k = divmod(U, KJ)
                    C = U * hd.chunks + ch
                    dve.wait_ge(sem("a_rows"), hd.chunk0 + C + 1)
                    if n >= 2 and U % KJ == 0 and ch == 0:
                        dve.wait_ge(sem("a_mt"), hd.step0 + n - 1)
                    bank = ps[:, MAX_BANK + C % 2, :]
                    if hd.causal:
                        w, st = (P, 0) if ch == 0 else (S, 1)
                        h0 = 4 * k + (0 if ch == 0 else 2 * (ch - 1))
                    else:
                        w, st, h0 = S, ch // 2, 4 * k + 2 * (ch % 2)
                    columns = mx[:, n % 2, 0:2 * HJ].rearrange("p (h st) -> p h st", st=2)
                    dve.tensor_reduce(columns[:, h0:h0 + 512 // w, st], bank.rearrange("p (h t) -> p h t", t=w),
                                      AX_X, ALU.max).then_inc(sem("a_max"), 1)

                def collect(U):
                    n, k = divmod(U, KJ)
                    dve.wait_ge(sem("a_sum"), hd.unit0 + U + 1)
                    dve.tensor_copy(att[:, n % 2, :, k * 4 * d1:(k + 1) * 4 * d1],
                                    ps[:, SUM_BANK, 0:8 * d1].rearrange("p (t q) -> p t q", t=2)
                                    ).then_inc(sem("a_att"), 1)

                def finish(n):
                    b, j = divmod(n, 2)
                    dve.wait_ge(sem("a_att"), hd.unit0 + (n + 1) * KJ)
                    v = att[:, n % 2, :, 0:HJ * d1].rearrange("p t (h d) -> p t h d", d=d1)
                    c.step(dve.reciprocal(attr[:, :, 0:HJ], v[:, :, :, D]))
                    r = attr[:, :, 0:HJ].rearrange("p t (h o) -> p t h o", o=1).broadcast_to([P, 2, HJ, D])
                    c.step(dve.tensor_tensor(attn[:, :, :].rearrange("p t (h d) -> p t h d", d=D),
                                             v[:, :, :, 0:D], r, ALU.mult))
                    cols = slice(j * P, (j + 1) * P)
                    if hd.causal:
                        dve.tensor_copy(z[:, 2 * b:2 * b + 2, cols], attn[:, :, :]).then_inc(sem("z_ready"), 1)
                    else:
                        c.step(dve.tensor_tensor(x[:, 2 * b:2 * b + 2, cols], x[:, 2 * b:2 * b + 2, cols],
                                                 attn[:, :, :], ALU.add))

                for s in units(hd):
                    mU, _, _, gU = stages(hd, s)
                    if mU < hd.units:
                        maxima(mU, 0)
                    if mU % KJ == 0 and 0 < mU <= hd.units:
                        n = mU // KJ - 1
                        dve.wait_ge(sem("a_mhi"), hd.step0 + n + 1)
                        dve.tensor_tensor(mT[0:2 * HJ, n % 2, 1, :], ps[0:2 * HJ, SUM_BANK, 384:512],
                                          mT[0:2 * HJ, n % 2, 0, :].bitcast(F32), ALU.subtract
                                          ).then_inc(sem("a_mlo"), 1)
                    if mU < hd.units:
                        maxima(mU, 1)
                        maxima(mU, 2)
                    if 0 <= gU < hd.units:
                        collect(gU)
                    if mU < hd.units and hd.chunks == 4:
                        maxima(mU, 3)
                    if 0 <= gU < hd.units and gU % KJ == KJ - 1:
                        finish(gU // KJ)

            def queries():
                normalise(x, z, 0, "a2_q")
                normalise(x, z, 1, "a2_q")
                dve.wait_ge(sem("a2_sq"), TILES)
                inverse_root(rsum[:, :], 1.0 / H, 0, TILES)
                qn = ef[:, 0:2048].rearrange("p (t d) -> p t d", d=H)
                for t in range(TILES):
                    c.mark(dve.scalar_tensor_tensor(qn[:, t, :], z[:, t, :], rstd[:, t:t + 1], qw[:, :],
                                                    ALU.mult, ALU.mult))
                c.join()
                rotate(qn, z[:, :, :], ef[:, 2048:2560], 2, 8)
                for t in range(TILES):
                    dve.sem_inc(sem("z_ready"), 1)

            def project():
                for i in range(4):
                    dve.wait_ge(sem("o2_y"), i + 1)
                    o = x[:, 2 * i:2 * i + 2, :]
                    c.mark(dve.tensor_tensor(o, ps[:, (0, 1, 6, 7)[i], :].rearrange("p (t d) -> p t d", d=H), o,
                                             ALU.add))
                c.join()

            def experts3():
                for pair in range(4):
                    for t in range(TILES):
                        n = pair * TILES + t
                        dve.wait_ge(sem("f3_y"), n + 1)
                        for i in (0, 1):
                            ins = dve.scalar_tensor_tensor(x[:, t, :], ps[:, n % 4, i * H:(i + 1) * H],
                                                           gw[:, t, 2 * pair + i:2 * pair + i + 1], x[:, t, :],
                                                           ALU.mult, ALU.add)
                            if i == 0:
                                c.step(ins)
                            else:
                                ins.then_inc(sem("f3_add"), 1)

            attention0()
            dve.wait_ge(sem("l_ident"), 16)
            dve.wait_ge(sem("l_att"), 48)
            c.mark(dve.tensor_copy(identb[:, :], ident[:, :]))
            for m, mask in enumerate((mask_q, mask_k)):
                c.mark(dve.tensor_copy(mask[:, :].rearrange("p (g s) -> p g s", g=4),
                                       hide[:, m * P:(m + 1) * P].rearrange("p (o s) -> p o s", o=1)
                                       .broadcast_to([P, 4, P])))
            c.join()
            normalise(x, z, 0, "z_ready")
            normalise(x, z, 1, "z_ready")
            split_lo("f0", 0)
            split_lo("f0", 1)
            gate(0)
            experts(0)
            normalise(x, z, 0, "z_ready", 8)
            normalise(x, z, 1, "z_ready", 8)
            split_lo("a1", 0)
            split_lo("a1", 1)
            attention(1)
            normalise(x, z, 0, "z_ready")
            normalise(x, z, 1, "z_ready")
            split_lo("f1", 0)
            split_lo("f1", 1)
            gate(1)
            experts(1)
            queries()
            split_lo("a2", 0)
            split_lo("a2", 1)
            attention(2)
            split_lo("o2", 0)
            split_lo("o2", 1)
            project()
            normalise(x, z, 0, "z_ready")
            normalise(x, z, 1, "z_ready")
            split_lo("f2", 0)
            split_lo("f2", 1)
            gate(2)
            experts(2)
            normalise(x, z, 0, "z_ready", 8)
            normalise(x, z, 1, "z_ready", 8)
            split_lo("a3", 0)
            split_lo("a3", 1)
            attention(3)
            normalise(x, z, 0, "z_ready")
            normalise(x, z, 1, "z_ready")
            split_lo("f3", 0)
            split_lo("f3", 1)
            gate(3)
            experts3()


def constants():
    i = np.arange(P)
    hide = np.where(i[None, :] > i[:, None], -1e30, 0.0).astype(np.float32)
    inv = 1.0 / 10000.0 ** (np.arange(0, 16, 2, dtype=np.float32) / 16)
    angle = np.outer(np.arange(S, dtype=np.float32), inv.astype(np.float32)).astype(np.float32)
    angle = np.concatenate([angle, angle], -1)
    cos, sin = np.cos(angle), np.sin(angle)
    sin[:, :8] *= -1.0
    turn = lambda v: np.ascontiguousarray(v.reshape(2, P, 16).transpose(1, 0, 2)).astype(np.float32)
    sel = {}
    for d in (8, 16):
        s = np.zeros((P, 2, d + 1), np.float32)
        for cg in range(4):
            for r in range(d + 1):
                s[32 * cg + r, cg % 2, r] = 1.0
        sel[d] = s.reshape(P, 2 * (d + 1))
    return {
        "ident": np.eye(P, dtype=np.float32), "hide": np.concatenate([hide, hide.T], axis=1),
        "cos": turn(cos), "sin": turn(sin), "sel8": sel[8], "sel16": sel[16],
    }


def kernel(**inp):
    import concourse.bacc as _bacc
    from concourse.bass_utils import run_bass_kernel_spmd as _run

    g = {k: np.asarray(v) for k, v in inp.items()}

    def rows(w):
        return w.reshape(2, P, -1).transpose(1, 0, 2)

    def packed(gate, up, down):
        flat = [w.reshape(-1, 2, P, P).transpose(0, 2, 1, 3).reshape(-1, P, 2 * P) for w in (gate, up) if w is not None]
        return np.concatenate(flat + [down], axis=2)

    by_kd = np.arange(CTX).reshape(8, 8).T.reshape(-1)
    arrays = dict(constants())
    arrays.update({
        "x": g["x"].reshape(TOK, H),
        "ctx": g["ctx_512"].reshape(TOK, CTX),
        "ctxP": g["ctx_512"].reshape(TOK, CTX).T[by_kd],
        "wqk": np.stack([g["L0_xattn_Wq"].T[by_kd], g["L0_xattn_Wk"].T[by_kd]], axis=1),
        "bqk": np.stack([g["L0_xattn_bq"], g["L0_xattn_bk"]], axis=1),
        "m1": np.ascontiguousarray(g["mask_SxS2_bk1"]).view(np.uint32),
        "m2": np.ascontiguousarray(g["mask_BxS2_bf0"]).view(np.uint32),
        "router": rows(np.concatenate([g["L0_ffn_classifier_w"].T, g["L1_ffn_gate_w"], g["L2_ffn_Wgate"].T,
                                       g["L3_ffn_gate_w"].T], axis=1)),
        "dense": np.stack([rows(g["L1_ffn_expert_weight"]), rows(g["L2_xattn_w_out"].T)], axis=1),
        "bias0": g["L0_ffn_e_score_correction_bias"],
        "bias3": g["L3_ffn_expert_b"],
        "gamma": g["L1_ffn_ln_gamma"], "beta": g["L1_ffn_ln_beta"],
        "qw": g["L2_xattn_q_norm_w"], "kw": g["L2_xattn_k_norm_w"],
        "experts0": packed(g["L0_ffn_gate_w"].transpose(0, 2, 1), g["L0_ffn_up_w"].transpose(0, 2, 1),
                           g["L0_ffn_down_w"].transpose(0, 2, 1)),
        "experts1": packed(None, g["L1_ffn_up_w"].reshape(H, 8, P).transpose(1, 0, 2),
                           g["L1_ffn_down_w"].reshape(8, P, H)),
        "experts2": packed(g["L2_ffn_Wg"], g["L2_ffn_Wu"], g["L2_ffn_Wd"]),
        "experts3": g["L3_ffn_expert_w"].transpose(0, 2, 1).reshape(4, 2, 2, P, H).transpose(0, 3, 2, 1, 4)
                     .reshape(4, P, 1024),
    })
    arrays = {f"in_{k}": np.ascontiguousarray(v) for k, v in arrays.items()}
    nc = _bacc.Bacc("TRN2", target_bir_lowering=False, num_devices=1)
    aps = {k[3:]: nc.dram_tensor(k, v.shape, mybir.dt.from_np(v.dtype), kind="ExternalInput").ap()
           for k, v in arrays.items()}
    out = nc.dram_tensor("out_x", (TOK, H), F32, kind="ExternalOutput").ap()
    build(nc, aps, out)
    r = _run(nc, [arrays], core_ids=[0])
    return r.results[0]["out_x"].reshape(B, S, H)
```

```python
from contextlib import ExitStack

import numpy as np

import concourse.bass as bass
from concourse import mybir

F32 = mybir.dt.float32
F32R = mybir.dt.float32r
BF16 = mybir.dt.bfloat16
I32 = mybir.dt.int32
U8 = mybir.dt.uint8
U32 = mybir.dt.uint32
ALU = mybir.AluOpType
ACT = mybir.ActivationFunctionType
AX_X = mybir.AxisListType.X

P = 128
B, S, H = 4, 256, 256
TOK = B * S
TILES = TOK // P
HALF = TOK // 2
CTX = 64
EPS = 1e-5
ROOT_GUESS = float(0x5F3759DF)
MASKED = -3.0e38
TURN_BANKS = {"a": ((0, 2), (6, 7)), "f": ((0, 1), (2, 3)), "o": ((0, 1), (2, 3))}
SPREAD_BANK = 2
PROJECT_BANKS = (0, 1, 6, 4)
MAX_BANK = 0
ST_BANK = 2
OT_BANK, SUM_BANK = 6, 7
G_BANK, U_BANK, LOGIT_BANK = 4, 5, 7
ROUTED = (12, 8, 32, 8)
ROUTER_AT = (0, 12, 20, 52)
SENTINEL = -3.0e38
TAKEN = 3.0e38


class Chain:

    def __init__(self, eng, sem):
        self.eng, self.sem, self.n = eng, sem, 0

    def mark(self, ins):
        ins.then_inc(self.sem, 1)
        self.n += 1

    def join(self):
        self.eng.wait_ge(self.sem, self.n)

    def step(self, ins):
        self.mark(ins)
        self.join()


def product3(pe, out, parts, start, stop):
    ins = None
    for n, (Lh, Ll, Rh, Rl) in enumerate(parts):
        first, last = n == 0, n == len(parts) - 1
        pe.matmul(out, Lh, Rh, start=start and first, stop=False, skip_group_check=True)
        pe.matmul(out, Lh, Rl, start=False, stop=False, skip_group_check=True)
        ins = pe.matmul(out, Ll, Rh, start=False, stop=stop and last, skip_group_check=True)
    return ins


TURNS = ("f0", "a1", "f1", "a2", "o2", "f2", "a3", "f3")


def z_at(tag, n):
    return TILES * TURNS.index(tag) + n


def bank_at(tag, n):
    return 4 * TURNS.index(tag) + n


class Head:

    def __init__(self, D, causal, before, peer=None):
        self.D, self.causal = D, causal
        self.HJ = P // D
        self.KJ = self.HJ // 4
        self.R = 4 * D + 2
        self.scale = D ** -0.5
        self.steps = 2 * B
        self.units = self.steps * self.KJ
        self.chunks = 3 if causal else 4
        self.bufs = 4 if causal else 3
        self.tile = "c" if causal else "g"
        self.first = peer.first + peer.steps if peer else 0
        self.step0 = before.step0 + before.steps if before else 0
        self.unit0 = before.unit0 + before.units if before else 0
        self.chunk0 = before.chunk0 + before.units * before.chunks if before else 0

    def buf(self, n):
        return (self.first + n) % self.bufs

    def uses(self, n):
        return (self.first + n) // self.bufs + 1

    def q_sem(self, n):
        return f"a_{self.tile}q{self.buf(n)}"

    def k_sem(self, n):
        return f"a_{self.tile}k{self.buf(n)}"

    def m_sem(self, n):
        return f"a_{self.tile}m{self.buf(n)}"


def build(nc, a, out):
    ctx = ExitStack()
    with ctx:
        def sb(name, shape, dt=F32):
            return ctx.enter_context(nc.sbuf_tensor(name, list(shape), dt))

        sems = {}

        def sem(name):
            if name not in sems:
                sems[name] = ctx.enter_context(nc.semaphore(name))
            return sems[name]

        ps = ctx.enter_context(nc.psum_tensor("ps", [P, 8, 512], F32))

        x = sb("x", [P, TILES, H])
        z = sb("z", [P, TILES, H])
        zh = sb("zh", [P, 2, TOK], F32R)
        zl = sb("zl", [P, 2, TOK], F32R)
        ident = sb("ident", [P, P])
        identb = sb("identb", [P, P], BF16)
        mask_q = sb("mask_q", [P, 512], BF16)
        mask_k = sb("mask_k", [P, 512], BF16)
        sel8 = sb("sel8", [P, 36])
        sel16 = sb("sel16", [P, 68])
        cosr = sb("cosr", [P, 2, 16])
        sinr = sb("sinr", [P, 2, 16])
        qw = sb("qw", [P, H])
        kw = sb("kw", [P, CTX])
        ctxt = sb("ctxt", [P, TILES, CTX])
        kr = sb("kr", [P, TILES, CTX])
        v8 = sb("v8", [P, TILES, 8, 32])
        v16 = sb("v16", [P, TILES, 4, 32])
        ctxT = sb("ctxT", [CTX, TOK])
        wqk = sb("wqk", [CTX, 2, CTX])
        bqk = sb("bqk", [CTX, 2])
        mask8 = sb("mask8", [P, TILES, S], U8)
        raw = sb("raw", [P, 2, 1024])
        wh = sb("wh", [P, 2, 1024], F32R)
        wl = sb("wl", [P, 2, 1024], F32R)
        router = sb("router", [P, 2, 60])
        router_s = sb("router_s", [P, 2, 2, 60], F32R)
        dense = sb("dense", [P, 2, 2, H])
        dense_h = sb("dense_h", [P, 2, 2, H], F32R)
        dense_l = sb("dense_l", [P, 2, 2, H], F32R)
        gamma = sb("gamma", [P, H])
        beta = sb("beta", [P, H])
        bias0 = sb("bias0", [P, 12])
        bias3 = sb("bias3", [8, H])
        bias3h = sb("bias3h", [8, H], F32R)
        bias3l = sb("bias3l", [8, H], F32R)
        one = sb("one", [P, 1])
        ones2f = sb("ones2f", [2, P])
        ones2 = sb("ones2", [2, P], F32R)
        qs = sb("qs", [P, 3, 4096], F32R)
        ks8 = sb("ks8", [P, 3, 4 * S], F32R)
        ks16 = sb("ks16", [P, 4, 2 * S], F32R)
        zeros = sb("zeros", [2, 1, S])
        e = sb("e", [P, 2, 2, 1024])
        ot = sb("ot", [P, 2, 512])
        mx = sb("mx", [P, 2, 32])
        mT = sb("mT", [32, 2, 2, P], F32R)
        att = sb("att", [P, 2, 2, 16 * 9 + 8])
        attr = sb("attr", [P, 2, 2, 16])
        attn = sb("attn", [P, 2, P])
        ef = e[:, :, :, :].rearrange("p a b c -> p (a b c)")
        qf = qs[:, :, :].rearrange("p a b -> p (a b)")

        def stacked(hd, n, r0=0, r1=P):
            at = hd.buf(n) * hd.HJ * S
            return qf[r0:r1, at:at + hd.HJ * S]

        def pair_of(flat, at, rows=P, n=512):
            return flat[0:rows, at:at + 2 * n].rearrange("p (a b) -> p a b", a=2)

        sg, t1, hm = (pair_of(ef, at) for at in (0, 1024, 2048))
        acc = pair_of(ef, 0, n=TOK)
        hh, hl = (pair_of(qf, at) for at in (0, 1024))
        brow = pair_of(qf, 2048, 2, TOK)
        wT = ef[0:32, 3072:4096]
        spread = pair_of(qf, 8192, n=TOK)
        gs = sb("gs", [P, TILES, 40])
        gr = sb("gr", [P, TILES, 40])
        gp = sb("gp", [P, TILES, 32])
        gw = sb("gw", [P, TILES, 32])
        g8 = sb("g8", [P, TILES, 8])
        ga = sb("ga", [P, TILES])
        gb = sb("gb", [P, TILES])
        bst = sb("bst", [P, TILES, 6])
        mv = sb("mv", [P, TILES, 2])
        rstd = sb("rstd", [P, TILES])
        shift = sb("shift", [P, 4])
        var = sb("var", [P, TILES])
        root = sb("root", [P, TILES])
        nmx = sb("nmx", [P, TILES])
        rsum = sb("rsum", [P, TILES])

        kst8 = nc.dram_tensor("kst8", [32, 8, TOK], F32).ap()
        kst16 = nc.dram_tensor("kst16", [64, 4, TOK], F32).ap()
        wsc = {L: nc.dram_tensor(f"wsc{L}", [ROUTED[L], TOK], F32).ap() for L in (0, 2)}

        def routers(L, j, parts=2):
            return router_s[:, j, 0:parts, ROUTER_AT[L]:ROUTER_AT[L] + ROUTED[L]]

        grouped = {1: Head(8, False, None)}
        grouped[2] = Head(16, True, grouped[1])
        grouped[3] = Head(8, False, grouped[2], grouped[1])
        NEXP = {0: 8, 1: 8, 2: 32}
        WCOLS = {0: 768, 1: 512, 2: 768}

        def units(hd):
            return range(hd.units + hd.KJ + 4)

        def max_banks(hd, C):
            return 4 if C < (hd.KJ + 1) * hd.chunks else 2

        def stages(hd, s):
            return s, s - hd.KJ - 2, s - hd.KJ - 3, s - hd.KJ - 4

        hi8, lo8 = hh[0:CTX, :, :].rearrange("p a b -> p (a b)"), hl[0:CTX, :, :].rearrange("p a b -> p (a b)")
        hi16, lo16 = wh[0:CTX, 0, :], wl[0:CTX, 0, :]

        m1 = gw[:, 0:4, :].rearrange("p a b -> p (a b)").rearrange("p (t s) -> p t s", t=2).bitcast(U32)
        m2 = gp[:, :, :].rearrange("p a b -> p (a b)").rearrange("p (t s) -> p t s", t=B).bitcast(U32)
        hide = att[:, :, :, :].rearrange("p a b c -> p (a b c)")[:, 0:2 * P]
        a0q, a0k = ef[0:CTX, 2048:3072], ef[0:CTX, 3072:4096]
        a0s = ef[:, 0:2048].rearrange("p (t s) -> p t s", s=S)
        qn, qsin = (ef[:, at:at + 2048].rearrange("p (t d) -> p t d", d=H) for at in (0, 2048))
        qc = raw[:, :, :].rearrange("p a (t d) -> p (a t) d", d=H)
        rotation = ot[:, :, :].rearrange("p m (t d) -> p m t d", t=2)

        def b3(pair):
            return brow[:, pair // 2, (pair % 2) * 512:(pair % 2 + 1) * 512]

        block = ctx.enter_context(nc.Block())

        @block.sync
        def _(sp):
            def load(dst, src, s):
                sp.dma_start(dst, src).then_inc(sem(s), 16)

            load(ctxT[:, :], a["ctxP"], "l_ctxT")
            load(wqk[:, :, :], a["wqk"], "l_ctxT")
            load(bqk[:, :], a["bqk"], "l_ctxT")
            for hf in (0, 1):
                load(x[:, 4 * hf:4 * hf + 4, :],
                     a["x"][hf * HALF:(hf + 1) * HALF, :].rearrange("(t p) d -> p t d", p=P), f"l_x{hf}")
            load(m1, a["m1"].rearrange("(t p) s -> p t s", p=P), "l_mask")
            load(m2, a["m2"].partition_broadcast(P), "l_mask")
            load(ident[:, :], a["ident"], "l_ident")
            load(router[:, :, :], a["router"], "l_router")
            load(bias0[:, :], a["bias0"].partition_broadcast(P), "l_router")
            load(hide, a["hide"], "l_ident")
            load(ctxt[:, :, :], a["ctx"].rearrange("(t p) d -> p t d", p=P), "l_ctx")
            load(dense[:, :, :, :], a["dense"], "l_dense")
            load(bias3[:, :], a["bias3"], "l_dense")
            load(kw[:, :], a["kw"].partition_broadcast(P), "l_keys")
            load(cosr[:, :, :], a["cos"], "l_keys")
            load(sinr[:, :, :], a["sin"], "l_keys")
            load(sel8[:, :], a["sel8"], "l_keys")
            load(sel16[:, :], a["sel16"], "l_keys")
            load(gamma[:, :], a["gamma"].partition_broadcast(P), "l_keys")
            load(beta[:, :], a["beta"].partition_broadcast(P), "l_keys")
            load(qw[:, :], a["qw"].partition_broadcast(P), "l_keys")
            sp.wait_ge(sem("k8_split"), 2)
            for part, src in enumerate((0, 0, 1, 1)):
                load(kst8[part * 8:part * 8 + 8, :, :], (hi8, lo8)[src].bitcast(F32), "k8_stored")

            def store_keys16():
                sp.wait_ge(sem("k16_split"), 2)
                for part, src in enumerate((0, 0, 1, 1)):
                    load(kst16[part * 16:part * 16 + 16, :, :], (hi16, lo16)[src].bitcast(F32), "k16_stored")

            def experts(L):
                pk = a[f"experts{L}"]

                def raw_load(pair, eb):
                    sp.dma_start(raw[:, eb, 0:WCOLS[L]], pk[2 * pair + eb, :, :]).then_inc(sem(f"f{L}_raw{eb}"), 16)

                def row_load(pair, eb):
                    sp.dma_start(spread[:, eb, :].bitcast(F32), wsc[L][2 * pair + eb, :].partition_broadcast(P)
                                 ).then_inc(sem(f"f{L}_row{eb}"), 16)

                gated = L != 1
                if L == 0:
                    sp.wait_ge(sem("pads"), 1)
                if L > 0:
                    sp.wait_ge(sem(f"f{L-1}_split0"), NEXP[L - 1] // 2)
                    sp.wait_ge(sem(f"f{L-1}_split1"), NEXP[L - 1] // 2)
                raw_load(0, 0)
                raw_load(0, 1)
                if gated:
                    sp.wait_ge(sem(f"f{L}_wT"), 1)
                    sp.dma_start(wsc[L][:, :], wT[0:ROUTED[L], :]).then_inc(sem(f"f{L}_wsc"), 16)
                    sp.wait_ge(sem(f"f{L}_wsc"), 16)
                    row_load(0, 1)
                with sp.Fori(1, NEXP[L] // 2) as pair:
                    for eb in (0, 1):
                        sp.wait_ge(sem(f"f{L}_split{eb}"), pair)
                        raw_load(pair, eb)
                        if gated:
                            sp.wait_ge(sem(f"f{L}_hm"), pair * 4 + (2 * eb - 2))
                            row_load(pair, eb)

            def attention(L):
                hd = grouped[L]
                sp.wait_ge(sem("lo_ready"), bank_at(f"a{L}", 2))
                def step_load(n):
                    b, j = divmod(n, 2)
                    if n == 4:
                        sp.wait_ge(sem("lo_ready"), bank_at(f"a{L}", 4))
                    if n >= hd.bufs:
                        sp.wait_ge(sem("a_st1"), hd.unit0 + (n - hd.bufs + 1) * hd.KJ)
                    cols = slice(b * S, b * S + S)
                    for part, src in enumerate((zh, zl, zh, zl)):
                        sp.dma_start(stacked(hd, n, part * hd.D, (part + 1) * hd.D).bitcast(F32),
                                     src[:, j, cols].bitcast(F32)).then_inc(sem(hd.q_sem(n)), 16)

                for n in range(3):
                    step_load(n)
                for n in range(hd.steps):
                    sp.wait_ge(sem("a_mlo"), hd.step0 + n + 1)
                    for part in (0, 1):
                        row = 4 * hd.D + part
                        sp.dma_start(stacked(hd, n, row, row + 1).bitcast(F32),
                                     mT[0:2 * hd.HJ, n % 2, part, :].bitcast(F32)).then_inc(sem(hd.m_sem(n)), 16)
                    if 1 <= n < hd.steps - 2:
                        step_load(n + 2)

            experts(0)
            attention(1)
            store_keys16()
            experts(1)
            attention(2)
            experts(2)
            attention(3)
            sp.wait_ge(sem("a_st1"), grouped[3].unit0 + grouped[3].units)
            sp.dma_start(brow[0:1, :, :].bitcast(F32), bias3h[:, :].bitcast(F32)).then_inc(sem("bias3_ready"), 16)
            sp.dma_start(brow[1:2, :, :].bitcast(F32), bias3l[:, :].bitcast(F32)).then_inc(sem("bias3_ready"), 16)
            sp.wait_ge(sem("f2_split0"), 16)
            sp.wait_ge(sem("f2_split1"), 16)
            for pair in range(4):
                if pair >= 2:
                    sp.wait_ge(sem(f"f3_split{pair % 2}"), pair // 2)
                sp.dma_start(raw[:, pair % 2, :], a["experts3"][pair]).then_inc(sem(f"f3_raw{pair % 2}"), 16)
            for t in range(TILES):
                sp.wait_ge(sem("f3_add"), 3 * TILES + t + 1)
                sp.dma_start(out[t * P:(t + 1) * P, :], x[:, t, :]).then_inc(sem("stored"), 16)
            sp.wait_ge(sem("stored"), 16 * TILES)

        @block.gpsimd
        def _(pool):
            c = Chain(pool, sem("pool_step"))
            c.mark(pool.memset(one[:, :], 1.0))
            c.mark(pool.memset(zeros[:, :, :], 0.0))
            pool.wait_ge(sem("l_ctxT"), 48)
            pool.tensor_copy(hi8, ctxT[:, :]).then_inc(sem("k8_split"), 1)
            pool.wait_ge(sem("k8_split"), 1)
            pool.tensor_tensor(lo8, ctxT[:, :], hi8.bitcast(F32), ALU.subtract).then_inc(sem("k8_split"), 1)
            pool.memset(qf[:, 2048:12288].bitcast(F32), 0.0).then_inc(sem("pads"), 1)
            pool.wait_ge(sem("l_router"), 32)
            c.step(pool.tensor_copy(router_s[:, :, 0, :], router[:, :, :]))
            pool.tensor_tensor(router_s[:, :, 1, :], router[:, :, :], router_s[:, :, 0, :].bitcast(F32),
                               ALU.subtract).then_inc(sem("router_split"), 1)

            def tables():
                c.mark(pool.memset(v8[:, :, :, :], 0.0))
                c.mark(pool.memset(v16[:, :, :, :], 0.0))
                c.mark(pool.memset(ks8[:, :, :].bitcast(F32), 0.0))
                c.mark(pool.memset(ks16[:, :, :].bitcast(F32), 0.0))
                c.join()
                c.mark(pool.memset(v8[:, :, :, 8:9], 1.0))
                c.mark(pool.memset(v16[:, :, :, 16:17], 1.0))
                c.join()
                c.step(pool.memset(ks8[32:34, :, :].bitcast(F32), -1.0))
                c.step(pool.memset(ks16[64:66, :, :].bitcast(F32), -1.0))
                pool.wait_ge(sem("l_ctx"), 16)
                pool.tensor_copy(v8[:, :, :, 0:8], ctxt[:, :, :].rearrange("p t (k d) -> p t k d", d=8)
                                 ).then_inc(sem("tables_ready"), 1)
                pool.tensor_copy(v16[:, :, :, 0:16], ctxt[:, :, :].rearrange("p t (k d) -> p t k d", d=16)
                                 ).then_inc(sem("tables_ready"), 1)
                pool.wait_ge(sem("l_ident"), 32)
                pool.tensor_copy(identb[:, :], ident[:, :]).then_inc(sem("tables_ready"), 1)
                for m, mask in enumerate((mask_q, mask_k)):
                    pool.tensor_copy(mask[:, :].rearrange("p (g s) -> p g s", g=4),
                                     hide[:, m * P:(m + 1) * P].rearrange("p (o s) -> p o s", o=1)
                                     .broadcast_to([P, 4, P])).then_inc(sem("tables_ready"), 1)
                pool.wait_ge(sem("l_dense"), 32)
                c.mark(pool.tensor_copy(dense_h[:, :, :, :], dense[:, :, :, :]))
                c.mark(pool.tensor_copy(bias3h[:, :], bias3[:, :]))
                c.join()
                pool.tensor_tensor(dense_l[:, :, :, :], dense[:, :, :, :], dense_h[:, :, :, :].bitcast(F32),
                                   ALU.subtract).then_inc(sem("dense_split"), 1)
                pool.tensor_tensor(bias3l[:, :], bias3[:, :], bias3h[:, :].bitcast(F32),
                                   ALU.subtract).then_inc(sem("dense_split"), 1)

            def keys():
                pool.wait_ge(sem("l_keys"), 128)
                flat = raw[:, 1, :]
                sq = flat[:, 0:TILES * CTX].rearrange("p (t d) -> p t d", d=CTX)
                kn = flat[:, 512:512 + TILES * CTX].rearrange("p (t d) -> p t d", d=CTX)
                w_ = raw[:, 0, 0:256].rearrange("p (b h d) -> p b h d", b=B, d=16)
                total, v, y, h = (raw[:, 0, 256 + 8 * i:264 + 8 * i] for i in range(4))
                c.step(pool.tensor_tensor(sq, ctxt[:, :, :], ctxt[:, :, :], ALU.mult))
                n = CTX
                while n > 1:
                    n //= 2
                    o = total.rearrange("p (t o) -> p t o", o=1) if n == 1 else sq[:, :, 0:n]
                    c.step(pool.tensor_tensor(o, sq[:, :, 0:n], sq[:, :, n:2 * n], ALU.add))
                c.step(pool.tensor_scalar(v, total, 1.0 / CTX, EPS, ALU.mult, ALU.add))
                c.step(pool.tensor_scalar(y.bitcast(I32), v.bitcast(I32), -0.5, ROOT_GUESS, ALU.mult, ALU.add))
                for _ in range(3):
                    c.step(pool.tensor_tensor(h, y, y, ALU.mult))
                    c.step(pool.tensor_tensor(h, h, v, ALU.mult))
                    c.step(pool.tensor_scalar(h, h, -0.5, 1.5, ALU.mult, ALU.add))
                    c.step(pool.tensor_tensor(y, y, h, ALU.mult))
                c.step(pool.tensor_tensor(kn, ctxt[:, :, :], y.rearrange("p (t o) -> p t o", o=1)
                                          .broadcast_to([P, TILES, CTX]), ALU.mult))
                c.step(pool.tensor_tensor(kn, kn, kw[:, :].rearrange("p (o d) -> p o d", o=1)
                                          .broadcast_to([P, TILES, CTX]), ALU.mult))
                q = kn.rearrange("p (b t) (h d) -> p b t h d", t=2, d=16)
                o = kr[:, :, :].rearrange("p (b t) (d h) -> p b t h d", t=2, d=16)
                for st in (0, 1):
                    cb = cosr[:, st:st + 1, :].rearrange("p (a b) d -> p a b d", a=1)
                    sb_ = sinr[:, st:st + 1, :].rearrange("p (a b) d -> p a b d", a=1)
                    c.mark(pool.tensor_tensor(o[:, :, st], q[:, :, st], cb.broadcast_to([P, B, 4, 16]), ALU.mult))
                    for lo, hi in ((0, 8), (8, 0)):
                        c.mark(pool.tensor_tensor(w_[:, :, :, lo:lo + 8], q[:, :, st, :, hi:hi + 8],
                                                  sb_[:, :, :, lo:lo + 8].broadcast_to([P, B, 4, 8]), ALU.mult))
                    c.join()
                    pool.tensor_tensor(o[:, :, st], o[:, :, st], w_, ALU.add).then_inc(sem("kr_ready"), 1)
                    pool.wait_ge(sem("kr_ready"), st + 1)

            def rotation_tables():
                pool.wait_ge(sem("l_keys"), 128)
                pool.wait_ge(sem("a_sum"), grouped[1].unit0 + grouped[1].units)
                w = qw[:, :].rearrange("p (h d) -> p h d", d=16)
                for st in (0, 1):
                    co, si = (rotation[:, m, st, :].rearrange("p (h d) -> p h d", d=16) for m in (0, 1))
                    pool.tensor_tensor(co, w, cosr[:, st:st + 1, :].broadcast_to([P, 16, 16]), ALU.mult
                                       ).then_inc(sem("rotation_ready"), 1)
                    for lo, hi in ((0, 8), (8, 0)):
                        pool.tensor_tensor(si[:, :, lo:lo + 8], w[:, :, hi:hi + 8],
                                           sinr[:, st:st + 1, lo:lo + 8].broadcast_to([P, 16, 8]), ALU.mult
                                           ).then_inc(sem("rotation_ready"), 1)
                pool.wait_ge(sem("z_ready"), z_at("f1", TILES))
                pool.tensor_tensor(x[:, :, :], x[:, :, :], beta[:, :].rearrange("p (o d) -> p o d", o=1)
                                   .broadcast_to([P, TILES, H]), ALU.add).then_inc(sem("beta_added"), 1)
                pool.wait_ge(sem("rotation_ready"), 6)

            def experts(L):
                cols = WCOLS[L]
                n_pair = NEXP[L] // 2
                if L == 1:
                    pool.wait_ge(sem("k16_stored"), 64)
                if L > 0:
                    pool.wait_ge(sem(f"f{L-1}_down"), 2 * NEXP[L - 1])

                def split(pair, eb, peeled):
                    pool.wait_ge(sem(f"f{L}_raw{eb}"), 16 * (pair + 1))
                    if not peeled:
                        pool.wait_ge(sem(f"f{L}_down"), pair * 4 + (2 * eb - 2))
                    pool.tensor_tensor(wh[:, eb, 0:cols], raw[:, eb, 0:cols], one[:, :].broadcast_to([P, cols]),
                                       ALU.mult).then_inc(sem(f"f{L}_hi{eb}"), 1)
                    pool.wait_ge(sem(f"f{L}_hi{eb}"), pair + 1)
                    pool.tensor_tensor(wl[:, eb, 0:cols], raw[:, eb, 0:cols], wh[:, eb, 0:cols].bitcast(F32),
                                       ALU.subtract).then_inc(sem(f"f{L}_split{eb}"), 1)

                split(0, 0, True)
                split(0, 1, True)
                if L == 0:
                    tables()
                if L == 1:
                    rotation_tables()
                with pool.Fori(1, n_pair) as pair:
                    split(pair, 0, False)
                    split(pair, 1, False)

            def attention(L):
                hd, ks = grouped[L], (ks16 if grouped[L].causal else ks8)
                kst = kst16 if hd.causal else kst8
                pool.wait_ge(sem("lo_ready"), bank_at(f"a{L}", 2))
                if L == 1:
                    pool.wait_ge(sem("k8_stored"), 64)
                if L == 2:
                    pool.wait_ge(sem("k16_stored"), 64)

                def load(n):
                    b, j = divmod(n, 2)
                    if n >= hd.bufs:
                        pool.wait_ge(sem("a_st1"), hd.unit0 + (n - hd.bufs + 1) * hd.KJ)
                    pool.dma_start(ks[0:4 * hd.D, hd.buf(n), :].rearrange("r (k t) -> r k t", t=S).bitcast(F32),
                                   kst[:, j * hd.KJ:(j + 1) * hd.KJ, b * S:b * S + S]).then_inc(sem(hd.k_sem(n)), 16)
                    pool.dma_start(stacked(hd, n, 4 * hd.D, 4 * hd.D + 2).rearrange("r (h s) -> r h s", s=S).bitcast(F32),
                                   zeros[:, :, :].broadcast_to([2, hd.HJ, S])).then_inc(sem(hd.k_sem(n)), 16)

                def finish(n):
                    b, j = divmod(n, 2)
                    pool.wait_ge(sem("a_recip"), hd.step0 + n + 1)
                    v = att[:, n % 2, :, 0:hd.HJ * (hd.D + 1)].rearrange("p t (h d) -> p t h d", d=hd.D + 1)
                    r = attr[:, n % 2, :, 0:hd.HJ].rearrange("p t (h o) -> p t h o", o=1
                                                             ).broadcast_to([P, 2, hd.HJ, hd.D])
                    at = (slice(None), slice(2 * b, 2 * b + 2), slice(j * P, (j + 1) * P))
                    o = z[at] if hd.causal else attn[:, :, :]
                    pool.tensor_tensor(o.rearrange("p t (h d) -> p t h d", d=hd.D), v[:, :, :, 0:hd.D], r, ALU.mult
                                       ).then_inc(sem("z_ready" if hd.causal else "a_divided"), 1)
                    if not hd.causal:
                        done = n + 1 + (hd.steps if L == 3 else 0)
                        pool.wait_ge(sem("a_divided"), done)
                        pool.tensor_tensor(x[at], x[at], attn[:, :, :], ALU.add).then_inc(sem("a_done"), 1)
                        pool.wait_ge(sem("a_done"), done)

                for n in range(hd.bufs):
                    load(n)
                if L == 1:
                    keys()
                for n in range(hd.bufs, hd.steps):
                    load(n)
                    finish(n - hd.bufs)
                for n in range(hd.steps - hd.bufs, hd.steps):
                    finish(n)

            def queries():
                pool.wait_ge(sem("f1_y"), 4)
                pool.tensor_tensor(z[:, 4:8, :], z[:, 4:8, :], gamma[:, :].rearrange("p (o d) -> p o d", o=1)
                                   .broadcast_to([P, 4, H]), ALU.mult).then_inc(sem("f1_y"), 1)
                cut = "p (h d) -> p h d"
                for t in range(TILES):
                    pool.wait_ge(sem("a2_qn"), t + 1)
                    c.mark(pool.tensor_tensor(qsin[:, t, :].rearrange(cut, d=16)[:, :, 0:8],
                                       qn[:, t, :].rearrange(cut, d=16)[:, :, 8:16],
                                       rotation[:, 1, t % 2, :].rearrange(cut, d=16)[:, :, 0:8], ALU.mult))
                    pool.tensor_tensor(qsin[:, t, :].rearrange(cut, d=16)[:, :, 8:16],
                                       qn[:, t, :].rearrange(cut, d=16)[:, :, 0:8],
                                       rotation[:, 1, t % 2, :].rearrange(cut, d=16)[:, :, 8:16], ALU.mult
                                       ).then_inc(sem("a2_qs"), 1)

            experts(0)
            attention(1)
            experts(1)
            queries()
            attention(2)
            experts(2)
            attention(3)
            pool.wait_ge(sem("f2_down"), 2 * NEXP[2])
            for pair in range(4):
                eb = pair % 2
                pool.wait_ge(sem(f"f3_raw{eb}"), 16 * (pair // 2 + 1))
                if pair >= 2:
                    pool.wait_ge(sem("f3_y"), 8 * (pair - 1))
                pool.tensor_copy(wh[:, eb, :], raw[:, eb, :]).then_inc(sem(f"f3_hi{eb}"), 1)
                pool.wait_ge(sem(f"f3_hi{eb}"), pair // 2 + 1)
                pool.tensor_tensor(wl[:, eb, :], raw[:, eb, :], wh[:, eb, :].bitcast(F32),
                                   ALU.subtract).then_inc(sem(f"f3_split{eb}"), 1)

        @block.tensor
        def _(pe):
            def turn(tag, hf, tiles=(0, 1)):
                pe.wait_ge(sem("z_ready"), z_at(tag, 4 * hf + 4))
                for j in tiles:
                    for q in range(4):
                        ins = pe.transpose(ps[:, TURN_BANKS[tag[0]][hf][j], q * P:(q + 1) * P],
                                           z[:, hf * 4 + q, j * P:(j + 1) * P], ident[:, :])
                    ins.then_inc(sem("turned"), 1)

            def attention0():
                pe.wait_ge(sem("l_ctxT"), 48)
                for m in (0, 1):
                    for hf in (0, 1):
                        pe.matmul(ps[0:CTX, 2 * m + hf, :], wqk[:, m, :], ctxT[:, hf * HALF:(hf + 1) * HALF],
                                  start=True, stop=True).then_inc(sem("a0_proj"), 1)
                pe.wait_ge(sem("a0_qk"), 4)
                for t in range(TILES):
                    b = t // 2
                    ins = pe.matmul(ps[:, 4 + t // 2, (t % 2) * S:(t % 2 + 1) * S], a0q[:, t * P:(t + 1) * P],
                                    a0k[:, b * S:(b + 1) * S], start=True, stop=True)
                    if t % 2:
                        ins.then_inc(sem("a0_scores"), 1)

            def logits(L, hf):
                pe.wait_ge(sem("lo_ready"), bank_at(f"f{L}", 2 * hf + 2))
                if L == 0:
                    pe.wait_ge(sem("router_split"), 1)
                E = ROUTED[L]
                for t in range(4 * hf, 4 * hf + 4):
                    tok = slice(t * P, (t + 1) * P)
                    o = ps[:, LOGIT_BANK, t * 2 * E:(t + 1) * 2 * E]
                    for j in (0, 1):
                        pe.matmul(o, zh[:, j, tok], routers(L, j), start=j == 0, stop=False, skip_group_check=True)
                        ins = pe.matmul(o[:, 0:E], zl[:, j, tok], routers(L, j, 1), start=False, stop=j == 1,
                                        skip_group_check=True)
                ins.then_inc(sem("logits"), 1)

            def experts(L):
                gated = L != 1
                n_pair = NEXP[L] // 2

                def up(eb, hf, bank, at, signal):
                    tok = slice(hf * HALF, (hf + 1) * HALF)
                    parts = [(wh[:, eb, at + k * P:at + (k + 1) * P], wl[:, eb, at + k * P:at + (k + 1) * P],
                              zh[:, k, tok], zl[:, k, tok]) for k in (0, 1)]
                    product3(pe, ps[:, bank, :], parts, True, True).then_inc(sem(signal), 1)

                def down(unit, eb, hf, first, last):
                    if L == 1 and first and hf == 0:
                        pe.wait_ge(sem("f1_moe_read"), 4)
                    pe.wait_ge(sem(f"f{L}_hl"), unit + 1)
                    at = WCOLS[L] - H
                    for hb in (0, 1):
                        cols = slice(at + hb * P, at + (hb + 1) * P)
                        ins = product3(pe, ps[:, 2 * hb + hf, :],
                                       [(wh[:, eb, cols], wl[:, eb, cols], hh[:, hf, :], hl[:, hf, :])], first, last)
                    ins.then_inc(sem(f"f{L}_down"), 1)

                def pair_units(pair, first, last):
                    for eb in (0, 1):
                        pe.wait_ge(sem(f"f{L}_split{eb}"), pair + 1)
                        for hf in (0, 1):
                            k = 2 * eb + hf
                            unit = pair * 4 + k
                            start = first and k == 0
                            if gated:
                                early = first and k < 2
                                if not early:
                                    pe.wait_ge(sem(f"f{L}_act"), unit - 1)
                                up(eb, hf, G_BANK + 2 * hf, 0, f"f{L}_g")
                                if first and k == 1:
                                    turn_weights(L)
                                    pe.wait_ge(sem(f"f{L}_gd"), 1)
                                if not early:
                                    pe.wait_ge(sem(f"f{L}_gu"), unit - 1)
                                up(eb, hf, U_BANK + 2 * hf, H, f"f{L}_u")
                                if first and k == 1:
                                    spread_first(L)
                            else:
                                if not (first and k < 2):
                                    pe.wait_ge(sem(f"f{L}_hm"), unit - 1)
                                up(eb, hf, G_BANK + hf, 0, f"f{L}_u")
                            if not start:
                                before = (eb, 0) if hf else (1 - eb, 1)
                                down(unit - 1, *before, first and k in (1, 2), last and k == 3)
                    if last:
                        if gated:
                            pe.wait_ge(sem(f"f{L}_gu"), 4 * n_pair)
                            pe.wait_ge(sem(f"f{L}_act"), 4 * n_pair)
                        else:
                            pe.wait_ge(sem(f"f{L}_hm"), 4 * n_pair)
                        turn_back(0)
                        down(4 * n_pair - 1, 1, 1, False, True)
                        turn_back(1)

                def turn_back(hf):
                    pe.wait_ge(sem(f"f{L}_acc"), 2 * hf + 2)
                    for i in (2 * hf, 2 * hf + 1):
                        for t in (2 * i, 2 * i + 1):
                            for hb in (0, 1):
                                ins = pe.transpose(ps[:, 4 + i, (t % 2) * H + hb * P:(t % 2) * H + (hb + 1) * P],
                                                   acc[:, hb, t * P:(t + 1) * P], ident[:, :])
                        ins.then_inc(sem(f"f{L}_back"), 1)

                def turn_weights(L):
                    E = ROUTED[L]
                    pe.wait_ge(sem(f"f{L}_w"), 1)
                    for t in range(TILES):
                        ins = pe.transpose(ps[0:E, t // 4, (t % 4) * P:(t % 4 + 1) * P],
                                           gw[:, t, 0:E], ident[:, :])
                    ins.then_inc(sem(f"f{L}_wturned"), 1)

                def spread_first(L):
                    pe.wait_ge(sem(f"f{L}_wT"), 1)
                    for hf in (0, 1):
                        pe.matmul(ps[:, SPREAD_BANK + hf, :], ones2f[0:1, :], wT[0:1, hf * HALF:(hf + 1) * HALF],
                                  start=True, stop=True).then_inc(sem(f"f{L}_spread"), 1)

                if L == 1:
                    pe.wait_ge(sem("dense_split"), 2)
                    for i in range(4):
                        for t in (2 * i, 2 * i + 1):
                            tok = slice(t * P, (t + 1) * P)
                            parts = [(zh[:, j, tok], zl[:, j, tok], dense_h[:, 0, j, :], dense_l[:, 0, j, :])
                                     for j in (0, 1)]
                            ins = product3(pe, ps[:, i, (t % 2) * H:(t % 2 + 1) * H], parts, True, True)
                        ins.then_inc(sem("f1_moe"), 1)
                pair_units(0, True, False)
                with pe.Fori(1, n_pair - 1) as pair:
                    pair_units(pair, False, False)
                pair_units(n_pair - 1, False, True)

            def attention(L):
                hd, ks = grouped[L], (ks16 if grouped[L].causal else ks8)
                D, KJ = hd.D, hd.KJ
                v = v16 if hd.causal else v8
                sel = sel16 if hd.causal else sel8
                if L == 1:
                    pe.wait_ge(sem("tables_ready"), 5)
                    pe.wait_ge(sem("l_keys"), 128)

                def q_of(n, h0, h1, s0=0, s1=S):
                    return stacked(hd, n).rearrange("r (h s) -> r h s", s=S)[:, h0:h1, s0:s1]

                def k_of(n, k, t0, t1):
                    return ks[:, hd.buf(n), k * S + t0:k * S + t1]

                def max_chunk(U, c):
                    n, k = divmod(U, KJ)
                    C = U * hd.chunks + c
                    m = max_banks(hd, C)
                    if C >= m:
                        pe.wait_ge(sem("a_max"), hd.chunk0 + C - m + 1)
                    out = ps[:, MAX_BANK + C % m, :]
                    if not hd.causal:
                        st, hp = divmod(c, 2)
                        for i in (0, 1):
                            h = 4 * k + 2 * hp + i
                            ins = pe.matmul(out[:, i * S:(i + 1) * S], q_of(n, h, h + 1, st * P, st * P + P),
                                            k_of(n, k, 0, S), start=i == 0, stop=i == 1, skip_group_check=True)
                    elif c == 0:
                        for i in range(4):
                            h = 4 * k + i
                            pe.matmul(out[:, i * P:(i + 1) * P], q_of(n, h, h + 1, 0, P),
                                      k_of(n, k, 0, P), start=i == 0, stop=False, skip_group_check=True)
                        ins = pe.matmul(out, identb[:, :], mask_q[:, :], start=False, stop=True, skip_group_check=True)
                    else:
                        for i in (0, 1):
                            h = 4 * k + 2 * (c - 1) + i
                            pe.matmul(out[:, i * S:(i + 1) * S], q_of(n, h, h + 1, P, S),
                                      k_of(n, k, 0, S), start=i == 0, stop=False, skip_group_check=True)
                        ins = pe.matmul(out.rearrange("p (h t) -> p h t", t=S)[:, :, P:S], identb[:, :],
                                        mask_q[:, 0:S], start=False, stop=True, skip_group_check=True)
                    ins.then_inc(sem("a_rows"), 1)

                def scores(U, tt):
                    n, k = divmod(U, KJ)
                    if U >= 1:
                        pe.wait_ge(sem(f"a_e{tt}"), hd.unit0 + U)
                    bank = ST_BANK + 2 * tt
                    kt = k_of(n, k, tt * P, (tt + 1) * P)
                    if hd.causal and tt == 1:
                        pe.matmul(ps[:, bank, :], kt, q_of(n, 4 * k, 4 * k + 4, P, S), start=True, stop=False,
                                  skip_group_check=True)
                        ins = pe.matmul(ps[:, bank, :], identb[:, :], mask_k[:, :], start=False, stop=True,
                                        skip_group_check=True)
                    else:
                        for i in (0, 1):
                            ins = pe.matmul(ps[:, bank + i, :], kt, q_of(n, 4 * k + 2 * i, 4 * k + 2 * i + 2),
                                            start=True, stop=not hd.causal, skip_group_check=True)
                            if hd.causal:
                                ins = pe.matmul(ps[:, bank + i, :].rearrange("p (h s) -> p h s", s=S)[:, :, 0:P],
                                                identb[:, :], mask_k[:, 0:S], start=False, stop=True,
                                                skip_group_check=True)
                    ins.then_inc(sem(f"a_st{tt}"), 1)

                def values(U):
                    n, k = divmod(U, KJ)
                    b, j = divmod(n, 2)
                    if U >= 2:
                        pe.wait_ge(sem("a_ot"), hd.unit0 + U - 1)
                    for tt in (0, 1):
                        pe.wait_ge(sem(f"a_e{tt}"), hd.unit0 + U + 1)
                        for h in range(4):
                            o = ps[32 * h:32 * h + 32, OT_BANK, U % 2 * S:U % 2 * S + S]
                            w = S
                            if hd.causal and tt == 1:
                                o, w = o[:, P:S], P
                            ins = pe.matmul(o, v[:, 2 * b + tt, j * KJ + k, :], e[:, U % 2, tt, h * w:(h + 1) * w],
                                            start=tt == 0, stop=tt == 1, skip_group_check=True)
                    ins.then_inc(sem("a_pv"), 1)

                def gather(U):
                    pe.wait_ge(sem("a_ot"), hd.unit0 + U + 1)
                    if U >= 1:
                        pe.wait_ge(sem("a_att"), hd.unit0 + U)
                    w = 4 * (D + 1)
                    for st in (0, 1):
                        ins = pe.matmul(ps[:, SUM_BANK, st * w:(st + 1) * w], ot[:, U % 2, st * P:st * P + P], sel[:, :],
                                        start=st == 0, stop=st == 1, skip_group_check=True)
                    ins.then_inc(sem("a_sum"), 1)

                def turn_max(n, gathered):
                    pe.wait_ge(sem("a_max"), hd.chunk0 + (n + 1) * KJ * hd.chunks)
                    if gathered:
                        pe.wait_ge(sem("a_att"), hd.unit0 + gathered)
                    pe.transpose(ps[0:2 * hd.HJ, SUM_BANK, 384:512],
                                 mx[:, n % 2, 0:2 * hd.HJ], ident[:, :]).then_inc(sem("a_mt"), 1)

                for s in units(hd):
                    mU, sU, vU, gU = stages(hd, s)
                    if mU < hd.units:
                        if mU % KJ == 0:
                            pe.wait_ge(sem(hd.q_sem(mU // KJ)), 64 * hd.uses(mU // KJ))
                            pe.wait_ge(sem(hd.k_sem(mU // KJ)), 32 * hd.uses(mU // KJ))
                        max_chunk(mU, 0)
                    if mU == KJ:
                        pe.wait_ge(sem("lo_ready"), bank_at(f"a{L}", 4))
                    if mU % KJ == 0 and 0 < mU <= hd.units:
                        turn_max(mU // KJ - 1, max(0, gU))
                    if 0 <= sU < hd.units:
                        if sU % KJ == 0:
                            pe.wait_ge(sem(hd.m_sem(sU // KJ)), 32 * hd.uses(sU // KJ))
                        scores(sU, 0)
                    if mU < hd.units:
                        max_chunk(mU, 1)
                    if 0 <= sU < hd.units:
                        scores(sU, 1)
                    if mU < hd.units:
                        max_chunk(mU, 2)
                    if 0 <= gU < hd.units:
                        pe.wait_ge(sem("a_mlo"), hd.step0 + min(mU // KJ, hd.steps))
                        gather(gU)
                    if mU < hd.units and hd.chunks == 4:
                        max_chunk(mU, 3)
                    if 0 <= vU < hd.units:
                        values(vU)
                    if s < 2:
                        turn(f"a{L}", 1, (s,))
                    tail = s - hd.units
                    if tail == 0:
                        pe.wait_ge(sem("a_max"), hd.chunk0 + hd.units * hd.chunks)
                    if L == 2:
                        if tail == 0:
                            turn("o2", 0)
                        if tail == 2:
                            project(0)
                        continue
                    if L == 1 and tail == 0:
                        turn_keys()
                    if tail == 3:
                        if L == 1:
                            pe.wait_ge(sem("k16_split"), 2)
                        turn(f"f{L}", 0)

            def attention_end(L):
                pe.wait_ge(sem("a_att"), grouped[L].unit0 + grouped[L].units)

            def turn_keys():
                pe.wait_ge(sem("kr_ready"), 2)
                for t in range(TILES):
                    ins = pe.transpose(ps[0:CTX, t // 4, (t % 4) * P:(t % 4 + 1) * P], kr[:, t, :], ident[:, :])
                ins.then_inc(sem("kr_turned"), 1)

            def project(hf):
                pe.wait_ge(sem("lo_ready"), bank_at("o2", 2 * hf + 2))
                for i in (2 * hf, 2 * hf + 1):
                    for t in (2 * i, 2 * i + 1):
                        tok = slice(t * P, (t + 1) * P)
                        parts = [(zh[:, j, tok], zl[:, j, tok], dense_h[:, 1, j, :], dense_l[:, 1, j, :])
                                 for j in (0, 1)]
                        ins = product3(pe, ps[:, PROJECT_BANKS[i], (t % 2) * H:(t % 2 + 1) * H], parts, True, True)
                    ins.then_inc(sem("o2_y"), 1)

            def experts3():
                for pair in range(4):
                    eb = pair % 2
                    pe.wait_ge(sem(f"f3_split{eb}"), pair // 2 + 1)
                    if pair == 0:
                        pe.wait_ge(sem("bias3_ready"), 32)
                    for t in range(TILES):
                        n = pair * TILES + t
                        if n >= 4:
                            pe.wait_ge(sem("f3_add"), n - 3)
                        tok = slice(t * P, (t + 1) * P)
                        o = ps[:, n % 4, :]
                        pe.matmul(o, ones2[:, :], b3(pair), start=True, stop=False, skip_group_check=True)
                        parts = [(zh[:, j, tok], zl[:, j, tok], wh[:, eb, j * 512:(j + 1) * 512],
                                  wl[:, eb, j * 512:(j + 1) * 512]) for j in (0, 1)]
                        product3(pe, o, parts, False, True).then_inc(sem("f3_y"), 1)

            attention0()
            pe.wait_ge(sem("l_ident"), 32)
            turn("f0", 0)
            logits(0, 0)
            turn("f0", 1)
            logits(0, 1)
            experts(0)
            turn("a1", 0)
            attention(1)
            attention_end(1)
            logits(1, 0)
            turn("f1", 1)
            logits(1, 1)
            experts(1)
            turn("a2", 0)
            attention(2)
            attention_end(2)
            turn("o2", 1)
            turn("f2", 0)
            project(1)
            logits(2, 0)
            turn("f2", 1)
            logits(2, 1)
            experts(2)
            turn("a3", 0)
            attention(3)
            attention_end(3)
            logits(3, 0)
            turn("f3", 1)
            logits(3, 1)
            experts3()

        @block.scalar
        def _(act):
            def split_hi(tag, hf):
                for j in (0, 1):
                    act.wait_ge(sem("turned"), bank_at(tag, 2 * hf + j + 1))
                    act.copy(zh[:, j, hf * HALF:(hf + 1) * HALF], ps[:, TURN_BANKS[tag[0]][hf][j], :]
                             ).then_inc(sem("hi_ready"), 1)

            def centre(src, dst, n, signal, D=None):
                act.wait_ge(sem("shift_ready"), n)
                for t in range(4, TILES):
                    o, i = dst[:, t, :], src[:, t, :]
                    if D:
                        o = o.rearrange("p (j d h) -> p j d h", j=2, d=D)
                        i = i.rearrange("p (j h d) -> p j d h", j=2, d=D)
                    act.activation(o, i, ACT.Identity, bias=shift[:, t - 4:t - 3], scale=rstd[:, t:t + 1]
                                   ).then_inc(sem(signal), 1)

            def attention0():
                act.wait_ge(sem("l_ctxT"), 48)
                for m, dst in ((0, a0q), (1, a0k)):
                    for hf in (0, 1):
                        act.wait_ge(sem("a0_proj"), 2 * m + hf + 1)
                        act.activation(dst[:, hf * HALF:(hf + 1) * HALF], ps[0:CTX, 2 * m + hf, :], ACT.Identity,
                                       bias=bqk[:, m:m + 1]).then_inc(sem("a0_qk"), 1)
                centre(x, z, 1, "a0_z")
                for t in range(TILES):
                    act.wait_ge(sem("a0_nmx"), t // 4 + 1)
                    act.activation(a0s[:, t, :], a0s[:, t, :], ACT.Exp, bias=nmx[:, t:t + 1],
                                   accum_out=rsum[:, t:t + 1]).then_inc(sem("a0_exp"), 1)

            def gate(L):
                if L != 1:
                    act.wait_ge(sem(f"f{L}_gd"), 1)
                    act.activation(gp[:, :, 0:ROUTED[L]], gp[:, :, 0:ROUTED[L]], ACT.Exp).then_inc(sem(f"f{L}_ge"), 1)

            def experts(L):
                gated = L != 1
                n_pair = NEXP[L] // 2

                def pair_units(pair, first):
                    for k in range(4):
                        hf = k % 2
                        unit = pair * 4 + k
                        early = first and k < 2
                        act.wait_ge(sem(f"f{L}_g" if gated else f"f{L}_u"), unit + 1)
                        if not early:
                            act.wait_ge(sem(f"f{L}_gu" if gated else f"f{L}_hm"), unit - 1)
                        act.activation(sg[:, hf, :], ps[:, G_BANK + 2 * hf if gated else G_BANK + hf, :],
                                       ACT.Silu if gated else ACT.Relu).then_inc(sem(f"f{L}_act"), 1)
                        if gated and first and k == 0:
                            act.wait_ge(sem(f"f{L}_wturned"), 1)
                            act.copy(wT[0:ROUTED[L], :].rearrange("e (a b) -> e a b", a=2),
                                     ps[0:ROUTED[L], 0:2, :]).then_inc(sem(f"f{L}_wT"), 1)
                        act.wait_ge(sem(f"f{L}_hm"), unit + 1)
                        if not early:
                            act.wait_ge(sem(f"f{L}_down"), unit - 1)
                        act.copy(hh[:, hf, :], hm[:, hf, :]).then_inc(sem(f"f{L}_hh"), 1)

                if L == 0:
                    act.wait_ge(sem("k8_stored"), 64)
                pair_units(0, True)
                with act.Fori(1, n_pair) as pair:
                    pair_units(pair, False)
                for hf in (0, 1):
                    act.wait_ge(sem(f"f{L}_down"), 4 * n_pair - 1 + hf)
                    for hb in (0, 1):
                        act.copy(acc[:, hb, hf * HALF:(hf + 1) * HALF], ps[:, 2 * hb + hf, :]
                                 ).then_inc(sem(f"f{L}_acc"), 1)

            def attention(L):
                hd = grouped[L]
                for s in units(hd):
                    mU, sU, vU, _ = stages(hd, s)
                    if mU % hd.KJ == 0 and 0 < mU <= hd.units:
                        n = mU // hd.KJ - 1
                        act.wait_ge(sem("a_mt"), hd.step0 + n + 1)
                        if n >= 2:
                            act.wait_ge(sem(hd.m_sem(n - 2)), 32 * hd.uses(n - 2))
                        act.copy(mT[0:2 * hd.HJ, n % 2, 0, :], ps[0:2 * hd.HJ, SUM_BANK, 384:512]
                                 ).then_inc(sem("a_mhi"), 1)
                    for tt in (0, 1):
                        if 0 <= sU < hd.units:
                            act.wait_ge(sem(f"a_st{tt}"), hd.unit0 + sU + 1)
                            if sU >= 2:
                                act.wait_ge(sem("a_pv"), hd.unit0 + sU - 1)
                            if hd.causal and tt == 1:
                                dst, src = e[:, sU % 2, 1, 0:512], ps[:, ST_BANK + 2, :]
                            else:
                                dst = e[:, sU % 2, tt, :].rearrange("p (a b) -> p a b", a=2)
                                src = ps[:, ST_BANK + 2 * tt:ST_BANK + 2 * tt + 2, :]
                            act.activation(dst, src, ACT.Exp, scale=hd.scale).then_inc(sem(f"a_e{tt}"), 1)
                    if 0 <= vU < hd.units:
                        act.wait_ge(sem("a_pv"), hd.unit0 + vU + 1)
                        if vU >= 2:
                            act.wait_ge(sem("a_sum"), hd.unit0 + vU - 1)
                        act.copy(ot[:, vU % 2, 0:S], ps[:, OT_BANK, vU % 2 * S:vU % 2 * S + S]
                                 ).then_inc(sem("a_ot"), 1)
                    tail = s - hd.units
                    if L == 2 and tail == 1:
                        split_hi("o2", 0)
                    if L == 1 and tail == 1:
                        act.wait_ge(sem("kr_turned"), 1)
                        act.copy(hi16.rearrange("p (a b) -> p a b", a=2), ps[0:CTX, 0:2, :]
                                 ).then_inc(sem("k16_split"), 1)
                    if L != 2 and tail == 3:
                        split_hi(f"f{L}", 0)

            attention0()
            split_hi("f0", 0)
            split_hi("f0", 1)
            gate(0)
            experts(0)
            split_hi("a1", 0)
            centre(x, z, 2, "z_ready", 8)
            split_hi("a1", 1)
            attention(1)
            split_hi("f1", 1)
            experts(1)
            centre(z, z, 3, "f1_y")
            centre(x, qn, 4, "a2_qn")
            split_hi("a2", 0)
            split_hi("a2", 1)
            attention(2)
            split_hi("o2", 1)
            split_hi("f2", 0)
            split_hi("f2", 1)
            gate(2)
            experts(2)
            split_hi("a3", 0)
            centre(x, z, 5, "z_ready", 8)
            split_hi("a3", 1)
            attention(3)
            split_hi("f3", 1)
            gate(3)

        @block.vector
        def _(dve):
            c = Chain(dve, sem("dve_step"))

            halves = (0, 1)

            def hand_over():
                dve.scalar_tensor_tensor(shift[:, :], mv[:, 4:8, 0], -1.0, rstd[:, 4:8], ALU.mult, ALU.mult
                                         ).then_inc(sem("shift_ready"), 1)

            def statistics(src, t0, t1):
                for t in range(t0, t1):
                    c.mark(dve.bn_stats(bst[:, t, :], src[:, t, :]))
                c.join()
                for t in range(t0, t1):
                    c.mark(dve.bn_aggr(mv[:, t, :], bst[:, t, :]))
                c.join()

            def roots(t0, t1, scale=1.0, add=EPS):
                tiles = slice(t0, t1)
                y, w, h = rstd[:, tiles], var[:, tiles], root[:, tiles]
                c.step(dve.tensor_scalar(w, mv[:, tiles, 1], scale, add, ALU.mult, ALU.add))
                c.step(dve.tensor_scalar(y.bitcast(I32), w.bitcast(I32), -0.5, ROOT_GUESS, ALU.mult, ALU.add))
                for _ in range(3):
                    c.step(dve.tensor_tensor(h, y, y, ALU.mult))
                    c.step(dve.scalar_tensor_tensor(h, h, -0.5, w, ALU.mult, ALU.mult))
                    c.step(dve.scalar_tensor_tensor(y, h, 1.5, y, ALU.add, ALU.mult))

            def centre(src, dst, t0, t1, signal, D=None):
                for t in range(t0, t1):
                    o, i = dst[:, t, :], src[:, t, :]
                    if D:
                        o = o.rearrange("p (j d h) -> p j d h", j=2, d=D)
                        i = i.rearrange("p (j h d) -> p j d h", j=2, d=D)
                    dve.tensor_scalar(o, i, mv[:, t, 0:1], rstd[:, t:t + 1],
                                      ALU.subtract, ALU.mult).then_inc(sem(signal), 1)

            def split_lo(tag, hf, tiles=(0, 1)):
                for j in tiles:
                    tok = slice(hf * HALF, (hf + 1) * HALF)
                    dve.wait_ge(sem("hi_ready"), bank_at(tag, 2 * hf + j + 1))
                    dve.tensor_tensor(zl[:, j, tok], ps[:, TURN_BANKS[tag[0]][hf][j], :],
                                      zh[:, j, tok].bitcast(F32), ALU.subtract).then_inc(sem("lo_ready"), 1)

            def attention0():
                c.step(dve.memset(ones2f[:, :], 1.0))
                c.step(dve.tensor_copy(ones2[:, :], ones2f[:, :]))
                for hf in (0, 1):
                    dve.wait_ge(sem(f"l_x{hf}"), 16)
                    statistics(x, 4 * hf, 4 * hf + 4)
                roots(0, 8)
                centre(x, z, 0, 4, "a0_z")
                hand_over()
                dve.wait_ge(sem("l_mask"), 32)
                for b in range(B):
                    c.mark(dve.tensor_tensor(mask8[:, 2 * b:2 * b + 2, :].bitcast(U32), m1,
                                             m2[:, b:b + 1, :].broadcast_to([P, 2, S // 4]), ALU.bitwise_or))
                hidden = attn[:, :, :].rearrange("p a b -> p (a b)")
                c.mark(dve.memset(hidden, MASKED))
                for hf in (0, 1):
                    dve.wait_ge(sem("a0_z"), 4 * hf + 4)
                    tiles = slice(4 * hf, 4 * hf + 4)
                    for i in (2 * hf, 2 * hf + 1):
                        dve.wait_ge(sem("a0_scores"), i + 1)
                        c.mark(dve.scalar_tensor_tensor(a0s[:, 2 * i:2 * i + 2, :],
                                                        ps[:, 4 + i, :].rearrange("p (t s) -> p t s", s=S), CTX ** -0.5,
                                                        z[:, 2 * i:2 * i + 2, :], ALU.mult, ALU.mult))
                    c.join()
                    for t in range(4 * hf, 4 * hf + 4):
                        c.mark(dve.copy_predicated(a0s[:, t, :], mask8[:, t, :], hidden))
                    c.join()
                    c.step(dve.tensor_reduce(ga[:, tiles], a0s[:, tiles, :], AX_X, ALU.max))
                    dve.tensor_scalar(nmx[:, tiles], ga[:, tiles], -1.0, None, ALU.mult).then_inc(sem("a0_nmx"), 1)

            def weights0(hf):
                dve.wait_ge(sem("a0_exp"), 4 * hf + 4)
                c.step(dve.reciprocal(gb[:, 4 * hf:4 * hf + 4], rsum[:, 4 * hf:4 * hf + 4]))
                for t in range(4 * hf, 4 * hf + 4):
                    c.mark(dve.scalar_tensor_tensor(x[:, t, :], a0s[:, t, :], gb[:, t:t + 1], x[:, t, :],
                                                    ALU.mult, ALU.add))
                c.join()

            def choose(L, k, width):
                W = width + 8 - k
                for t in range(TILES):
                    c.mark(dve.max(g8[:, t, :], gs[:, t, 0:W]))
                c.join()
                if L == 3:
                    c.mark(dve.tensor_copy(ga[:, :], g8[:, :, 0]))
                c.step(dve.memset(g8[:, :, k:8], SENTINEL))
                for t in range(TILES):
                    c.mark(dve.match_replace(gr[:, t, 0:W], g8[:, t, :], gs[:, t, 0:W], TAKEN))
                c.join()
                c.step(dve.tensor_scalar(gr[:, :, 0:width], gr[:, :, 0:width], TAKEN, None, ALU.is_equal))

            def per_tile(v, n):
                return v[:, :].rearrange("p (t o) -> p t o", o=1).broadcast_to([P, TILES, n])

            def gate(L):
                E = ROUTED[L]
                dve.wait_ge(sem("logits"), 2 * L + 2)
                both = ps[:, LOGIT_BANK, 0:TILES * 2 * E].rearrange("p (t v e) -> p t v e", v=2, e=E)
                lg = gs[:, :, 0:E]
                c.step(dve.tensor_copy(lg, both[:, :, 0]))
                c.step(dve.tensor_tensor(lg, lg, both[:, :, 1], ALU.add))
                p_ = gp[:, :, 0:E]
                if L == 1:
                    for t in range(TILES):
                        c.mark(dve.max(g8[:, t, :], lg[:, t, :]))
                    c.join()
                    c.step(dve.tensor_tensor(ga[:, :], g8[:, :, 0], g8[:, :, 1], ALU.add))
                    return
                if L == 3:
                    c.step(dve.memset(gs[:, :, E:E + 6], SENTINEL))
                    choose(3, 2, E)
                    dve.tensor_tensor(p_, gs[:, :, 0:E], per_tile(ga, E), ALU.subtract).then_inc(sem("f3_gd"), 1)
                    dve.wait_ge(sem("f3_ge"), 1)
                    c.step(dve.tensor_tensor(gw[:, :, 0:E], gr[:, :, 0:E], p_, ALU.mult))
                    c.step(dve.tensor_reduce(ga[:, :], gw[:, :, 0:E], AX_X, ALU.add))
                    c.step(dve.reciprocal(gb[:, :], ga[:, :]))
                    c.step(dve.tensor_tensor(gw[:, :, 0:E], gw[:, :, 0:E], per_tile(gb, E), ALU.mult))
                    return
                c.step(dve.tensor_reduce(ga[:, :], lg, AX_X, ALU.max))
                dve.tensor_tensor(p_, lg, per_tile(ga, E), ALU.subtract).then_inc(sem(f"f{L}_gd"), 1)
                k = 2 if L == 0 else 4
                c.mark(dve.memset(gs[:, :, E:E + 8 - k], SENTINEL))
                dve.wait_ge(sem(f"f{L}_ge"), 1)
                c.step(dve.tensor_reduce(ga[:, :], p_, AX_X, ALU.add))
                c.step(dve.reciprocal(gb[:, :], ga[:, :]))
                if L == 0:
                    c.step(dve.tensor_tensor(p_, p_, per_tile(gb, E), ALU.mult))
                    dve.wait_ge(sem("l_router"), 32)
                    c.step(dve.tensor_tensor(gs[:, :, 0:E], p_, bias0[:, :].rearrange("p (o e) -> p o e", o=1)
                                             .broadcast_to([P, TILES, E]), ALU.add))
                    choose(0, 2, E)
                    dve.scalar_tensor_tensor(gw[:, :, 0:E], gr[:, :, 0:E], 1.5, p_, ALU.mult, ALU.mult
                                             ).then_inc(sem("f0_w"), 1)
                else:
                    c.step(dve.tensor_tensor(gs[:, :, 0:E], p_, per_tile(gb, E), ALU.mult))
                    choose(2, 4, E)
                    dve.tensor_tensor(gw[:, :, 0:E], gr[:, :, 0:E], gs[:, :, 0:E], ALU.mult).then_inc(sem("f2_w"), 1)

            def experts(L):
                gated = L != 1
                n_pair = NEXP[L] // 2

                def pair_units(pair, first):
                    for k in range(4):
                        hf = k % 2
                        unit = pair * 4 + k
                        early = first and k < 2
                        if L == 0 and first and k > 0:
                            for t in ((0, 1, 2), (3, 4, 5), (6, 7))[k - 1]:
                                c.mark(dve.scalar_tensor_tensor(x[:, t, :], z[:, t, :], gb[:, t:t + 1], x[:, t, :],
                                                                ALU.mult, ALU.add))
                        dve.wait_ge(sem(f"f{L}_act"), unit + 1)
                        dve.wait_ge(sem(f"f{L}_u"), unit + 1)
                        if gated:
                            dve.tensor_tensor(t1[:, hf, :], sg[:, hf, :], ps[:, U_BANK + 2 * hf, :], ALU.mult
                                              ).then_inc(sem(f"f{L}_gu"), 1)
                            dve.wait_ge(sem(f"f{L}_gu"), unit + 1)
                            if early:
                                dve.wait_ge(sem(f"f{L}_spread"), hf + 1)
                                weights = ps[:, SPREAD_BANK + hf, :]
                            else:
                                dve.wait_ge(sem(f"f{L}_row{k // 2}"), 16 * pair + 16 * (k // 2))
                                weights = spread[:, k // 2, hf * HALF:(hf + 1) * HALF].bitcast(F32)
                        if not early:
                            dve.wait_ge(sem(f"f{L}_hh"), unit - 1)
                        if gated:
                            ins = dve.tensor_tensor(hm[:, hf, :], t1[:, hf, :], weights, ALU.mult)
                        else:
                            ins = dve.tensor_tensor(hm[:, hf, :], sg[:, hf, :], ps[:, G_BANK + hf, :], ALU.mult)
                        ins.then_inc(sem(f"f{L}_hm"), 1)
                        dve.wait_ge(sem(f"f{L}_hh"), unit + 1)
                        if not early:
                            dve.wait_ge(sem(f"f{L}_down"), unit - 1)
                        dve.tensor_tensor(hl[:, hf, :], hm[:, hf, :], hh[:, hf, :].bitcast(F32), ALU.subtract
                                          ).then_inc(sem(f"f{L}_hl"), 1)

                if L == 0:
                    dve.wait_ge(sem("f0_w"), 1)
                    c.step(dve.tensor_reduce(gb[:, :], gw[:, :, 8:12], AX_X, ALU.add))
                    dve.wait_ge(sem("k8_stored"), 64)
                if L == 1:
                    for i in range(4):
                        dve.wait_ge(sem("f1_moe"), i + 1)
                        c.mark(dve.tensor_scalar(z[:, 2 * i, :], ps[:, i, 0:H], ga[:, 2 * i:2 * i + 1], None,
                                                 ALU.mult))
                        c.join()
                        dve.tensor_scalar(z[:, 2 * i + 1, :], ps[:, i, H:2 * H], ga[:, 2 * i + 1:2 * i + 2], None,
                                          ALU.mult).then_inc(sem("f1_moe_read"), 1)
                    dve.wait_ge(sem("f1_moe_read"), 4)
                pair_units(0, True)
                with dve.Fori(1, n_pair) as pair:
                    pair_units(pair, False)
                c.join()

            def sum_up(L, hf):
                base = z if L == 1 else x
                for i in (2 * hf, 2 * hf + 1):
                    dve.wait_ge(sem(f"f{L}_back"), i + 1)
                    o = base[:, 2 * i:2 * i + 2, :]
                    c.mark(dve.tensor_tensor(o, ps[:, 4 + i, :].rearrange("p (t d) -> p t d", d=H), o, ALU.add))
                c.join()

            def attention(L):
                hd = grouped[L]
                D, KJ, HJ, d1 = hd.D, hd.KJ, hd.HJ, hd.D + 1

                def maxima(U, ch):
                    n, k = divmod(U, KJ)
                    C = U * hd.chunks + ch
                    dve.wait_ge(sem("a_rows"), hd.chunk0 + C + 1)
                    if n >= 2 and U % KJ == 0 and ch == 0:
                        dve.wait_ge(sem("a_mt"), hd.step0 + n - 1)
                    bank = ps[:, MAX_BANK + C % max_banks(hd, C), :]
                    if hd.causal:
                        w, st = (P, 0) if ch == 0 else (S, 1)
                        h0 = 4 * k + (0 if ch == 0 else 2 * (ch - 1))
                    else:
                        w, st, h0 = S, ch // 2, 4 * k + 2 * (ch % 2)
                    columns = mx[:, n % 2, 0:2 * HJ].rearrange("p (h st) -> p h st", st=2)
                    dve.tensor_reduce(columns[:, h0:h0 + 512 // w, st], bank.rearrange("p (h t) -> p h t", t=w),
                                      AX_X, ALU.max).then_inc(sem("a_max"), 1)

                def collect(U):
                    n, k = divmod(U, KJ)
                    if k == 0 and n >= 2:
                        if hd.causal:
                            dve.wait_ge(sem("z_ready"), z_at("o2", n - 1))
                        else:
                            dve.wait_ge(sem("a_divided"), n - 1 + (hd.steps if L == 3 else 0))
                    dve.wait_ge(sem("a_sum"), hd.unit0 + U + 1)
                    dve.tensor_copy(att[:, n % 2, :, k * 4 * d1:(k + 1) * 4 * d1],
                                    ps[:, SUM_BANK, 0:8 * d1].rearrange("p (t q) -> p t q", t=2)
                                    ).then_inc(sem("a_att"), 1)

                def invert(n):
                    dve.wait_ge(sem("a_att"), hd.unit0 + (n + 1) * KJ)
                    v = att[:, n % 2, :, 0:HJ * d1].rearrange("p t (h d) -> p t h d", d=d1)
                    dve.reciprocal(attr[:, n % 2, :, 0:HJ], v[:, :, :, D]).then_inc(sem("a_recip"), 1)

                for s in units(hd):
                    mU, _, _, gU = stages(hd, s)
                    tail = s - hd.units
                    if mU < hd.units:
                        maxima(mU, 0)
                    if mU % KJ == 0 and 0 < mU <= hd.units:
                        n = mU // KJ - 1
                        dve.wait_ge(sem("a_mhi"), hd.step0 + n + 1)
                        dve.tensor_tensor(mT[0:2 * HJ, n % 2, 1, :], ps[0:2 * HJ, SUM_BANK, 384:512],
                                          mT[0:2 * HJ, n % 2, 0, :].bitcast(F32), ALU.subtract
                                          ).then_inc(sem("a_mlo"), 1)
                    if mU < hd.units:
                        maxima(mU, 1)
                        maxima(mU, 2)
                    if 0 <= gU < hd.units:
                        collect(gU)
                    if mU < hd.units and hd.chunks == 4:
                        maxima(mU, 3)
                    if hd.causal and s == 1:
                        split_lo(f"a{L}", 1)
                    if not hd.causal and 1 <= s < 3:
                        split_lo(f"a{L}", 1, (s - 1,))
                    if 0 <= gU < hd.units and gU % KJ == KJ - 1:
                        invert(gU // KJ)
                    if L == 2:
                        if tail == 1:
                            split_lo("o2", 0)
                        if tail == 3:
                            project(0)
                            statistics(x, 0, 4)
                        if tail == 4:
                            roots(0, 4)
                        if tail == 5:
                            dve.wait_ge(sem("z_ready"), z_at("o2", TILES))
                            centre(x, z, 0, 4, "z_ready")
                        continue
                    if L == 1 and tail == 2:
                        dve.wait_ge(sem("k16_split"), 1)
                        dve.tensor_tensor(lo16.rearrange("p (a b) -> p a b", a=2), ps[0:CTX, 0:2, :],
                                          hi16.rearrange("p (a b) -> p a b", a=2).bitcast(F32), ALU.subtract
                                          ).then_inc(sem("k16_split"), 1)
                    before = hd.steps if L == 3 else 0
                    if tail == 0:
                        dve.wait_ge(sem("a_done"), before + 4)
                        statistics(x, 0, 4)
                    if tail == 1:
                        roots(0, 4)
                    if tail == 2:
                        centre(x, z, 0, 4, "z_ready")
                    if tail == 4:
                        split_lo(f"f{L}", 0)
                        dve.wait_ge(sem("a_done"), before + 6)
                        statistics(x, 4, 6)
                    if tail == 5:
                        roots(4, 6)
                    if tail == 6:
                        centre(x, z, 4, 6, "z_ready")

            def add_normalised(hf):
                if hf == 1:
                    dve.wait_ge(sem("f1_y"), 5)
                    c.step(dve.tensor_tensor(x[:, 4:8, :], x[:, 4:8, :], z[:, 4:8, :], ALU.add))
                    return
                for t in range(4 * hf, 4 * hf + 4):
                    c.mark(dve.scalar_tensor_tensor(z[:, t, :], z[:, t, :], mv[:, t, 0:1], gamma[:, :],
                                                    ALU.subtract, ALU.mult))
                c.join()
                if hf == 0:
                    dve.wait_ge(sem("beta_added"), 1)
                for t in range(4 * hf, 4 * hf + 4):
                    c.mark(dve.scalar_tensor_tensor(x[:, t, :], z[:, t, :], rstd[:, t:t + 1], x[:, t, :],
                                                    ALU.mult, ALU.add))
                c.join()

            def queries(hf):
                dve.wait_ge(sem("rotation_ready"), 6)
                dve.wait_ge(sem("a2_qn"), 4 * hf + 4)
                half = slice(4 * hf, 4 * hf + 4)
                by_tile = "p (b t) d -> p b t d"
                for st in (0, 1):
                    cb = rotation[:, 0, st:st + 1, :].broadcast_to([P, 2, H])
                    c.mark(dve.tensor_tensor(qc[:, half, :].rearrange(by_tile, t=2)[:, :, st],
                                             qn[:, half, :].rearrange(by_tile, t=2)[:, :, st], cb, ALU.mult))
                c.join()

            def add_rotated(hf):
                dve.wait_ge(sem("a2_qs"), 4 * hf + 4)
                for t in range(4 * hf, 4 * hf + 4):
                    order = "p (j h d) -> p j d h"
                    dve.tensor_tensor(z[:, t, :].rearrange("p (j d h) -> p j d h", j=2, d=16),
                                      qc[:, t, :].rearrange(order, j=2, d=16),
                                      qsin[:, t, :].rearrange(order, j=2, d=16), ALU.add
                                      ).then_inc(sem("z_ready"), 1)

            def project(hf):
                for i in (2 * hf, 2 * hf + 1):
                    dve.wait_ge(sem("o2_y"), i + 1)
                    o = x[:, 2 * i:2 * i + 2, :]
                    c.mark(dve.tensor_tensor(o, ps[:, PROJECT_BANKS[i], :].rearrange("p (t d) -> p t d", d=H), o,
                                             ALU.add))
                c.join()

            def experts3():
                for pair in range(4):
                    for t in range(TILES):
                        n = pair * TILES + t
                        dve.wait_ge(sem("f3_y"), n + 1)
                        for i in (0, 1):
                            ins = dve.scalar_tensor_tensor(x[:, t, :], ps[:, n % 4, i * H:(i + 1) * H],
                                                           gw[:, t, 2 * pair + i:2 * pair + i + 1], x[:, t, :],
                                                           ALU.mult, ALU.add)
                            if i == 0:
                                c.step(ins)
                            else:
                                ins.then_inc(sem("f3_add"), 1)

            attention0()
            for hf in halves:
                weights0(hf)
                statistics(x, 4 * hf, 4 * hf + 4)
            roots(0, 8)
            for hf in halves:
                centre(x, z, 4 * hf, 4 * hf + 4, "z_ready")
            for hf in halves:
                split_lo("f0", hf)
            gate(0)
            experts(0)

            def attention_input(L):
                sum_up(L - 1, 0)
                statistics(x, 0, 4)
                roots(0, 4)
                centre(x, z, 0, 4, "z_ready", 8)
                sum_up(L - 1, 1)
                split_lo(f"a{L}", 0)
                statistics(x, 4, 8)
                roots(4, 8)
                hand_over()

            def second_half(L):
                if L == 2:
                    statistics(x, 4, 8)
                    roots(4, 8)
                    centre(x, z, 4, 8, "z_ready")
                else:
                    dve.wait_ge(sem("a_done"), 16 if L == 3 else 8)
                    statistics(x, 6, 8)
                    roots(6, 8)
                    centre(x, z, 6, 8, "z_ready")
                split_lo(f"f{L}", 1)
                gate(L)

            attention_input(1)
            attention(1)
            second_half(1)
            experts(1)
            for hf in halves:
                sum_up(1, hf)
                statistics(z, 4 * hf, 4 * hf + 4)
            roots(0, 8)
            hand_over()
            for hf in halves:
                add_normalised(hf)
                statistics(x, 4 * hf, 4 * hf + 4)
            roots(0, 8, 1.0 + EPS, EPS * EPS)
            centre(x, qn, 0, 4, "a2_qn")
            hand_over()
            queries(0)
            add_rotated(0)
            queries(1)
            split_lo("a2", 0)
            add_rotated(1)
            attention(2)
            split_lo("o2", 1)
            split_lo("f2", 0)
            project(1)
            second_half(2)
            experts(2)
            attention_input(3)
            attention(3)
            second_half(3)
            experts3()


def constants():
    i = np.arange(P)
    hide = np.where(i[None, :] > i[:, None], -1e30, 0.0).astype(np.float32)
    inv = 1.0 / 10000.0 ** (np.arange(0, 16, 2, dtype=np.float32) / 16)
    angle = np.outer(np.arange(S, dtype=np.float32), inv.astype(np.float32)).astype(np.float32)
    angle = np.concatenate([angle, angle], -1)
    cos, sin = np.cos(angle), np.sin(angle)
    sin[:, :8] *= -1.0
    turn = lambda v: np.ascontiguousarray(v.reshape(2, P, 16).transpose(1, 0, 2)).astype(np.float32)
    sel = {}
    for d in (8, 16):
        s = np.zeros((P, 4, d + 1), np.float32)
        for h in range(4):
            for r in range(d + 1):
                s[32 * h + r, h, r] = 1.0
        sel[d] = s.reshape(P, 4 * (d + 1))
    return {
        "ident": np.eye(P, dtype=np.float32), "hide": np.concatenate([hide, hide.T], axis=1),
        "cos": turn(cos), "sin": turn(sin), "sel8": sel[8], "sel16": sel[16],
    }


def kernel(**inp):
    import concourse.bacc as _bacc
    from concourse.bass_utils import run_bass_kernel_spmd as _run

    g = {k: np.asarray(v) for k, v in inp.items()}

    def rows(w):
        return w.reshape(2, P, -1).transpose(1, 0, 2)

    def packed(gate, up, down):
        flat = [w.reshape(-1, 2, P, P).transpose(0, 2, 1, 3).reshape(-1, P, 2 * P) for w in (gate, up) if w is not None]
        return np.concatenate(flat + [down], axis=2)

    by_kd = np.arange(CTX).reshape(8, 8).T.reshape(-1)
    arrays = dict(constants())
    arrays.update({
        "x": g["x"].reshape(TOK, H),
        "ctx": g["ctx_512"].reshape(TOK, CTX),
        "ctxP": g["ctx_512"].reshape(TOK, CTX).T[by_kd],
        "wqk": np.stack([g["L0_xattn_Wq"].T[by_kd], g["L0_xattn_Wk"].T[by_kd]], axis=1),
        "bqk": np.stack([g["L0_xattn_bq"], g["L0_xattn_bk"]], axis=1),
        "m1": np.ascontiguousarray(g["mask_SxS2_bk1"]).view(np.uint32),
        "m2": np.ascontiguousarray(g["mask_BxS2_bf0"]).view(np.uint32),
        "router": rows(np.concatenate([g["L0_ffn_classifier_w"].T, g["L1_ffn_gate_w"], g["L2_ffn_Wgate"].T,
                                       g["L3_ffn_gate_w"].T], axis=1)),
        "dense": np.stack([rows(g["L1_ffn_expert_weight"]), rows(g["L2_xattn_w_out"].T)], axis=1),
        "bias0": g["L0_ffn_e_score_correction_bias"],
        "bias3": g["L3_ffn_expert_b"],
        "gamma": g["L1_ffn_ln_gamma"], "beta": g["L1_ffn_ln_beta"],
        "qw": g["L2_xattn_q_norm_w"], "kw": g["L2_xattn_k_norm_w"],
        "experts0": packed(g["L0_ffn_gate_w"].transpose(0, 2, 1), g["L0_ffn_up_w"].transpose(0, 2, 1),
                           g["L0_ffn_down_w"].transpose(0, 2, 1)),
        "experts1": packed(None, g["L1_ffn_up_w"].reshape(H, 8, P).transpose(1, 0, 2),
                           g["L1_ffn_down_w"].reshape(8, P, H)),
        "experts2": packed(g["L2_ffn_Wg"], g["L2_ffn_Wu"], g["L2_ffn_Wd"]),
        "experts3": g["L3_ffn_expert_w"].transpose(0, 2, 1).reshape(4, 2, 2, P, H).transpose(0, 3, 2, 1, 4)
                     .reshape(4, P, 1024),
    })
    arrays = {f"in_{k}": np.ascontiguousarray(v) for k, v in arrays.items()}
    nc = _bacc.Bacc("TRN2", target_bir_lowering=False, num_devices=1)
    aps = {k[3:]: nc.dram_tensor(k, v.shape, mybir.dt.from_np(v.dtype), kind="ExternalInput").ap()
           for k, v in arrays.items()}
    out = nc.dram_tensor("out_x", (TOK, H), F32, kind="ExternalOutput").ap()
    build(nc, aps, out)
    r = _run(nc, [arrays], core_ids=[0])
    return r.results[0]["out_x"].reshape(B, S, H)
```
